# Optimizing a Trainium2 kernel written in Bass

```python
import numpy as np
import jax
import jax.numpy as jnp

def _softmax(x, axis=-1):
    return jax.nn.softmax(x, axis=axis)

def _gelu(x):
    return jax.nn.gelu(x, approximate=True)

def _silu(x):
    return jax.nn.silu(x)

def _sigmoid(x):
    return jax.nn.sigmoid(x)

def _layernorm(x, axis=-1, eps=1e-05):
    m = jnp.mean(x, axis=axis, keepdims=True)
    v = jnp.var(x, axis=axis, keepdims=True)
    return (x - m) / jnp.sqrt(v + eps)

def _scatter_add(tgt, idx, src, axis=0):
    return tgt.at[idx].add(src)

def _segment_sum(src, seg, n):
    return jax.ops.segment_sum(src, seg, n)
kernel_name = 'mk_adj_ffn_d2_adj_r2_8f60da'

def setup_inputs(seed: int=0):
    np.random.seed(seed)
    _w = jnp.asarray

    def _rec_inputs():
        import jax
        import jax.numpy as jnp
        _gk = jax.random.key(seed)
        x = -0.0005963 + 1.001 * jax.random.normal(jax.random.fold_in(_gk, 1), (2048, 256), jnp.float32)
        _a = jax.random.bernoulli(jax.random.fold_in(_gk, 2), 0.000976562, (2048, 2048))
        _af = _a.astype(jnp.float32)
        adj = _af
        return (x, adj)
    x, adj = _rec_inputs()

    def _L0_gnn_setup():
        import jax, jax.numpy as jnp
        import numpy as np
        N = 3072
        D_IN = 256
        D_OUT = 256
        DENSITY = 0.005
        key = jax.random.key(seed)
        ks = jax.random.split(key, 12)
        x = jax.random.normal(ks[0], (N, D_IN), dtype=jnp.float32)
        adj_a = (jax.random.uniform(ks[1], (N, N)) < DENSITY).astype(jnp.float32)
        adj_b = (jax.random.uniform(ks[2], (N, N)) < DENSITY).astype(jnp.float32)
        W_sa = jax.random.normal(ks[3], (D_IN, D_OUT), dtype=jnp.float32) * (1.414 / np.sqrt(D_IN + D_OUT))
        a_sa = jax.random.normal(ks[4], (1, 2 * D_OUT), dtype=jnp.float32) * (1.414 / np.sqrt(1 + 2 * D_OUT))
        stdv = 1.0 / np.sqrt(D_OUT)
        W_gcnb = jax.random.uniform(ks[5], (D_IN, D_OUT), minval=-stdv, maxval=stdv, dtype=jnp.float32)
        b_gcnb = jax.random.uniform(ks[6], (D_OUT,), minval=-stdv, maxval=stdv, dtype=jnp.float32)
        s = 1.0 / np.sqrt(2 * D_IN)
        Wa = jax.random.uniform(ks[7], (1, 2 * D_IN), minval=-s, maxval=s, dtype=jnp.float32)
        ba = jax.random.uniform(ks[8], (1,), minval=-s, maxval=s, dtype=jnp.float32)
        Wb = jax.random.uniform(ks[9], (1, 2 * D_IN), minval=-s, maxval=s, dtype=jnp.float32)
        bb = jax.random.uniform(ks[10], (1,), minval=-s, maxval=s, dtype=jnp.float32)
        return {'x': x, 'adj_a': adj_a, 'adj_b': adj_b, 'W_sa': W_sa, 'a_sa': a_sa, 'W_gcnb': W_gcnb, 'b_gcnb': b_gcnb, 'Wa': Wa, 'ba': ba, 'Wb': Wb, 'bb': bb}
    _L0_gnn_all = _L0_gnn_setup()
    _L0_gnn_in = {k: v for k, v in _L0_gnn_all.items() if k in ('W_sa', 'a_sa', 'W_gcnb', 'b_gcnb', 'Wa', 'ba', 'Wb', 'bb')}
    del _L0_gnn_all

    def _L0_ffn_setup():
        import jax, jax.numpy as jnp
        import numpy as np
        DIM, DEPTH, MULT = (256, 3, 4)
        E = 2 ** DEPTH
        HID = MULT * DIM
        B, S = (4, 512)

        def _leaf_probs(flat_x, rw, rb):
            n_tok = flat_x.shape[0]
            leaf = jnp.ones((n_tok, 1), dtype=flat_x.dtype)
            for d in range(DEPTH):
                off, n = (2 ** d - 1, 2 ** d)
                logits = flat_x @ rw[off:off + n].T + rb[off:off + n]
                p = jax.nn.sigmoid(logits)
                leaf = (leaf[:, :, None] * jnp.stack([1.0 - p, p], axis=2)).reshape(n_tok, 2 * n)
            return leaf
        key = jax.random.key(seed)
        ks = jax.random.split(key, 7)
        sd = 1.0 / np.sqrt(DIM)
        sh = 1.0 / np.sqrt(HID)
        return {'x': jax.random.normal(ks[0], (B, S, DIM), dtype=jnp.float32), 'rw': jax.random.normal(ks[1], (E - 1, DIM), dtype=jnp.float32) * sd, 'rb': jax.random.normal(ks[2], (E - 1,), dtype=jnp.float32) * sd, 'w1': jax.random.normal(ks[3], (E, DIM, HID), dtype=jnp.float32) * sd, 'b1': jax.random.normal(ks[4], (E, HID), dtype=jnp.float32) * sd, 'w2': jax.random.normal(ks[5], (E, HID, DIM), dtype=jnp.float32) * sh, 'b2': jax.random.normal(ks[6], (E, DIM), dtype=jnp.float32) * sh}
    _L0_ffn_all = _L0_ffn_setup()
    _L0_ffn_in = {k: v for k, v in _L0_ffn_all.items() if k in ('rw', 'rb', 'w1', 'b1', 'w2', 'b2')}
    del _L0_ffn_all

    def _L1_gnn_setup():
        import jax, jax.numpy as jnp
        import numpy as np
        IN_C, HID_C = (256, 256)
        ALPHA = 0.2
        N = 4096
        NEG_BIG = -9000000000000000.0
        key = jax.random.key(seed)
        k1, k2, k3, k4, k5, k6, k7 = jax.random.split(key, 7)
        h = jax.random.normal(k1, (N, IN_C), dtype=jnp.float32)
        adj = jax.random.randint(k2, (N, N), 0, 2).astype(jnp.float32)
        gain = np.sqrt(2.0 / (1.0 + ALPHA ** 2))
        lim_W = gain * np.sqrt(6.0 / (2 * IN_C + HID_C))
        W = jax.random.uniform(k3, (2 * IN_C, HID_C), jnp.float32, -lim_W, lim_W)
        lim_a = np.sqrt(1.0 / HID_C)
        a_w = jax.random.uniform(k4, (HID_C,), jnp.float32, -lim_a, lim_a)
        a_b = jax.random.uniform(k5, (), jnp.float32, -lim_a, lim_a)
        lim_fc = np.sqrt(1.0 / IN_C)
        fc_w = jax.random.uniform(k6, (IN_C, HID_C), jnp.float32, -lim_fc, lim_fc)
        fc_b = jax.random.uniform(k7, (HID_C,), jnp.float32, -lim_fc, lim_fc)
        return {'h': h, 'adj': adj, 'W': W, 'a_w': a_w, 'a_b': a_b, 'fc_w': fc_w, 'fc_b': fc_b}
    _L1_gnn_all = _L1_gnn_setup()
    _L1_gnn_in = {k: v for k, v in _L1_gnn_all.items() if k in ('W', 'a_w', 'a_b', 'fc_w', 'fc_b')}
    del _L1_gnn_all

    def _L1_ffn_setup():
        import jax, jax.numpy as jnp
        import numpy as np
        D_MODEL = 256
        D_FF = 1024
        NUM_EXPERTS = 8
        TOP_K = 2
        key = jax.random.key(seed)
        ks = jax.random.split(key, 6)
        scale = 0.02
        x = jax.random.normal(ks[0], (4, 4096, D_MODEL), dtype=jnp.float32)
        gate_w = jax.random.normal(ks[1], (D_MODEL, NUM_EXPERTS), dtype=jnp.float32) * scale
        w1 = jax.random.normal(ks[2], (NUM_EXPERTS, D_MODEL, D_FF), dtype=jnp.float32) * scale
        b1 = jnp.zeros((NUM_EXPERTS, D_FF), dtype=jnp.float32)
        w2 = jax.random.normal(ks[3], (NUM_EXPERTS, D_FF, D_MODEL), dtype=jnp.float32) * scale
        b2 = jnp.zeros((NUM_EXPERTS, D_MODEL), dtype=jnp.float32)
        return {'x': x, 'gate_w': gate_w, 'w1': w1, 'b1': b1, 'w2': w2, 'b2': b2}
    _L1_ffn_all = _L1_ffn_setup()
    _L1_ffn_in = {k: v for k, v in _L1_ffn_all.items() if k in ('gate_w', 'w1', 'b1', 'w2', 'b2')}
    del _L1_ffn_all
    return {'x': x, 'adj': adj, 'L0_gnn_W_sa': _L0_gnn_in['W_sa'], 'L0_gnn_a_sa': _L0_gnn_in['a_sa'], 'L0_gnn_W_gcnb': _L0_gnn_in['W_gcnb'], 'L0_gnn_b_gcnb': _L0_gnn_in['b_gcnb'], 'L0_gnn_Wa': _L0_gnn_in['Wa'], 'L0_gnn_ba': _L0_gnn_in['ba'], 'L0_gnn_Wb': _L0_gnn_in['Wb'], 'L0_gnn_bb': _L0_gnn_in['bb'], 'L0_ffn_rw': _L0_ffn_in['rw'], 'L0_ffn_rb': _L0_ffn_in['rb'], 'L0_ffn_w1': _L0_ffn_in['w1'], 'L0_ffn_b1': _L0_ffn_in['b1'], 'L0_ffn_w2': _L0_ffn_in['w2'], 'L0_ffn_b2': _L0_ffn_in['b2'], 'L1_gnn_W': _L1_gnn_in['W'], 'L1_gnn_a_w': _L1_gnn_in['a_w'], 'L1_gnn_a_b': _L1_gnn_in['a_b'], 'L1_gnn_fc_w': _L1_gnn_in['fc_w'], 'L1_gnn_fc_b': _L1_gnn_in['fc_b'], 'L1_ffn_gate_w': _L1_ffn_in['gate_w'], 'L1_ffn_w1': _L1_ffn_in['w1'], 'L1_ffn_b1': _L1_ffn_in['b1'], 'L1_ffn_w2': _L1_ffn_in['w2'], 'L1_ffn_b2': _L1_ffn_in['b2']}

def reference(x, adj, L0_gnn_W_sa, L0_gnn_a_sa, L0_gnn_W_gcnb, L0_gnn_b_gcnb, L0_gnn_Wa, L0_gnn_ba, L0_gnn_Wb, L0_gnn_bb, L0_ffn_rw, L0_ffn_rb, L0_ffn_w1, L0_ffn_b1, L0_ffn_w2, L0_ffn_b2, L1_gnn_W, L1_gnn_a_w, L1_gnn_a_b, L1_gnn_fc_w, L1_gnn_fc_b, L1_ffn_gate_w, L1_ffn_w1, L1_ffn_b1, L1_ffn_w2, L1_ffn_b2):
    import jax
    import jax.numpy as jnp

    def _L0_gnn_ref(x, adj_a, adj_b, W_sa, a_sa, W_gcnb, b_gcnb, Wa, ba, Wb, bb):
        import jax, jax.numpy as jnp
        import numpy as np
        N = 3072
        D_IN = 256
        D_OUT = 256
        DENSITY = 0.005
        type_sum_a = adj_a @ x
        type_sum_b = adj_b @ x
        attn_a = jax.nn.sigmoid(jnp.concatenate([type_sum_a, x], axis=1) @ Wa.T + ba)
        attn_b = jax.nn.sigmoid(jnp.concatenate([type_sum_b, x], axis=1) @ Wb.T + bb)
        h = x @ W_sa
        Hd = h.shape[1]
        s_left = h @ a_sa[0, :Hd]
        s_right = h @ a_sa[0, Hd:]
        scores = s_left[:, None] + s_right[None, :]
        e = jnp.where(adj_a != 0, jnp.exp(-jax.nn.leaky_relu(scores, 0.01)), 0.0)
        attn = e / (jnp.sum(e, axis=1, keepdims=True) + 1e-05)
        x_a = attn @ h
        x_b = adj_b @ (x @ W_gcnb) + b_gcnb
        return jax.nn.sigmoid(attn_a * x_a + attn_b * x_b)

    def _L0_ffn_ref(x, rw, rb, w1, b1, w2, b2):
        import jax, jax.numpy as jnp
        import numpy as np
        DIM, DEPTH, MULT = (256, 3, 4)
        E = 2 ** DEPTH
        HID = MULT * DIM
        B, S = (4, 512)

        def _leaf_probs(flat_x, rw, rb):
            n_tok = flat_x.shape[0]
            leaf = jnp.ones((n_tok, 1), dtype=flat_x.dtype)
            for d in range(DEPTH):
                off, n = (2 ** d - 1, 2 ** d)
                logits = flat_x @ rw[off:off + n].T + rb[off:off + n]
                p = jax.nn.sigmoid(logits)
                leaf = (leaf[:, :, None] * jnp.stack([1.0 - p, p], axis=2)).reshape(n_tok, 2 * n)
            return leaf
        b, s, dim = x.shape
        flat_x = x.reshape(b * s, dim)
        leaf_probs = _leaf_probs(flat_x, rw, rb)
        h = jnp.einsum('nd,edh->neh', flat_x, w1) + b1[None]
        h = jax.nn.gelu(h, approximate=False)
        y = jnp.einsum('neh,ehd->ned', h, w2) + b2[None]
        out = jnp.einsum('ned,ne->nd', y, leaf_probs)
        return out.reshape(b, s, dim)

    def _L1_gnn_ref(h, adj, W, a_w, a_b, fc_w, fc_b):
        import jax, jax.numpy as jnp
        import numpy as np
        IN_C, HID_C = (256, 256)
        ALPHA = 0.2
        N = 4096
        NEG_BIG = -9000000000000000.0
        Wh1 = h @ W[:IN_C]
        Wh2 = h @ W[IN_C:]
        s1 = Wh1 @ a_w
        s2 = Wh2 @ a_w
        e = s1[:, None] + s2[None, :] + a_b
        e = jnp.where(e >= 0, e, ALPHA * e)
        e = jnp.where(adj > 0, e, NEG_BIG)
        att = jax.nn.softmax(e, axis=1)
        return att @ (h @ fc_w + fc_b)

    def _L1_ffn_ref(x, gate_w, w1, b1, w2, b2):
        import jax, jax.numpy as jnp
        import numpy as np
        D_MODEL = 256
        D_FF = 1024
        NUM_EXPERTS = 8
        TOP_K = 2
        B, S, D = x.shape
        xt = x.reshape(-1, D)
        logits = xt @ gate_w
        probs = jax.nn.softmax(logits, axis=-1)
        top_p, top_i = jax.lax.top_k(probs, TOP_K)
        top_p = top_p / jnp.sum(top_p, axis=-1, keepdims=True)
        w_te = jnp.sum(jax.nn.one_hot(top_i, NUM_EXPERTS, dtype=xt.dtype) * top_p[..., None], axis=1)
        out = jnp.zeros_like(xt)
        for e in range(NUM_EXPERTS):
            h = jax.nn.gelu(xt @ w1[e] + b1[e], approximate=False)
            y = h @ w2[e] + b2[e]
            out = out + w_te[:, e:e + 1] * y
        return out.reshape(B, S, D)
    x = x + _L0_gnn_ref(_layernorm(x, axis=-1), adj, adj, L0_gnn_W_sa, L0_gnn_a_sa, L0_gnn_W_gcnb, L0_gnn_b_gcnb, L0_gnn_Wa, L0_gnn_ba, L0_gnn_Wb, L0_gnn_bb)
    x = x + _L0_ffn_ref(_layernorm(x, axis=-1)[None], L0_ffn_rw, L0_ffn_rb, L0_ffn_w1, L0_ffn_b1, L0_ffn_w2, L0_ffn_b2)[0]
    x = x + _L1_gnn_ref(_layernorm(x, axis=-1), adj, L1_gnn_W, L1_gnn_a_w, L1_gnn_a_b, L1_gnn_fc_w, L1_gnn_fc_b)
    x = x + _L1_ffn_ref(_layernorm(x, axis=-1)[None], L1_ffn_gate_w, L1_ffn_w1, L1_ffn_b1, L1_ffn_w2, L1_ffn_b2)[0]
    return x

_drawn_inputs = setup_inputs


def setup_inputs(seed=0):
    import zlib

    import numpy as np

    out = dict(_drawn_inputs(seed))
    spreads = {'L1_ffn_b1': (0.0, 0.397), 'L1_ffn_b2': (0.0, 0.1)}
    factors = {'L0_gnn_b_gcnb': 7.681, 'L0_ffn_rb': 5.032, 'L0_ffn_b1': 2.893, 'L0_ffn_b2': 3.796}
    for name, (base, spread) in spreads.items():
        noise = np.random.default_rng([zlib.crc32(name.encode()), seed]).standard_normal(out[name].shape)
        drawn = base * np.exp(spread * noise) if base else spread * noise
        out[name] = jnp.asarray(drawn.astype(out[name].dtype))
    for name, factor in factors.items():
        out[name] = (out[name] * factor).astype(out[name].dtype)
    return out
```

```python
from contextlib import ExitStack

import concourse.bass as bass
from concourse import mybir
from concourse.alu_op_type import AluOpType as ALU

ACT = mybir.ActivationFunctionType
AX = mybir.AxisListType
F32 = mybir.dt.float32
F32R = mybir.dt.float32r
U32 = mybir.dt.uint32
ds = bass.ds

P = 128
N = 2048
D = 256
KD = D // P
T = N // P
G = 4
NG = T // G
GW = G * P
E = 8
HID = 1024
HC = HID // P
VW = D + 2
PW = D + 4
RING = 4
LN_EPS = 1e-5
BIG = 3.0e38
LEAK0, LEAK1 = 0.01, 0.2


class Count:

    def __init__(self, eng, sem):
        self.eng, self.sem, self.n = eng, sem, 0

    def link(self, ins):
        ins.then_inc(self.sem, 1)
        self.n = self.n + 1
        self.eng.wait_ge(self.sem, self.n)

    def loop(self, i, per):
        start = self.n
        self.n = i * per + start

        def end(turns):
            self.n = start + per * turns
        return end


def gnn_ffn_program(nc, a):
    with ExitStack() as ctx:
        place = {"at": -(-nc.sbuf_base // 32) * 32}
        limit = nc.sbuf_usable_end

        def sb(name, shape, dt=F32):
            size = 4
            for s in shape[1:]:
                size *= s
            t = nc.alloc_sbuf_tensor_at(name, shape, dt, offset=place["at"])
            place["at"] += -(-size // 32) * 32
            assert place["at"] <= limit, (name, place["at"] - limit)
            return t

        def sem(name):
            return ctx.enter_context(nc.semaphore(name))

        PS = ctx.enter_context(nc.psum_tensor("PS", [P, 8, 512], F32))

        X = sb("X", [P, T, D])
        ident = sb("ident", [P, P])
        ones = sb("ones", [P, P])
        ones_r = sb("ones_r", [P, P], F32R)
        ln_stat = sb("ln_stat", [P, T, 6])
        ln_mv = sb("ln_mv", [P, T, 2])
        ln_var = sb("ln_var", [P, T])
        ln_rstd = sb("ln_rstd", [P, T])
        ln_t = sb("ln_t", [P, T])
        minus_half = sb("minus_half", [P, T])
        xn = sb("xn", [P, G, D])
        diag = sb("diag", [P, G, P])
        cols = sb("cols", [P, T, 4])
        cols2 = sb("cols2", [P, T, 4])
        shared_end = place["at"]

        xr_hi = sb("xr_hi", [P, G, KD, P], F32R)
        xr_lo = sb("xr_lo", [P, G, KD, P], F32R)
        w_raw = sb("w_raw", [P, KD, VW])
        w_hi = sb("w_hi", [P, KD, VW], F32R)
        w_lo = sb("w_lo", [P, KD, VW], F32R)
        h_raw = sb("h_raw", [P, KD, PW])
        h_hi = sb("h_hi", [P, KD, PW], F32R)
        h_lo = sb("h_lo", [P, KD, PW], F32R)
        vec_row = sb("vec_row", [P, 2 * D])
        bias_row = sb("bias_row", [P, D])
        gate_bias = sb("gate_bias", [P, 2])
        scratch = sb("scratch", [P, D])
        graph_w_end = place["at"]
        row_a = sb("row_a", [P, N])
        at = sb("at", [P, RING, GW])
        e1 = sb("e1", [P, 2, GW])
        e2 = sb("e2", [P, 2, GW])
        ee = sb("ee", [P, 2, GW])
        em = sb("em", [P, 2, GW])
        e_hi = sb("e_hi", [P, RING, GW], F32R)
        e_lo = sb("e_lo", [P, RING, GW], F32R)
        stage = sb("stage", [P, G, 2, VW])
        small = sb("small", [P, 8, G])
        zt = sb("zt", [P, G, D])
        th = sb("th", [P, G, D])
        hh = sb("hh", [P, T, VW], F32R)
        hl = sb("hl", [P, T, VW], F32R)
        graph_end = place["at"]
        a_hi = sb("a_hi", [P, RING, GW], F32R)
        a_lo = sb("a_lo", [P, RING, GW], F32R)
        vh = sb("vh", [P, T, VW], F32R)
        vl = sb("vl", [P, T, VW], F32R)

        place["at"] = graph_end
        row_b = sb("row_b", [P, N])
        s2_row = sb("s2_row", [P, N])
        s2_pos = sb("s2_pos", [P, N])
        adj_rows = sb("adj_rows", [P, 2, N])
        masked = sb("masked", [P, 2, N])
        mean_row = sb("mean_row", [P, D])
        s2_min = sb("s2_min", [P, 1])
        mx = sb("mx", [P, 8, T])
        ff = sb("ff", [P, 2, D])

        place["at"] = shared_end
        xt_hi = sb("xt_hi", [P, KD, N], F32R)
        xt_lo = sb("xt_lo", [P, KD, N], F32R)
        acc = sb("acc", [P, KD, N])
        g_row = sb("g_row", [P, N], F32R)
        w1_raw = sb("w1_raw", [P, KD, HID])
        w2_raw = sb("w2_raw", [P, HC, D])
        w1_hi = sb("w1_hi", [P, 2, KD, HID], F32R)
        w1_lo = sb("w1_lo", [P, 2, KD, HID], F32R)
        w2_hi = sb("w2_hi", [P, 2, HC, D], F32R)
        w2_lo = sb("w2_lo", [P, 2, HC, D], F32R)
        hf = sb("hf", [P, 2, GW])
        hid_hi = sb("hid_hi", [P, RING, GW], F32R)
        hid_lo = sb("hid_lo", [P, RING, GW], F32R)
        gate_b = sb("gate_b", [P, 2, GW])
        yt = sb("yt", [P, 2, GW])
        b1_cols = sb("b1_cols", [P, E, HC])
        b2_cols = sb("b2_cols", [P, E, KD])
        place_gate = place["at"]
        gw_raw = sb("gw_raw", [P, KD, P])
        gw_hi = sb("gw_hi", [P, KD, P], F32R)
        gw_lo = sb("gw_lo", [P, KD, P], F32R)
        lg_t = sb("lg_t", [P, GW])
        lg = sb("lg", [P, G, E])
        pq = sb("pq", [P, 2, G, E])
        tree = sb("tree", [P, 2, G, E])
        gate = sb("gate", [P, G, E])
        gate_hi = sb("gate_hi", [P, G, E], F32R)
        gate2 = sb("gate2", [P, G, P])
        rb_col = sb("rb_col", [P, 1])
        top = sb("top", [P, G, 8])
        topi = sb("topi", [P, G, 8], U32)
        topf = sb("topf", [P, G, 8])
        iota8 = sb("iota8", [P, 8])
        hot = sb("hot", [P, G, 8])
        sel_f = sb("sel_f", [P, E, P])
        sel = sb("sel", [P, 2, P], F32R)

        x_in = [sem(f"x_in{g}") for g in range(NG)]
        w_in = sem("w_in")
        const_ready = sem("const_ready")
        pool_seq = sem("pool_seq")
        dve_seq = sem("dve_seq")
        act_seq = sem("act_seq")
        wts_hi = sem("wts_hi")
        wts_ready = sem("wts_ready")
        var_ready = sem("var_ready")
        rstd_ready = sem("rstd_ready")
        xn_ready = sem("xn_ready")
        xt_psum = sem("xt_psum")
        xt_hi_ready = sem("xt_hi_ready")
        xt_lo_ready = sem("xt_lo_ready")
        proj_done = sem("proj_done")
        proj_hi = sem("proj_hi")
        proj_out = sem("proj_out")
        diag_ready = sem("diag_ready")
        row_psum = sem("row_psum")
        row_copied = sem("row_copied")
        h_free = sem("h_free")
        nat_in = [sem(f"nat_in{i}") for i in range(2)]
        nat_used = sem("nat_used")
        max_cols = sem("max_cols")
        mean_psum = sem("mean_psum")
        x_done = sem("x_done")
        out_done = sem("out_done")

        waited = {e.engine: sem(f"waited_{k}") for k, e in
                  (("act", nc.scalar), ("pe", nc.tensor), ("dve", nc.vector))}

        def graph_sems(n):
            s = {k: sem(f"{k}_{n}") for k in (
                "exp_ready", "exp_used", "mask_done", "ehi_ready", "elo_ready", "ahi_ready", "alo_ready",
                "step_done", "acc_e", "acc_a", "st_e", "st_a", "fin", "z_ready", "th_ready")}
            s["at_in"] = [sem(f"at_in{i}_{n}") for i in range(RING)]
            return s

        def ffn_sems(n):
            return {k: sem(f"{k}_{n}") for k in (
                "lgt_psum", "lgt_ready", "lg_psum", "gate2_ready", "g2_psum", "g_row_ready",
                "raw1_in", "raw2_in", "split_done", "whi", "hid_psum", "hid_act", "hi_ready", "lo_ready",
                "hid_used", "y_done", "y_free", "y_tmp", "acc_done", "back_psum", "back_done",
                "aux_in", "e_ready", "tree_in")}

        GS = [graph_sems(0), graph_sems(1)]
        FS = [ffn_sems(0), ffn_sems(1)]

        def alone(eng):
            eng.sem_inc(waited[eng.engine], 1)

        def bank(i, lo, hi):
            return PS[:, i:i + 1, lo:hi]

        x_v = a["x"].rearrange("(g t p) d -> g p t d", p=P, t=G)
        out_v = a["out"].rearrange("(g t p) d -> g p t d", p=P, t=G)
        adj_v = a["adj"].rearrange("(t p) n -> p t n", p=P)
        adj_t = a["adj_t"].rearrange("(j p) (b w) -> j p b w", p=P, w=GW)
        block = ctx.enter_context(nc.Block())

        @block.sync
        def _(sp):
            def weights(src, dst, slow=False):
                sp.dma_start(dst, src, allow_slow_non_contiguous=slow).then_inc(w_in, 16)

            def chunked(w):
                return w.rearrange("(k p) n -> p k n", p=P)

            def column(v):
                return v.rearrange("(k p o) -> p k o", p=P, o=1)

            def adj_stream(s):
                with sp.Fori(0, NG) as ib:
                    for j in range(T):
                        n = ib * T + j
                        sp.wait_ge(s["mask_done"], n + 1)
                        if s is GS[0]:
                            sp.wait_ge(s["alo_ready"], n + 1)
                        sp.dma_start(at[:, j % RING:j % RING + 1, :], adj_t[j][:, ds(ib, 1), :]).then_inc(s["at_in"][j % RING], 16)

            def expert_weights(s, w1, w2, e, turn):
                sp.wait_ge(s["split_done"], turn)
                sp.dma_start(w1_raw[:, :, :], w1[e].rearrange("(k p) n -> p k n", p=P)).then_inc(s["raw1_in"], 16)
                sp.dma_start(w2_raw[:, :, :], w2[e].rearrange("(c p) n -> p c n", p=P)).then_inc(s["raw2_in"], 16)

            def ffn_loads(layer):
                s = FS[layer]
                name = f"L{layer}_ffn_"
                gw = a["L0_ffn_rw_t"] if layer == 0 else a["L1_ffn_gate_w"]
                n_logit = E - 1 if layer == 0 else E
                sp.wait_ge(x_done, 2 * layer * T + T)
                sp.dma_start(b1_cols[:, :, :], a[name + "b1_p"]).then_inc(s["aux_in"], 16)
                sp.dma_start(b2_cols[:, :, :], a[name + "b2_p"]).then_inc(s["aux_in"], 16)
                sp.wait_ge(s["tree_in"], 1)
                if layer == 0:
                    sp.dma_start(rb_col[0:E - 1, :], a["L0_ffn_rb"].rearrange("(e o) -> e o", o=1), allow_slow_non_contiguous=True).then_inc(s["aux_in"], 16)
                sp.dma_start(gw_raw[:, :, 0:n_logit], chunked(gw)).then_inc(s["aux_in"], 16)
                w1, w2 = a[name + "w1"], a[name + "w2"]
                sp.dma_start(w1_raw[:, :, :], w1[0].rearrange("(k p) n -> p k n", p=P)).then_inc(s["raw1_in"], 16)
                sp.dma_start(w2_raw[:, :, :], w2[0].rearrange("(c p) n -> p c n", p=P)).then_inc(s["raw2_in"], 16)
                for e in range(1, E):
                    expert_weights(s, w1, w2, e, e * NG)

            weights(chunked(a["L0_gnn_W_gcnb"]), w_raw[:, :, 0:D])
            weights(column(a["L0_gnn_Wa"][0, 0:D]), w_raw[:, :, D:D + 1], slow=True)
            weights(column(a["L0_gnn_Wb"][0, 0:D]), w_raw[:, :, D + 1:D + 2], slow=True)
            weights(chunked(a["L0_gnn_W_sa"]), h_raw[:, :, 0:D])
            weights(column(a["L0_gnn_Wa"][0, D:2 * D]), h_raw[:, :, D + 2:D + 3], slow=True)
            weights(column(a["L0_gnn_Wb"][0, D:2 * D]), h_raw[:, :, D + 3:D + 4], slow=True)
            weights(a["L0_gnn_a_sa"][0, :].partition_broadcast(P), vec_row[:, :])
            weights(a["L0_gnn_b_gcnb"].partition_broadcast(P), bias_row[:, :])
            weights(a["L0_gnn_ba"].partition_broadcast(P), gate_bias[:, 0:1])
            weights(a["L0_gnn_bb"].partition_broadcast(P), gate_bias[:, 1:2])
            for g in range(NG):
                sp.dma_start(X[:, g * G:(g + 1) * G, :], x_v[g]).then_inc(x_in[g], 16)
            adj_stream(GS[0])
            ffn_loads(0)

            sp.wait_ge(x_done, 2 * T)
            weights(chunked(a["L1_gnn_fc_w"]), w_raw[:, :, 0:D])
            weights(chunked(a["L1_gnn_W"][0:D, :]), h_raw[:, :, 0:D])
            weights(a["L1_gnn_a_w"].partition_broadcast(P), vec_row[:, 0:D])
            weights(a["L1_gnn_fc_b"].partition_broadcast(P), bias_row[:, :])
            weights(a["L1_gnn_a_b"].partition_broadcast(P), gate_bias[:, 0:1])
            sp.wait_ge(h_free, 1)
            weights(chunked(a["L1_gnn_W"][D:2 * D, :]), h_raw[:, :, 0:D])
            with sp.Fori(0, T // 2) as q:
                for r in range(2):
                    sp.wait_ge(nat_used, q * 2 + r + 1)
                    sp.dma_start(adj_rows[:, r:r + 1, :], adj_v[:, ds(q * 2 + r, 1), :]).then_inc(nat_in[r], 16)
            adj_stream(GS[1])
            ffn_loads(1)

            for g in range(NG):
                sp.wait_ge(x_done, 3 * T + (g + 1) * G)
                sp.dma_start(out_v[g], X[:, g * G:(g + 1) * G, :]).then_inc(out_done, 16)
            sp.wait_ge(out_done, 16 * NG)

        @block.gpsimd
        def _(pool):
            seq = Count(pool, pool_seq)
            seq.link(pool.memset(ident[:, :], 0.0))
            pool.affine_select(out=ident[:, :], in_=ident[:, :], compare_op=ALU.not_equal, fill=1.0, base=0,
                               pattern=[[-1, P]], channel_multiplier=1).then_inc(const_ready, 1)
            pool.memset(ones[:, :], 1.0).then_inc(const_ready, 1)
            pool.memset(minus_half[:, :], -0.5).then_inc(const_ready, 1)
            pool.memset(zt[:, 0, 0:T], 1.0).then_inc(const_ready, 1)
            pool.memset(zt[:, 1, 0:T], 0.0).then_inc(const_ready, 1)

            def rstd(stage_no):
                pool.wait_ge(var_ready, stage_no + 1)
                pool.tensor_tensor(ln_rstd[:, :], ln_var[:, :], minus_half[:, :], ALU.pow).then_inc(rstd_ready, 1)

            def ffn_consts(layer):
                s = FS[layer]
                pool.wait_ge(x_done, 2 * layer * T + T)
                pool.memset(gate2[:, :, :], 0.0).then_inc(pool_seq, 1)
                pool.memset(sel_f[:, :, :], 0.0).then_inc(pool_seq, 1)
                pool.memset(rb_col[:, :], 0.0).then_inc(pool_seq, 1)
                seq.n += 3
                seq.link(pool.memset(gw_raw[:, :, :], 0.0))
                pool.sem_inc(s["tree_in"], 1)
                seq.link(pool.affine_select(out=sel_f[:, :, :], in_=sel_f[:, :, :], compare_op=ALU.not_equal,
                                            fill=1.0, base=0, pattern=[[-1, E], [0, P]], channel_multiplier=1))
                seq.link(pool.affine_select(out=sel_f[:, :, :], in_=sel_f[:, :, :], compare_op=ALU.not_equal,
                                            fill=1.0, base=-E, pattern=[[-1, E], [0, P]], channel_multiplier=1))
                pool.iota(iota8[:, :], pattern=[[1, 8]], base=0, channel_multiplier=0,
                          allow_small_or_imprecise_dtypes=True).then_inc(s["tree_in"], 1)

            rstd(0)
            s = GS[0]
            with pool.Fori(0, NG) as ib:
                for j in range(T):
                    n = ib * T + j
                    pool.wait_ge(s["ahi_ready"], n + 1)
                    pool.wait_ge(s["step_done"], n + 1)
                    pool.tensor_tensor(a_lo[:, j % RING, :], at[:, j % RING, :], a_hi[:, j % RING, :].bitcast(F32),
                                       ALU.subtract).then_inc(s["alo_ready"], 1)
            ffn_consts(0)
            rstd(1)
            rstd(2)
            s = GS[1]
            with pool.Fori(0, NG) as ib:
                for j in range(T):
                    n = ib * T + j
                    pool.wait_ge(s["ehi_ready"], n + 1)
                    pool.wait_ge(s["step_done"], n + 1)
                    pool.tensor_tensor(e_lo[:, j % RING, :], em[:, j % 2, :], e_hi[:, j % RING, :].bitcast(F32),
                                       ALU.subtract).then_inc(s["elo_ready"], 1)
            ffn_consts(1)
            rstd(3)

        @block.scalar
        def _(act):
            def high_parts_of_x(stage_no, g, wide):
                for u in range(G):
                    act.wait_ge(xt_psum, g * G + u + 1 + stage_no * T)
                    src = PS[:, u, 0:D].rearrange("p (k n) -> p k n", k=KD)
                    dst = xt_hi[:, :, ds((g * G + u) * P, P)] if wide else xr_hi[:, u, :, :]
                    alone(act)
                    act.activation(dst, src, ACT.Copy).then_inc(xt_hi_ready, 1)

            def rows_out(k, dst):
                with act.Fori(0, NG) as q:
                    act.wait_ge(row_psum, (k * NG + 2) + q)
                    alone(act)
                    act.activation(dst[:, ds(q * GW, GW)], PS[:, 0, :], ACT.Copy).then_inc(row_copied, 1)

            def ffn(layer):
                s = FS[layer]
                with act.Fori(0, NG) as g:
                    high_parts_of_x(1 + 2 * layer, g, True)
                    act.wait_ge(s["lgt_psum"], g + 1)
                    if layer == 0:
                        act.activation(lg_t[:, :], PS[:, 4, :], ACT.Tanh, bias=rb_col[:, :], scale=0.5).then_inc(s["lgt_ready"], 1)
                    else:
                        act.activation(lg_t[:, :], PS[:, 4, :], ACT.Copy).then_inc(s["lgt_ready"], 1)
                        for u in range(G):
                            act.wait_ge(s["e_ready"], g * G + u + 1)
                            act.activation(lg[:, u, :], lg[:, u, :], ACT.Exp, bias=topf[:, u, 7:8], scale=1.0).then_inc(act_seq, 1)
                    act.wait_ge(s["g2_psum"], g + 1)
                    alone(act)
                    act.activation(g_row[:, ds(g * GW, GW)], PS[:, 6, :], ACT.Copy).then_inc(s["g_row_ready"], 1)

                act.wait_ge(s["aux_in"], 16 * (4 if layer == 0 else 3))
                with act.Fori(0, E) as e:
                    with act.Fori(0, 2) as gp:
                        for pg in range(2):
                            n = e * NG + gp * 2 + pg
                            for c in range(HC + 1):
                                act.wait_ge(s["hid_psum"], n * (HC + 1) + c + 1)
                                if c == 0:
                                    act.wait_ge(s["acc_done"], n + 1)
                                    act.activation(gate_b[:, pg, :], PS[:, 0, :], ACT.Copy).then_inc(s["hid_act"], 1)
                                else:
                                    act.wait_ge(s["lo_ready"], n * HC + c)
                                    alone(act)
                                    act.activation(hf[:, (c - 1) % 2, :], PS[:, c % 3, :], ACT.Gelu,
                                                   bias=b1_cols[:, ds(e, 1), c - 1], scale=1.0).then_inc(s["hid_act"], 1)

            act.wait_ge(const_ready, 5)
            act.activation(hh[:, :, D:D + 1].rearrange("p t o -> p (t o)"), zt[:, 0, 0:T], ACT.Copy).then_inc(act_seq, 1)
            act.activation(hh[:, :, D + 1:D + 2].rearrange("p t o -> p (t o)"), zt[:, 1, 0:T], ACT.Copy).then_inc(act_seq, 1)
            act.activation(hl[:, :, D:D + 1].rearrange("p t o -> p (t o)"), zt[:, 1, 0:T], ACT.Copy).then_inc(act_seq, 1)
            act.activation(hl[:, :, D + 1:D + 2].rearrange("p t o -> p (t o)"), zt[:, 1, 0:T], ACT.Copy).then_inc(act_seq, 1)
            act.activation(ones_r[:, :], ones[:, :], ACT.Copy).then_inc(act_seq, 1)
            with act.Fori(0, NG) as g:
                high_parts_of_x(0, g, False)
                for u in range(G):
                    act.wait_ge(proj_done, g * G + u + 1)
                    alone(act)
                    act.activation(vh[:, ds(g * G + u, 1), :], bank(4 + u % 2, 0, VW), ACT.Copy).then_inc(proj_hi, 1)
                    act.activation(hh[:, ds(g * G + u, 1), 0:D], bank(6 + u % 2, 0, D), ACT.Copy).then_inc(proj_hi, 1)
            rows_out(0, row_a)

            def graph_steps(s, layer):
                ra, rb = (row_a, row_a) if layer == 0 else (row_a, row_b)
                k1, k2 = (-1.0, -LEAK0) if layer == 0 else (1.0, 1.0)
                with act.Fori(0, NG) as ib:
                    for j in range(T):
                        n = ib * T + j
                        act.wait_ge(s["exp_used"], n + 1)
                        alone(act)
                        act.activation(e1[:, j % 2, :], ra[:, ds(ib * GW, GW)], ACT.Exp, bias=cols2[:, j, 0:1],
                                       scale=k1).then_inc(s["exp_ready"], 1)
                        act.activation(e2[:, j % 2, :], rb[:, ds(ib * GW, GW)], ACT.Exp, bias=cols2[:, j, 1:2],
                                       scale=k2).then_inc(s["exp_ready"], 1)
                        if layer == 0:
                            act.wait_ge(s["at_in"][j % RING], (ib * (T // RING) + j // RING + 1) * 16)
                            act.wait_ge(s["step_done"], n + 1)
                            act.activation(a_hi[:, j % RING, :], at[:, j % RING, :], ACT.Copy).then_inc(s["ahi_ready"], 1)
                    for it in range(G):
                        if layer == 0:
                            act.wait_ge(s["acc_e"], ib * G + it + 1)
                        elif it < G - 1:
                            act.wait_ge(s["acc_e"], ib * (G - 1) + it + 1)
                        else:
                            act.wait_ge(s["step_done"], ib * T + T + RING)
                        act.wait_ge(s["fin"], ib + 1)
                        act.activation(stage[:, it, 0, :], PS[:, it, 0:VW], ACT.Copy).then_inc(s["st_e"], 1)
                    if layer == 0:
                        for k in range(2):
                            act.wait_ge(s["z_ready"], ib * 2 + k + 1)
                            if k == 0:
                                act.activation(small[:, 4:6, :], small[:, 2:4, :], ACT.Tanh, scale=0.5).then_inc(s["th_ready"], 1)
                            else:
                                act.activation(th[:, :, :], zt[:, :, :], ACT.Tanh, scale=0.5).then_inc(s["th_ready"], 1)

            act.wait_ge(wts_ready, 2)
            graph_steps(GS[0], 0)
            ffn(0)
            act.wait_ge(const_ready, 5)
            with act.Fori(0, NG) as g:
                high_parts_of_x(2, g, False)
                for u in range(G):
                    act.wait_ge(proj_out, g * G + u + 1 + T)
                    alone(act)
                    act.activation(hh[:, ds(g * G + u, 1), 0:D], ff[:, u % 2:u % 2 + 1, :], ACT.Copy).then_inc(proj_hi, 1)
            rows_out(1, s2_row)
            rows_out(2, row_a)
            rows_out(3, row_b)
            graph_steps(GS[1], 1)
            ffn(1)

        @block.tensor
        def _(pe):
            def three(out, l_hi, l_lo, r_hi, r_lo, start, stop, sem_of=None):
                pe.matmul(out, l_hi, r_hi, start=start, stop=False)
                pe.matmul(out, l_hi, r_lo, start=False, stop=False)
                m = pe.matmul(out, l_lo, r_hi, start=False, stop=stop)
                if sem_of is not None:
                    m.then_inc(sem_of, 1)

            def transposes_of_x(stage_no, g):
                for u in range(G):
                    pe.wait_ge(xn_ready, g * G + u + 1 + stage_no * T)
                    pe.transpose(PS[:, u, 0:P], xn[:, u, 0:P], ident[:, :])
                    pe.transpose(PS[:, u, P:D], xn[:, u, P:D], ident[:, :]).then_inc(xt_psum, 1)

            def rows(k):
                alone(pe)
                with pe.Fori(0, NG) as q:
                    for r in range(G):
                        pe.wait_ge(diag_ready, q * G + (k * T + r + 1))
                        m = pe.matmul(PS[:, 0, r * P:(r + 1) * P], ones[:, :], diag[:, r, :], start=True, stop=True)
                    m.then_inc(row_psum, 1)
                    pe.wait_ge(row_copied, q + (k * NG + 1))

            def graph_steps(s, layer):
                alone(pe)
                with pe.Fori(0, NG) as ib:
                    for j in range(T):
                        n = ib * T + j
                        pe.wait_ge(s["elo_ready"], n + 1)
                        for it in range(G):
                            if j == 0:
                                pe.wait_ge(s["st_e"], ib * G + it + 1)
                            w = slice(it * P, (it + 1) * P)
                            done = s["acc_e"] if j == T - 1 else None
                            if layer == 1 and it == G - 1:
                                done = s["step_done"]
                            three(PS[:, it, 0:VW], e_hi[:, j % RING, w], e_lo[:, j % RING, w],
                                  hh[:, j, :], hl[:, j, :], j == 0, j == T - 1, done)
                        if layer == 1:
                            continue
                        pe.wait_ge(s["alo_ready"], n + 1 + RING)
                        for it in range(G):
                            if j == 0:
                                pe.wait_ge(s["st_a"], ib * G + it + 1)
                            w = slice(it * P, (it + 1) * P)
                            done = s["acc_a"] if j == T - 1 and it < G - 1 else s["step_done"] if it == G - 1 else None
                            three(PS[:, 4 + it, 0:VW], a_hi[:, j % RING, w], a_lo[:, j % RING, w],
                                  vh[:, j, :], vl[:, j, :], j == 0, j == T - 1, done)

            def ffn(layer):
                s = FS[layer]
                pe.wait_ge(wts_ready, 3 if layer == 0 else 6)
                alone(pe)
                with pe.Fori(0, NG) as g:
                    transposes_of_x(1 + 2 * layer, g)
                    pe.wait_ge(xt_lo_ready, (g + 1) * G + (1 + 2 * layer) * T)
                    for k in range(KD):
                        three(PS[:, 4, :], gw_hi[:, k, :], gw_lo[:, k, :], xt_hi[:, k, ds(g * GW, GW)],
                              xt_lo[:, k, ds(g * GW, GW)], k == 0, k == KD - 1,
                              s["lgt_psum"] if k == KD - 1 else None)
                    pe.wait_ge(s["lgt_ready"], g + 1)
                    for u in range(G):
                        m = pe.transpose(PS[:, 5, u * P:(u + 1) * P], lg_t[:, u * P:(u + 1) * P], ident[:, :])
                    m.then_inc(s["lg_psum"], 1)
                    pe.wait_ge(s["gate2_ready"], g + 1)
                    for u in range(G):
                        m = pe.transpose(PS[:, 6, u * P:(u + 1) * P], gate2[:, u, :], ident[:, :])
                    m.then_inc(s["g2_psum"], 1)
                pe.wait_ge(s["g_row_ready"], NG)

                def second(n, pg, c, par):
                    pe.wait_ge(s["lo_ready"], n * HC + c + 3)
                    if c == 0:
                        pe.wait_ge(s["y_free"], n + 1)
                    for d in range(KD):
                        w = slice(d * P, (d + 1) * P)
                        last = c == HC - 1
                        three(PS[:, 3 + 2 * pg + d, :], w2_hi[:, par, c, w], w2_lo[:, par, c, w],
                              hid_hi[:, c % RING, :], hid_lo[:, c % RING, :], c == 0, last,
                              s["hid_used"] if d == KD - 1 else s["y_done"] if last else None)

                alone(pe)
                with pe.Fori(0, E // 2) as ep:
                    for par in range(2):
                        e = ep * 2 + par
                        pe.wait_ge(s["split_done"], (e + 1) * NG)
                        alone(pe)
                        with pe.Fori(0, 2) as gp:
                            for pg in range(2):
                                n = e * NG + gp * 2 + pg
                                gcol = (gp * 2 + pg) * GW
                                for c in range(HC + 1):
                                    pe.wait_ge(s["hid_act"], n * (HC + 1) + c + 1)
                                    if c == 0:
                                        pe.matmul(PS[:, 0, :], sel[:, par, :], g_row[:, ds(gcol, GW)],
                                                  start=True, stop=True).then_inc(s["hid_psum"], 1)
                                        continue
                                    w = slice((c - 1) * P, c * P)
                                    for k in range(KD):
                                        three(PS[:, c % 3, :], w1_hi[:, par, k, w], w1_lo[:, par, k, w],
                                              xt_hi[:, k, ds(gcol, GW)], xt_lo[:, k, ds(gcol, GW)], k == 0, k == KD - 1,
                                              s["hid_psum"] if k == KD - 1 else None)
                                    if c >= 3:
                                        second(n, pg, c - 3, par)
                                second(n, pg, HC - 2, par)
                                second(n, pg, HC - 1, par)
                for t in range(T):
                    pe.wait_ge(s["acc_done"], E * NG + 2)
                    if t >= G:
                        pe.wait_ge(s["back_done"], t - G + 1)
                    for d in range(KD):
                        m = pe.transpose(PS[:, t % G, d * P:(d + 1) * P], acc[:, d, t * P:(t + 1) * P], ident[:, :])
                    m.then_inc(s["back_psum"], 1)

            pe.wait_ge(const_ready, 5)
            pe.wait_ge(wts_ready, 1)
            with pe.Fori(0, NG) as g:
                transposes_of_x(0, g)
                for u in range(G):
                    pe.wait_ge(xt_lo_ready, g * G + u + 1)
                    if u >= 2:
                        pe.wait_ge(proj_out, g * G + u - 1)
                    for k in range(KD):
                        three(PS[:, 4 + u % 2, 0:VW], xr_hi[:, u, k, :], xr_lo[:, u, k, :], w_hi[:, k, :], w_lo[:, k, :],
                              k == 0, k == KD - 1)
                    for k in range(KD):
                        three(PS[:, 6 + u % 2, 0:PW], xr_hi[:, u, k, :], xr_lo[:, u, k, :], h_hi[:, k, :], h_lo[:, k, :],
                              k == 0, k == KD - 1, proj_done if k == KD - 1 else None)
            rows(0)
            graph_steps(GS[0], 0)
            ffn(0)
            pe.wait_ge(wts_ready, 4)
            with pe.Fori(0, NG) as g:
                transposes_of_x(2, g)
                for u in range(G):
                    pe.wait_ge(xt_lo_ready, g * G + u + 1 + 2 * T)
                    if u >= 2:
                        pe.wait_ge(proj_out, g * G + u - 1 + T)
                    for k in range(KD):
                        three(PS[:, 4 + u % 2, 0:VW], xr_hi[:, u, k, :], xr_lo[:, u, k, :], w_hi[:, k, :], w_lo[:, k, :],
                              k == 0, k == KD - 1, proj_done if k == KD - 1 else None)
            pe.wait_ge(wts_ready, 5)
            for j in range(T):
                pe.matmul(PS[:, 6, 0:D], ones_r[:, :], hh[:, j, 0:D], start=j == 0, stop=False)
                m = pe.matmul(PS[:, 6, 0:D], ones_r[:, :], hl[:, j, 0:D], start=False, stop=j == T - 1)
            m.then_inc(mean_psum, 1)
            for k in (1, 2, 3):
                rows(k)
            graph_steps(GS[1], 1)
            ffn(1)

        @block.vector
        def _(dve):
            seq = Count(dve, dve_seq)
            V = nc.vector

            for s in GS:
                dve.sem_inc(s["exp_used"], 2)
                dve.sem_inc(s["mask_done"], RING)
                dve.sem_inc(s["alo_ready"], RING)
                dve.sem_inc(s["step_done"], RING)
                dve.sem_inc(s["st_e"], G)
                dve.sem_inc(s["st_a"], G)
                dve.sem_inc(s["fin"], 1)
            for s in FS:
                dve.sem_inc(s["hid_act"], 3)
                dve.sem_inc(s["lo_ready"], 2)
                dve.sem_inc(s["hid_used"], RING)
                dve.sem_inc(s["y_free"], 2)
                dve.sem_inc(s["acc_done"], 2)
            dve.sem_inc(row_psum, 1)
            dve.sem_inc(nat_used, 2)

            def norm_stats(stage_no):
                for t in range(T):
                    if stage_no == 0 and t % G == 0:
                        dve.wait_ge(x_in[t // G], 16)
                    V.bn_stats(ln_stat[:, t, :], X[:, t, :]).then_inc(dve_seq, 1)
                    seq.n += 1
                dve.wait_ge(dve_seq, seq.n)
                for t in range(T):
                    V.bn_aggr(ln_mv[:, t, :], ln_stat[:, t, :]).then_inc(dve_seq, 1)
                    seq.n += 1
                dve.wait_ge(dve_seq, seq.n)
                V.tensor_scalar(ln_var[:, :], ln_mv[:, :, 1], LN_EPS, None, ALU.add).then_inc(var_ready, 1)
                dve.wait_ge(rstd_ready, stage_no + 1)
                seq.link(V.tensor_tensor(ln_t[:, :], ln_rstd[:, :], ln_rstd[:, :], ALU.mult))
                seq.link(V.tensor_tensor(ln_t[:, :], ln_t[:, :], ln_var[:, :], ALU.mult))
                seq.link(V.tensor_scalar(ln_t[:, :], ln_t[:, :], -0.5, 1.5, ALU.mult, ALU.add))
                seq.link(V.tensor_tensor(ln_rstd[:, :], ln_rstd[:, :], ln_t[:, :], ALU.mult))

            def normalise(stage_no, g, wide):
                for u in range(G):
                    t = g * G + u
                    V.tensor_scalar(xn[:, u:u + 1, :], X[:, ds(t, 1), :], ln_mv[:, ds(t, 1), 0], ln_rstd[:, ds(t, 1)],
                                    ALU.subtract, ALU.mult).then_inc(xn_ready, 1)
                for u in range(G):
                    dve.wait_ge(xt_hi_ready, g * G + u + 1 + stage_no * T)
                    src = PS[:, u, 0:D].rearrange("p (k n) -> p k n", k=KD)
                    tok = ds((g * G + u) * P, P)
                    hi = xt_hi[:, :, tok] if wide else xr_hi[:, u, :, :]
                    lo = xt_lo[:, :, tok] if wide else xr_lo[:, u, :, :]
                    V.tensor_tensor(lo, src, hi.bitcast(F32), ALU.subtract).then_inc(xt_lo_ready, 1)

            def split(raw, hi, lo):
                seq.link(V.tensor_copy(hi, raw))
                seq.link(V.tensor_tensor(lo, raw, hi.bitcast(F32), ALU.subtract))

            def diagonals(k, col):
                alone(dve)
                with dve.Fori(0, NG) as q:
                    dve.wait_ge(row_psum, q + (k * NG + 1))
                    for r in range(G):
                        V.tensor_scalar(diag[:, r, :], ident[:, :], col(q * G + r), None, ALU.mult).then_inc(diag_ready, 1)

            def product_column(dst, w, row):
                seq.link(V.tensor_tensor_reduce(scratch[:, :], w, row, 1.0, 0.0, ALU.mult, ALU.add, dst))

            dve.wait_ge(const_ready, 5)
            dve.wait_ge(w_in, 160)
            for k in range(KD):
                product_column(h_raw[:, k, D:D + 1], h_raw[:, k, 0:D], vec_row[:, 0:D])
                product_column(h_raw[:, k, D + 1:D + 2], h_raw[:, k, 0:D], vec_row[:, D:2 * D])
            split(w_raw[:, :, :], w_hi[:, :, :], w_lo[:, :, :])
            seq.link(V.tensor_copy(h_hi[:, :, :], h_raw[:, :, :]))
            V.tensor_tensor(h_lo[:, :, :], h_raw[:, :, :], h_hi[:, :, :].bitcast(F32), ALU.subtract).then_inc(wts_ready, 1)
            norm_stats(0)
            with dve.Fori(0, NG) as g:
                normalise(0, g, False)
                for u in range(G):
                    t = ds(g * G + u, 1)
                    dve.wait_ge(proj_hi, (g * G + u) * 2 + 2)
                    V.tensor_tensor(vl[:, t, :], bank(4 + u % 2, 0, VW), vh[:, t, :].bitcast(F32), ALU.subtract)
                    V.tensor_tensor(hl[:, t, 0:D], bank(6 + u % 2, 0, D), hh[:, t, 0:D].bitcast(F32), ALU.subtract)
                    V.tensor_copy(cols[:, t, :], bank(6 + u % 2, D, D + 4)).then_inc(proj_out, 1)
            dve.wait_ge(proj_out, T)
            seq.link(V.tensor_scalar(cols2[:, :, 0], cols[:, :, 1], -1.0, None, ALU.mult))
            V.tensor_scalar(cols2[:, :, 1], cols[:, :, 1], -LEAK0, None, ALU.mult).then_inc(wts_ready, 1)
            for k in range(2):
                seq.link(V.tensor_scalar(cols2[:, :, 2 + k], cols[:, :, 2 + k], gate_bias[:, k:k + 1], None, ALU.add))
            diagonals(0, lambda t: cols[:, ds(t, 1), 0])
            s = GS[0]
            with dve.Fori(0, NG) as ib:
                for j in range(T):
                    n = ib * T + j
                    b, r = j % 2, j % RING
                    dve.wait_ge(s["exp_ready"], n * 2 + 2)
                    V.scalar_tensor_tensor(out=ee[:, b, :], in0=e1[:, b, :], scalar=BIG, in1=e2[:, b, :],
                                           op0=ALU.min, op1=ALU.min).then_inc(s["exp_used"], 1)
                    dve.wait_ge(s["exp_used"], n + 3)
                    dve.wait_ge(s["at_in"][r], (ib * (T // RING) + j // RING + 1) * 16)
                    V.scalar_tensor_tensor(out=em[:, b, :], in0=at[:, r, :], scalar=0.0, in1=ee[:, b, :],
                                           op0=ALU.not_equal, op1=ALU.mult).then_inc(s["mask_done"], 1)
                    dve.wait_ge(s["mask_done"], n + 1 + RING)
                    dve.wait_ge(s["step_done"], n + 1)
                    V.tensor_copy(e_hi[:, r, :], em[:, b, :]).then_inc(s["ehi_ready"], 1)
                    dve.wait_ge(s["ehi_ready"], n + 1)
                    V.tensor_tensor(e_lo[:, r, :], em[:, b, :], e_hi[:, r, :].bitcast(F32), ALU.subtract)\
                        .then_inc(s["elo_ready"], 1)
                end = seq.loop(ib, 13)
                for it in range(G):
                    if it < G - 1:
                        dve.wait_ge(s["acc_a"], ib * (G - 1) + it + 1)
                    else:
                        dve.wait_ge(s["step_done"], ib * T + T + RING)
                    V.tensor_copy(stage[:, it, 1, :], PS[:, 4 + it, 0:VW]).then_inc(s["st_a"], 1)
                dve.wait_ge(s["st_a"], ib * G + 2 * G)
                dve.wait_ge(s["st_e"], ib * G + 2 * G)
                seq.link(V.tensor_scalar(small[:, 0, :], stage[:, :, 0, D], 1e-5, None, ALU.add))
                seq.link(V.reciprocal(small[:, 1, :], small[:, 0, :]))
                seq.link(V.tensor_tensor(small[:, 2, :], stage[:, :, 1, D], cols2[:, ds(ib * G, G), 2], ALU.add))
                V.tensor_tensor(small[:, 3, :], stage[:, :, 1, D + 1], cols2[:, ds(ib * G, G), 3], ALU.add)\
                    .then_inc(s["z_ready"], 1)
                dve.wait_ge(s["th_ready"], ib * 2 + 1)
                seq.link(V.tensor_scalar(small[:, 6:8, :], small[:, 4:6, :], 0.5, 0.5, ALU.mult, ALU.add))
                seq.link(V.tensor_tensor(small[:, 0, :], small[:, 6, :], small[:, 1, :], ALU.mult))
                for it in range(G):
                    i1 = V.tensor_tensor(stage[:, it, 1, 0:D], stage[:, it, 1, 0:D], bias_row[:, :], ALU.add)
                    i1.then_inc(dve_seq, 1)
                seq.n = seq.n + G
                dve.wait_ge(dve_seq, seq.n)
                for it in range(G):
                    i1 = V.tensor_scalar(stage[:, it, 1, 0:D], stage[:, it, 1, 0:D], small[:, 7, it:it + 1], None, ALU.mult)
                    i1.then_inc(dve_seq, 1)
                seq.n = seq.n + G
                dve.wait_ge(dve_seq, seq.n)
                for it in range(G):
                    i1 = V.scalar_tensor_tensor(out=zt[:, it, :], in0=stage[:, it, 0, 0:D], scalar=small[:, 0, it:it + 1],
                                                in1=stage[:, it, 1, 0:D], op0=ALU.mult, op1=ALU.add)
                i1.then_inc(s["z_ready"], 1)
                dve.wait_ge(s["th_ready"], ib * 2 + 2)
                xg = X[:, ds(ib * G, G), :]
                V.scalar_tensor_tensor(out=xg.rearrange("p t d -> p (t d)"), in0=th[:, :, :].rearrange("p t d -> p (t d)"), scalar=0.5,
                                       in1=xg.rearrange("p t d -> p (t d)"), op0=ALU.mult, op1=ALU.add).then_inc(s["fin"], 1)
                dve.wait_ge(s["fin"], ib + 2)
                V.tensor_scalar(xg.rearrange("p t d -> p (t d)"), xg.rearrange("p t d -> p (t d)"), 0.5, None, ALU.add).then_inc(x_done, G)
                end(NG)
            dve.wait_ge(x_done, T)

            def ffn(layer):
                s = FS[layer]
                st = 1 + 2 * layer
                norm_stats(st)
                dve.wait_ge(s["aux_in"], 16 * (4 if layer == 0 else 3))
                dve.wait_ge(s["tree_in"], 2)
                split(gw_raw[:, :, :], gw_hi[:, :, :], gw_lo[:, :, :])
                if layer == 0:
                    seq.link(V.tensor_scalar(rb_col[:, :], rb_col[:, :], 0.5, None, ALU.mult))
                V.tensor_copy(sel[:, 0, :], sel_f[:, 0, :]).then_inc(wts_ready, 1)
                alone(dve)
                with dve.Fori(0, NG) as g:
                    normalise(st, g, True)
                    end = seq.loop(g, 10 if layer == 0 else 27)
                    dve.wait_ge(s["lg_psum"], g + 1)
                    lgp = PS[:, 5, :].rearrange("p (u n) -> p u n", u=G)[:, :, 0:E]
                    if layer == 0:
                        seq.link(V.tensor_scalar(pq[:, 0, :, :], lgp, 0.5, 0.5, ALU.mult, ALU.add))
                        seq.link(V.tensor_scalar(pq[:, 1, :, :], lgp, -0.5, 0.5, ALU.mult, ALU.add))
                        p_, q_ = pq[:, 0], pq[:, 1]
                        seq.link(V.tensor_copy(tree[:, 0, :, 0:1], q_[:, :, 0:1]))
                        seq.link(V.tensor_copy(tree[:, 0, :, 1:2], p_[:, :, 0:1]))
                        seq.link(V.tensor_tensor(tree[:, 1, :, 0:4:2], tree[:, 0, :, 0:2], q_[:, :, 1:3], ALU.mult))
                        seq.link(V.tensor_tensor(tree[:, 1, :, 1:4:2], tree[:, 0, :, 0:2], p_[:, :, 1:3], ALU.mult))
                        seq.link(V.tensor_tensor(gate[:, :, 0:8:2], tree[:, 1, :, 0:4], q_[:, :, 3:7], ALU.mult))
                        seq.link(V.tensor_tensor(gate[:, :, 1:8:2], tree[:, 1, :, 0:4], p_[:, :, 3:7], ALU.mult))
                    else:
                        seq.link(V.tensor_copy(lg[:, :, :], lgp))
                        for u in range(G):
                            alone(dve)
                            seq.link(V.max(top[:, u, :], lg[:, u, :]))
                            alone(dve)
                            seq.link(V.max_index(topi[:, u, :], top[:, u, :], lg[:, u, :]))
                            seq.link(V.tensor_copy(topf[:, u, 0:2], topi[:, u, 0:2]))
                            V.tensor_scalar(topf[:, u, 7:8], top[:, u, 0:1], -1.0, None, ALU.mult).then_inc(s["e_ready"], 1)
                        for u in range(G):
                            seq.link(V.tensor_scalar(hot[:, u, :], iota8[:, :], topf[:, u, 0:1], None, ALU.is_equal))
                            seq.link(V.scalar_tensor_tensor(out=hot[:, u, :], in0=iota8[:, :], scalar=topf[:, u, 1:2],
                                                            in1=hot[:, u, :], op0=ALU.is_equal, op1=ALU.add))
                        dve.wait_ge(act_seq, (g + 1) * G + 5)
                        seq.link(V.tensor_tensor(hot[:, :, :], hot[:, :, :], lg[:, :, :], ALU.mult))
                        seq.link(V.tensor_reduce(topf[:, :, 4:5], hot[:, :, :], AX.X, ALU.add))
                        V.reciprocal(topf[:, :, 5:6], topf[:, :, 4:5]).then_inc(dve_seq, 1)
                        seq.n = seq.n + 1
                        dve.wait_ge(dve_seq, seq.n)
                        for u in range(G):
                            i1 = V.tensor_scalar(gate[:, u, :], hot[:, u, :], topf[:, u, 5:6], None, ALU.mult)
                        seq.link(i1)
                    seq.link(V.tensor_copy(gate_hi[:, :, :], gate[:, :, :]))
                    seq.link(V.tensor_copy(gate2[:, :, 0:E], gate_hi[:, :, :].bitcast(F32)))
                    V.tensor_tensor(gate2[:, :, E:2 * E], gate[:, :, :], gate_hi[:, :, :].bitcast(F32), ALU.subtract)\
                        .then_inc(s["gate2_ready"], 1)
                    end(NG)
                dve.memset(acc[:, :, :], 0.0).then_inc(dve_seq, 1)
                seq.n += 1
                dve.wait_ge(dve_seq, seq.n)

                def split_quarter(e_next, q, par, first=False):
                    c1 = ds(q * D, D)
                    c2 = ds(q * 2, 2)
                    n = e_next * (2 * NG) + q * 2
                    V.tensor_copy(w1_hi[:, par, :, c1], w1_raw[:, :, c1]).then_inc(s["whi"], 1)
                    V.tensor_copy(w2_hi[:, par, c2, :], w2_raw[:, c2, :]).then_inc(s["whi"], 1)
                    if not first:
                        V.tensor_copy(sel[:, par:par + 1, :], sel_f[:, ds(e_next, 1), :])
                    dve.wait_ge(s["whi"], n + 2)
                    V.tensor_tensor(w1_lo[:, par, :, c1], w1_raw[:, :, c1], w1_hi[:, par, :, c1].bitcast(F32), ALU.subtract)
                    V.tensor_tensor(w2_lo[:, par, c2, :], w2_raw[:, c2, :], w2_hi[:, par, c2, :].bitcast(F32), ALU.subtract)\
                        .then_inc(s["split_done"], 1)

                dve.wait_ge(s["raw1_in"], 16)
                dve.wait_ge(s["raw2_in"], 16)
                for q in range(NG):
                    split_quarter(0, q, 0, first=True)

                def pair(ep, last):
                    for par in range(2):
                        e = ep * 2 + par
                        more = not (last and par == 1)
                        if more:
                            dve.wait_ge(s["raw1_in"], (e + 2) * 16)
                            dve.wait_ge(s["raw2_in"], (e + 2) * 16)
                        alone(dve)
                        with dve.Fori(0, 2) as gp:
                            for pg in range(2):
                                g = gp * 2 + pg
                                n = e * NG + g
                                for c in range(HC):
                                    m = n * HC + c
                                    dve.wait_ge(s["hid_act"], n * (HC + 1) + c + 2 + 3)
                                    dve.wait_ge(s["hid_used"], m + 1)
                                    V.tensor_copy(hid_hi[:, c % RING, :], hf[:, c % 2, :]).then_inc(s["hi_ready"], 1)
                                    dve.wait_ge(s["hi_ready"], m + 1)
                                    V.tensor_tensor(hid_lo[:, c % RING, :], hf[:, c % 2, :],
                                                    hid_hi[:, c % RING, :].bitcast(F32), ALU.subtract).then_inc(s["lo_ready"], 1)
                                    if c == RING and more:
                                        split_quarter(e + 1, g, 1 - par)
                                for d in range(KD):
                                    dve.wait_ge(s["y_done"], n + 1)
                                    if d == KD - 1:
                                        dve.wait_ge(s["hid_used"], (n + 1) * HC + RING)
                                    i1 = V.scalar_tensor_tensor(out=yt[:, d, :], in0=PS[:, 3 + 2 * pg + d, :],
                                                                scalar=b2_cols[:, ds(e, 1), d], in1=gate_b[:, pg, :],
                                                                op0=ALU.add, op1=ALU.mult)
                                    i1.then_inc(s["y_tmp"], 1)
                                dve.wait_ge(s["y_tmp"], n * 2 + 2)
                                dve.sem_inc(s["y_free"], 1)
                                i1 = V.tensor_tensor(acc[:, :, ds(g * GW, GW)], acc[:, :, ds(g * GW, GW)], yt[:, :, :], ALU.add)
                                i1.then_inc(s["acc_done"], 1)

                alone(dve)
                with dve.Fori(0, E // 2 - 1) as ep:
                    pair(ep, False)
                pair(E // 2 - 1, True)
                for t in range(T):
                    dve.wait_ge(s["back_psum"], t + 1)
                    V.tensor_tensor(X[:, t, :], X[:, t, :], PS[:, t % G, 0:D], ALU.add).then_inc(s["back_done"], 1)
                    dve.wait_ge(s["back_done"], t + 1)
                    dve.sem_inc(x_done, 1)

            ffn(0)
            dve.wait_ge(w_in, 160 + 80)
            for k in range(KD):
                product_column(w_raw[:, k, D:D + 1], h_raw[:, k, 0:D], vec_row[:, 0:D])
            dve.sem_inc(h_free, 1)
            dve.wait_ge(w_in, 160 + 96)
            for k in range(KD):
                product_column(w_raw[:, k, D + 1:D + 2], h_raw[:, k, 0:D], vec_row[:, 0:D])
            seq.link(V.memset(ff[:, :, 0:T], 0.0))
            seq.link(V.memset(ff[:, 0, 0:T], 1.0))
            seq.link(V.tensor_copy(hh[:, :, D], ff[:, 0, 0:T]))
            seq.link(V.tensor_copy(hh[:, :, D + 1], ff[:, 1, 0:T]))
            seq.link(V.tensor_copy(hl[:, :, D], ff[:, 1, 0:T]))
            seq.link(V.tensor_copy(hl[:, :, D + 1], ff[:, 1, 0:T]))
            seq.link(V.tensor_copy(w_hi[:, :, :], w_raw[:, :, :]))
            V.tensor_tensor(w_lo[:, :, :], w_raw[:, :, :], w_hi[:, :, :].bitcast(F32), ALU.subtract).then_inc(wts_ready, 1)
            norm_stats(2)
            with dve.Fori(0, NG) as g:
                normalise(2, g, False)
                for u in range(G):
                    t = ds(g * G + u, 1)
                    dve.wait_ge(proj_done, g * G + u + 1 + T)
                    if u >= 2:
                        dve.wait_ge(proj_hi, g * G + u + 2 * T - 1)
                    V.tensor_copy(cols[:, t, 0:2], bank(4 + u % 2, D, D + 2))
                    V.tensor_tensor(ff[:, u % 2, :], PS[:, 4 + u % 2, 0:D], bias_row[:, :], ALU.add).then_inc(proj_out, 1)
                    dve.wait_ge(proj_hi, g * G + u + 1 + 2 * T)
                    V.tensor_tensor(hl[:, t, 0:D], ff[:, u % 2:u % 2 + 1, :], hh[:, t, 0:D].bitcast(F32), ALU.subtract)\
                        .then_inc(dve_seq, 1)
            seq.n += T
            dve.wait_ge(dve_seq, seq.n)
            seq.link(V.tensor_scalar(cols2[:, :, 2], cols[:, :, 0], gate_bias[:, 0:1], None, ALU.add))
            seq.link(V.tensor_copy(cols2[:, :, 0], cols[:, :, 1]))
            V.tensor_scalar(cols2[:, :, 1], cols[:, :, 1], LEAK1, None, ALU.mult).then_inc(wts_ready, 1)
            diagonals(1, lambda t: cols[:, ds(t, 1), 1])
            dve.wait_ge(row_copied, 2 * NG)
            seq.link(V.tensor_reduce(s2_min[:, :], s2_row[:, :], AX.X, ALU.min))
            seq.link(V.tensor_scalar(s2_pos[:, :], s2_row[:, :], s2_min[:, :], 1.0, ALU.subtract, ALU.add))
            with dve.Fori(0, T // 2) as q:
                end = seq.loop(q, 2)
                for r in range(2):
                    dve.wait_ge(nat_in[r], q * 16 + 16)
                    V.scalar_tensor_tensor(out=masked[:, r, :], in0=adj_rows[:, r, :], scalar=0.0, in1=s2_pos[:, :],
                                           op0=ALU.is_gt, op1=ALU.mult).then_inc(nat_used, 1)
                    dve.wait_ge(nat_used, q * 2 + r + 3)
                    seq.link(V.tensor_reduce(mx[:, 0, ds(q * 2 + r, 1)], masked[:, r, :], AX.X, ALU.max))
                end(T // 2)
            seq.link(V.tensor_scalar(mx[:, 1, :], mx[:, 0, :], 0.0, None, ALU.is_le))
            seq.link(V.tensor_scalar(mx[:, 2, :], mx[:, 0, :], s2_min[:, :], -1.0, ALU.add, ALU.add))
            seq.link(V.tensor_tensor(mx[:, 2, :], mx[:, 2, :], cols2[:, :, 2], ALU.add))
            seq.link(V.scalar_tensor_tensor(out=mx[:, 3, :], in0=mx[:, 2, :], scalar=LEAK1, in1=mx[:, 2, :],
                                            op0=ALU.mult, op1=ALU.max))
            seq.link(V.tensor_tensor(mx[:, 4, :], cols2[:, :, 2], mx[:, 3, :], ALU.subtract))
            seq.link(V.scalar_tensor_tensor(out=mx[:, 5, :], in0=cols2[:, :, 2], scalar=LEAK1, in1=mx[:, 3, :],
                                            op0=ALU.mult, op1=ALU.subtract))
            diagonals(2, lambda t: mx[:, 4, ds(t, 1)])
            diagonals(3, lambda t: mx[:, 5, ds(t, 1)])
            dve.wait_ge(mean_psum, 1)
            seq.link(V.tensor_scalar(mean_row[:, :], PS[:, 6, 0:D], 1.0 / N, None, ALU.mult))
            s = GS[1]
            with dve.Fori(0, NG) as ib:
                for j in range(T):
                    n = ib * T + j
                    b, r = j % 2, j % RING
                    dve.wait_ge(s["exp_ready"], n * 2 + 2)
                    V.tensor_tensor(ee[:, b, :], e1[:, b, :], e2[:, b, :], ALU.max).then_inc(s["exp_used"], 1)
                    dve.wait_ge(s["exp_used"], n + 3)
                    dve.wait_ge(s["at_in"][r], (ib * (T // RING) + j // RING + 1) * 16)
                    if j >= 2:
                        dve.wait_ge(s["elo_ready"], n - 1)
                    V.scalar_tensor_tensor(out=em[:, b, :], in0=at[:, r, :], scalar=0.0, in1=ee[:, b, :],
                                           op0=ALU.is_gt, op1=ALU.min).then_inc(s["mask_done"], 1)
                    dve.wait_ge(s["mask_done"], n + 1 + RING)
                    dve.wait_ge(s["step_done"], n + 1)
                    V.tensor_copy(e_hi[:, r, :], em[:, b, :]).then_inc(s["ehi_ready"], 1)
                end = seq.loop(ib, 10)
                dve.wait_ge(s["st_e"], ib * G + 2 * G)
                iso = mx[:, 1, ds(ib * G, G)]
                seq.link(V.tensor_tensor(small[:, 0, :], stage[:, :, 0, D], iso, ALU.add))
                seq.link(V.reciprocal(small[:, 1, :], small[:, 0, :]))
                for it in range(G):
                    seq.link(V.scalar_tensor_tensor(out=X[:, ds(ib * G + it, 1), :], in0=stage[:, it:it + 1, 0, 0:D],
                                                    scalar=small[:, 1, it:it + 1], in1=X[:, ds(ib * G + it, 1), :],
                                                    op0=ALU.mult, op1=ALU.add))
                dve.sem_inc(s["fin"], 1)
                for it in range(G):
                    seq.link(V.scalar_tensor_tensor(out=X[:, ds(ib * G + it, 1), :], in0=mean_row[:, :].unsqueeze(1),
                                                    scalar=mx[:, 1, ds(ib * G + it, 1)], in1=X[:, ds(ib * G + it, 1), :],
                                                    op0=ALU.mult, op1=ALU.add))
                dve.sem_inc(x_done, G)
                end(NG)
            ffn(1)


def kernel(**inputs):
    import numpy as np
    import concourse.bacc as bacc
    from concourse.bass_utils import run_bass_kernel_spmd

    def laid(b):
        e, n = b.shape
        return np.ascontiguousarray(b.reshape(e, n // 128, 128).transpose(2, 0, 1))

    arrays = {k: np.ascontiguousarray(v) for k, v in inputs.items()}
    arrays["L1_gnn_a_b"] = arrays["L1_gnn_a_b"].reshape(1)
    arrays["adj_t"] = np.ascontiguousarray(arrays["adj"].T)
    arrays["L0_ffn_rw_t"] = np.ascontiguousarray(arrays.pop("L0_ffn_rw").T)
    for layer in (0, 1):
        for b in ("b1", "b2"):
            arrays[f"L{layer}_ffn_{b}_p"] = laid(arrays.pop(f"L{layer}_ffn_{b}"))
    nc = bacc.Bacc("TRN2", target_bir_lowering=False, num_devices=1)
    aps = {k: nc.dram_tensor(k + "_dram", v.shape, mybir.dt.from_np(v.dtype), kind="ExternalInput").ap()
           for k, v in arrays.items()}
    aps["out"] = nc.dram_tensor("out_dram", (2048, 256), mybir.dt.float32, kind="ExternalOutput").ap()
    gnn_ffn_program(nc, aps)
    r = run_bass_kernel_spmd(nc, [{k + "_dram": v for k, v in arrays.items()}], core_ids=[0])
    return r.results[0]["out_dram"]
```

```python
from contextlib import ExitStack

import concourse.bass as bass
from concourse import mybir
from concourse.alu_op_type import AluOpType as ALU

ACT = mybir.ActivationFunctionType
AX = mybir.AxisListType
F32 = mybir.dt.float32
F32R = mybir.dt.float32r
U32 = mybir.dt.uint32
ds = bass.ds

P = 128
N = 2048
D = 256
KD = D // P
T = N // P
G = 4
NG = T // G
GW = G * P
E = 8
HID = 1024
HC = HID // P
VW = D + 2
PW = D + 4
RING = 4
LN_EPS = 1e-5
BIG = 3.0e38
RT = 2 * P
NT = (2 * N + E * (RT - 1)) // RT
CUT = 2 * GW // E
LEAK0, LEAK1 = 0.01, 0.2


class Count:

    def __init__(self, eng, sem):
        self.eng, self.sem, self.n = eng, sem, 0

    def link(self, ins):
        ins.then_inc(self.sem, 1)
        self.n = self.n + 1
        self.eng.wait_ge(self.sem, self.n)

    def loop(self, i, per):
        start = self.n
        self.n = i * per + start

        def end(turns):
            self.n = start + per * turns
        return end


def gnn_ffn_program(nc, a):
    with ExitStack() as ctx:
        place = {"at": -(-nc.sbuf_base // 32) * 32}
        limit = nc.sbuf_usable_end

        def sb(name, shape, dt=F32):
            size = 4
            for s in shape[1:]:
                size *= s
            t = nc.alloc_sbuf_tensor_at(name, shape, dt, offset=place["at"])
            place["at"] += -(-size // 32) * 32
            assert place["at"] <= limit, (name, place["at"] - limit)
            return t

        def sem(name):
            return ctx.enter_context(nc.semaphore(name))

        PS = ctx.enter_context(nc.psum_tensor("PS", [P, 8, 512], F32))

        X = sb("X", [P, T, D])
        ident = sb("ident", [P, P])
        ones = sb("ones", [P, P])
        ones_r = sb("ones_r", [P, P], F32R)
        ln_stat = sb("ln_stat", [P, T, 6])
        ln_mv = sb("ln_mv", [P, T, 2])
        ln_var = sb("ln_var", [P, T])
        ln_rstd = sb("ln_rstd", [P, T])
        ln_t = sb("ln_t", [P, T])
        minus_half = sb("minus_half", [P, T])
        xn = sb("xn", [P, G, D])
        diag = sb("diag", [P, G, P])
        cols = sb("cols", [P, T, 4])
        cols2 = sb("cols2", [P, T, 4])
        shared_end = place["at"]

        xr_hi = sb("xr_hi", [P, G, KD, P], F32R)
        xr_lo = sb("xr_lo", [P, G, KD, P], F32R)
        w_raw = sb("w_raw", [P, KD, VW])
        w_hi = sb("w_hi", [P, KD, VW], F32R)
        w_lo = sb("w_lo", [P, KD, VW], F32R)
        h_raw = sb("h_raw", [P, KD, PW])
        h_hi = sb("h_hi", [P, KD, PW], F32R)
        h_lo = sb("h_lo", [P, KD, PW], F32R)
        vec_row = sb("vec_row", [P, 2 * D])
        bias_row = sb("bias_row", [P, D])
        gate_bias = sb("gate_bias", [P, 2])
        scratch = sb("scratch", [P, D])
        graph_w_end = place["at"]
        row_a = sb("row_a", [P, N])
        at = sb("at", [P, RING, GW])
        e1 = sb("e1", [P, 2, GW])
        e2 = sb("e2", [P, 2, GW])
        ee = sb("ee", [P, 2, GW])
        em = sb("em", [P, 2, GW])
        e_hi = sb("e_hi", [P, RING, GW], F32R)
        e_lo = sb("e_lo", [P, RING, GW], F32R)
        stage = sb("stage", [P, G, 2, VW])
        small = sb("small", [P, 8, G])
        zt = sb("zt", [P, G, D])
        th = sb("th", [P, G, D])
        hh = sb("hh", [P, T, VW], F32R)
        hl = sb("hl", [P, T, VW], F32R)
        graph_end = place["at"]
        a_hi = sb("a_hi", [P, RING, GW], F32R)
        a_lo = sb("a_lo", [P, RING, GW], F32R)
        vh = sb("vh", [P, T, VW], F32R)
        vl = sb("vl", [P, T, VW], F32R)

        place["at"] = graph_end
        row_b = sb("row_b", [P, N])
        s2_row = sb("s2_row", [P, N])
        s2_pos = sb("s2_pos", [P, N])
        adj_rows = sb("adj_rows", [P, 2, N])
        masked = sb("masked", [P, 2, N])
        mean_row = sb("mean_row", [P, D])
        s2_min = sb("s2_min", [P, 1])
        mx = sb("mx", [P, 8, T])
        ff = sb("ff", [P, 2, D])

        place["at"] = shared_end
        xt_hi = sb("xt_hi", [P, KD, N], F32R)
        xt_lo = sb("xt_lo", [P, KD, N], F32R)
        acc = sb("acc", [P, KD, N])
        g_row = sb("g_row", [P, N], F32R)
        w1_raw = sb("w1_raw", [P, KD, HID])
        w2_raw = sb("w2_raw", [P, HC, D])
        w1_hi = sb("w1_hi", [P, 2, KD, HID], F32R)
        w1_lo = sb("w1_lo", [P, 2, KD, HID], F32R)
        w2_hi = sb("w2_hi", [P, 2, HC, D], F32R)
        w2_lo = sb("w2_lo", [P, 2, HC, D], F32R)
        hf = sb("hf", [P, 2, GW])
        hid_hi = sb("hid_hi", [P, RING, GW], F32R)
        hid_lo = sb("hid_lo", [P, RING, GW], F32R)
        gate_b = sb("gate_b", [P, 2, GW])
        yt = sb("yt", [P, 2, GW])
        b1_cols = sb("b1_cols", [P, E, HC])
        b2_cols = sb("b2_cols", [P, E, KD])
        place_gate = place["at"]
        gw_raw = sb("gw_raw", [P, KD, P])
        gw_hi = sb("gw_hi", [P, KD, P], F32R)
        gw_lo = sb("gw_lo", [P, KD, P], F32R)
        lg_t = sb("lg_t", [P, GW])
        lg = sb("lg", [P, G, E])
        pq = sb("pq", [P, 2, G, E])
        tree = sb("tree", [P, 2, G, E])
        gate = sb("gate", [P, G, E])
        gate_hi = sb("gate_hi", [P, G, E], F32R)
        gate2 = sb("gate2", [P, G, P])
        rb_col = sb("rb_col", [P, 1])
        zeros = sb("zeros", [P, 4 * D])
        sel_f = sb("sel_f", [P, E, P])
        sel = sb("sel", [P, 2, P], F32R)

        place["at"] = shared_end
        place["at"] += 2 * KD * N * 4
        gw1_raw = sb("gw1_raw", [P, KD, P])
        gw1_hi = sb("gw1_hi", [P, KD, P], F32R)
        gw1_lo = sb("gw1_lo", [P, KD, P], F32R)
        lg1_t = sb("lg1_t", [P, GW])
        xn_all = sb("xn_all", [P, T, D])
        lga = sb("lga", [P, T, E])
        top = sb("top", [P, T, 8])
        topi = sb("topi", [P, T, 8], U32)
        topf = sb("topf", [P, T, 2])
        gate_e = sb("gate_e", [P, 4, T])
        iota8 = sb("iota8", [P, 1, E])
        before = sb("before", [P, P])
        hot = sb("hot", [P, 3, T, E])
        slot = sb("slot", [P, T, E])
        slot_t = sb("slot_t", [P, T, E])
        count_t = sb("count_t", [P, T + 1, E])
        tiles_e = sb("tiles_e", [P, 1, E])
        tile_end = sb("tile_end", [P, 1, E + 1])
        row_of = sb("row_of", [P, 2, T])
        row_u = sb("row_u", [P, 2, T], U32)
        iota_t = sb("iota_t", [P, NT + 1])
        tile_e = sb("tile_e", [P, NT + 1])
        tile_u = sb("tile_u", [P, NT + 1], U32)
        raw_at = place["at"]
        w1r_raw = sb("w1r_raw", [P, 2, KD, HID])
        w2r_raw = sb("w2r_raw", [P, 2, HC, D])
        w1r_hi = sb("w1r_hi", [P, 2, KD, HID], F32R)
        w1r_lo = sb("w1r_lo", [P, 2, KD, HID], F32R)
        w2r_hi = sb("w2r_hi", [P, 2, HC, D], F32R)
        w2r_lo = sb("w2r_lo", [P, 2, HC, D], F32R)
        routed_end = place["at"]
        place["at"] = shared_end
        y1 = sb("y1", [P, T, D])
        xg = sb("xg", [P, 2, 2, D])
        xg_hi = sb("xg_hi", [P, 2, KD, RT], F32R)
        xg_lo = sb("xg_lo", [P, 2, KD, RT], F32R)
        assert place["at"] <= shared_end + 2 * KD * N * 4
        place["at"] = routed_end
        b1_t = sb("b1_t", [P, 2, HC])
        b2_t = sb("b2_t", [P, 2, D])
        hfr = sb("hfr", [P, 2, RT])
        hr_hi = sb("hr_hi", [P, RING, RT], F32R)
        hr_lo = sb("hr_lo", [P, RING, RT], F32R)
        y_sb = sb("y_sb", [P, 2, 2, D])
        place["at"] = raw_at
        y2 = sb("y2", [P, T, D])

        xg_rows = nc.dram_tensor("xg_rows", [(NT + 1) * RT, D], F32).ap()
        yg_rows = nc.dram_tensor("yg_rows", [NT * RT, D], F32).ap()

        x_in = [sem(f"x_in{g}") for g in range(NG)]
        w_in = sem("w_in")
        const_ready = sem("const_ready")
        pool_seq = sem("pool_seq")
        dve_seq = sem("dve_seq")
        act_seq = sem("act_seq")
        wts_hi = sem("wts_hi")
        wts_ready = sem("wts_ready")
        var_ready = sem("var_ready")
        rstd_ready = sem("rstd_ready")
        xn_ready = sem("xn_ready")
        xt_psum = sem("xt_psum")
        xt_hi_ready = sem("xt_hi_ready")
        xt_lo_ready = sem("xt_lo_ready")
        proj_done = sem("proj_done")
        proj_hi = sem("proj_hi")
        proj_out = sem("proj_out")
        diag_ready = sem("diag_ready")
        row_psum = sem("row_psum")
        row_copied = sem("row_copied")
        h_free = sem("h_free")
        nat_in = [sem(f"nat_in{i}") for i in range(2)]
        nat_used = sem("nat_used")
        max_cols = sem("max_cols")
        mean_psum = sem("mean_psum")
        x_done = sem("x_done")
        out_done = sem("out_done")

        waited = {e.engine: sem(f"waited_{k}") for k, e in
                  (("act", nc.scalar), ("pe", nc.tensor), ("dve", nc.vector))}

        def graph_sems(n):
            s = {k: sem(f"{k}_{n}") for k in (
                "exp_ready", "exp_used", "mask_done", "ehi_ready", "elo_ready", "ahi_ready", "alo_ready",
                "step_done", "acc_e", "acc_a", "st_e", "st_a", "fin", "z_ready", "th_ready")}
            s["at_in"] = [sem(f"at_in{i}_{n}") for i in range(RING)]
            return s

        def ffn_sems(n):
            return {k: sem(f"{k}_{n}") for k in (
                "lgt_psum", "lgt_ready", "lg_psum", "gate2_ready", "g2_psum", "g_row_ready",
                "raw1_in", "raw2_in", "split_done", "whi", "hid_psum", "hid_act", "hi_ready", "lo_ready",
                "hid_used", "y_done", "y_free", "y_tmp", "acc_done", "back_psum", "back_done",
                "aux_in", "tree_in")}

        GS = [graph_sems(0), graph_sems(1)]
        FS = [ffn_sems(0)]
        rows_zeroed = sem("rows_zeroed")
        zeros_ready = sem("zeros_ready")
        R = {k: sem(f"r_{k}") for k in (
            "gw_room", "gw_in", "consts", "lgt_psum", "lgt_ready", "lg_psum", "gap_ready", "gap_exp", "hot_ready",
            "count_psum", "routed", "scattered", "w1_split", "w2_split", "w_hi", "xg_psum", "xg_hi", "xg_lo",
            "hid_psum", "hid_act", "hi_ready", "lo_ready", "hid_used", "y_done", "y_out")}
        for k in ("raw1", "raw2", "b1", "b2", "xg", "y_kept"):
            R[k] = [sem(f"r_{k}{i}") for i in range(2)]
        gathered = [sem(f"gathered{g}") for g in range(NG)]

        def alone(eng):
            eng.sem_inc(waited[eng.engine], 1)

        def bank(i, lo, hi):
            return PS[:, i:i + 1, lo:hi]

        x_v = a["x"].rearrange("(g t p) d -> g p t d", p=P, t=G)
        out_v = a["out"].rearrange("(g t p) d -> g p t d", p=P, t=G)
        adj_v = a["adj"].rearrange("(t p) n -> p t n", p=P)
        adj_t = a["adj_t"].rearrange("(j p) (b w) -> j p b w", p=P, w=GW)
        block = ctx.enter_context(nc.Block())

        @block.sync
        def _(sp):
            def weights(src, dst, slow=False):
                sp.dma_start(dst, src, allow_slow_non_contiguous=slow).then_inc(w_in, 16)

            def chunked(w):
                return w.rearrange("(k p) n -> p k n", p=P)

            def column(v):
                return v.rearrange("(k p o) -> p k o", p=P, o=1)

            def adj_stream(s):
                with sp.Fori(0, NG) as ib:
                    for j in range(T):
                        n = ib * T + j
                        sp.wait_ge(s["mask_done"], n + 1)
                        if s is GS[0]:
                            sp.wait_ge(s["alo_ready"], n + 1)
                        sp.dma_start(at[:, j % RING:j % RING + 1, :], adj_t[j][:, ds(ib, 1), :]).then_inc(s["at_in"][j % RING], 16)

            def expert_weights(s, w1, w2, e, turn):
                sp.wait_ge(s["split_done"], turn)
                sp.dma_start(w1_raw[:, :, :], w1[e].rearrange("(k p) n -> p k n", p=P)).then_inc(s["raw1_in"], 16)
                sp.dma_start(w2_raw[:, :, :], w2[e].rearrange("(c p) n -> p c n", p=P)).then_inc(s["raw2_in"], 16)

            def ffn_loads(layer):
                s = FS[layer]
                name = f"L{layer}_ffn_"
                sp.wait_ge(x_done, 2 * layer * T + T)
                sp.dma_start(b1_cols[:, :, :], a[name + "b1_p"]).then_inc(s["aux_in"], 16)
                sp.dma_start(b2_cols[:, :, :], a[name + "b2_p"]).then_inc(s["aux_in"], 16)
                sp.wait_ge(s["tree_in"], 1)
                if layer == 0:
                    sp.dma_start(rb_col[0:E - 1, :], a["L0_ffn_rb"].rearrange("(e o) -> e o", o=1), allow_slow_non_contiguous=True).then_inc(s["aux_in"], 16)
                sp.dma_start(gw_raw[:, :, 0:E - 1], chunked(a["L0_ffn_rw_t"])).then_inc(s["aux_in"], 16)
                w1, w2 = a[name + "w1"], a[name + "w2"]
                sp.dma_start(w1_raw[:, :, :], w1[0].rearrange("(k p) n -> p k n", p=P)).then_inc(s["raw1_in"], 16)
                sp.dma_start(w2_raw[:, :, :], w2[0].rearrange("(c p) n -> p c n", p=P)).then_inc(s["raw2_in"], 16)
                for e in range(1, E):
                    expert_weights(s, w1, w2, e, e * NG)

            weights(chunked(a["L0_gnn_W_gcnb"]), w_raw[:, :, 0:D])
            weights(column(a["L0_gnn_Wa"][0, 0:D]), w_raw[:, :, D:D + 1], slow=True)
            weights(column(a["L0_gnn_Wb"][0, 0:D]), w_raw[:, :, D + 1:D + 2], slow=True)
            weights(chunked(a["L0_gnn_W_sa"]), h_raw[:, :, 0:D])
            weights(column(a["L0_gnn_Wa"][0, D:2 * D]), h_raw[:, :, D + 2:D + 3], slow=True)
            weights(column(a["L0_gnn_Wb"][0, D:2 * D]), h_raw[:, :, D + 3:D + 4], slow=True)
            weights(a["L0_gnn_a_sa"][0, :].partition_broadcast(P), vec_row[:, :])
            weights(a["L0_gnn_b_gcnb"].partition_broadcast(P), bias_row[:, :])
            weights(a["L0_gnn_ba"].partition_broadcast(P), gate_bias[:, 0:1])
            weights(a["L0_gnn_bb"].partition_broadcast(P), gate_bias[:, 1:2])
            for g in range(NG):
                sp.dma_start(X[:, g * G:(g + 1) * G, :], x_v[g]).then_inc(x_in[g], 16)
            adj_stream(GS[0])
            ffn_loads(0)
            sp.wait_ge(zeros_ready, 1)
            zero_v = xg_rows.rearrange("(b p r) d -> b p (r d)", p=P, r=4)
            for b in range((NT + 1) * RT // (4 * P)):
                sp.dma_start(zero_v[b], zeros[:, :]).then_inc(rows_zeroed, 16)

            sp.wait_ge(x_done, 2 * T)
            weights(chunked(a["L1_gnn_fc_w"]), w_raw[:, :, 0:D])
            weights(chunked(a["L1_gnn_W"][0:D, :]), h_raw[:, :, 0:D])
            weights(a["L1_gnn_a_w"].partition_broadcast(P), vec_row[:, 0:D])
            weights(a["L1_gnn_fc_b"].partition_broadcast(P), bias_row[:, :])
            weights(a["L1_gnn_a_b"].partition_broadcast(P), gate_bias[:, 0:1])
            sp.wait_ge(h_free, 1)
            weights(chunked(a["L1_gnn_W"][D:2 * D, :]), h_raw[:, :, 0:D])
            with sp.Fori(0, T // 2) as q:
                for r in range(2):
                    sp.wait_ge(nat_used, q * 2 + r + 1)
                    sp.dma_start(adj_rows[:, r:r + 1, :], adj_v[:, ds(q * 2 + r, 1), :]).then_inc(nat_in[r], 16)
            adj_stream(GS[1])
            sp.wait_ge(x_done, 3 * T)
            sp.wait_ge(R["gw_room"], 1)
            sp.dma_start(gw1_raw[:, :, 0:E], chunked(a["L1_ffn_gate_w"])).then_inc(R["gw_in"], 16)
            sp.wait_ge(R["routed"], 1)
            w1, w2 = a["L1_ffn_w1"], a["L1_ffn_w2"]
            xg_v = xg_rows.rearrange("(i r p) d -> p i r d", p=P, r=2)
            yg_v = yg_rows.rearrange("(i r p) d -> p i r d", p=P, r=2)

            def tile_loads(i, z):
                e = sp.value_load(tile_u[0:1, ds(i, 1)], min_val=0, max_val=E - 1)
                sp.wait_ge(R["w1_split"], i * G + G)
                sp.dma_start(w1r_raw[:, z:z + 1, :, :],
                             w1.rearrange("e (k p) n -> p e k n", p=P)[:, ds(e, 1)]).then_inc(R["raw1"][z], 16)
                sp.wait_ge(R["y_out"], i + 1)
                sp.dma_start(b1_t[:, z:z + 1, :], a["L1_ffn_b1_p"][:, ds(e, 1), :]).then_inc(R["b1"][z], 16)
                sp.dma_start(b2_t[:, z, :], a["L1_ffn_b2"][ds(e, 1), :].rearrange("e d -> (e d)").partition_broadcast(P))\
                  .then_inc(R["b2"][z], 16)
                sp.wait_ge(R["w2_split"], i * G + G)
                sp.dma_start(w2r_raw[:, z:z + 1, :, :],
                             w2.rearrange("e (c p) n -> p e c n", p=P)[:, ds(e, 1)]).then_inc(R["raw2"][z], 16)
                sp.wait_ge(R["scattered"], 2 * T * 16)
                sp.dma_start(xg[:, z:z + 1, :, :], xg_v[:, ds(i, 1)]).then_inc(R["xg"][z], 16)

            def tile_store(i, z):
                sp.wait_ge(R["y_out"], i + 3)
                sp.dma_start(yg_v[:, ds(i, 1)], y_sb[:, z:z + 1, :, :]).then_inc(R["y_kept"][z], 16)

            tile_loads(0, 0)
            tile_loads(1, 1)
            with sp.Fori(0, (NT - 3) // 2) as q:
                for z in range(2):
                    tile_loads(q * 2 + z + 2, z)
                    tile_store(q * 2 + z, z)
            tile_loads(NT - 1, (NT - 1) % 2)
            for i in range(NT - 3, NT):
                tile_store(i, i % 2)

            for g in range(NG):
                sp.wait_ge(x_done, 3 * T + (g + 1) * G)
                sp.dma_start(out_v[g], X[:, g * G:(g + 1) * G, :]).then_inc(out_done, 16)
            sp.wait_ge(out_done, 16 * NG)

        @block.gpsimd
        def _(pool):
            seq = Count(pool, pool_seq)
            seq.link(pool.memset(ident[:, :], 0.0))
            pool.affine_select(out=ident[:, :], in_=ident[:, :], compare_op=ALU.not_equal, fill=1.0, base=0,
                               pattern=[[-1, P]], channel_multiplier=1).then_inc(const_ready, 1)
            pool.memset(ones[:, :], 1.0).then_inc(const_ready, 1)
            pool.memset(minus_half[:, :], -0.5).then_inc(const_ready, 1)
            pool.memset(zt[:, 0, 0:T], 1.0).then_inc(const_ready, 1)
            pool.memset(zt[:, 1, 0:T], 0.0).then_inc(const_ready, 1)

            def rstd(stage_no):
                pool.wait_ge(var_ready, stage_no + 1)
                pool.tensor_tensor(ln_rstd[:, :], ln_var[:, :], minus_half[:, :], ALU.pow).then_inc(rstd_ready, 1)

            def ffn_consts(layer):
                s = FS[layer]
                pool.wait_ge(x_done, 2 * layer * T + T)
                pool.memset(gate2[:, :, :], 0.0).then_inc(pool_seq, 1)
                pool.memset(sel_f[:, :, :], 0.0).then_inc(pool_seq, 1)
                pool.memset(rb_col[:, :], 0.0).then_inc(pool_seq, 1)
                seq.n += 3
                seq.link(pool.memset(gw_raw[:, :, :], 0.0))
                pool.sem_inc(s["tree_in"], 1)
                pool.memset(zeros[:, :], 0.0).then_inc(zeros_ready, 1)
                seq.link(pool.affine_select(out=sel_f[:, :, :], in_=sel_f[:, :, :], compare_op=ALU.not_equal,
                                            fill=1.0, base=0, pattern=[[-1, E], [0, P]], channel_multiplier=1))
                pool.affine_select(out=sel_f[:, :, :], in_=sel_f[:, :, :], compare_op=ALU.not_equal,
                                   fill=1.0, base=-E, pattern=[[-1, E], [0, P]], channel_multiplier=1)\
                    .then_inc(s["tree_in"], 1)

            rstd(0)
            s = GS[0]
            with pool.Fori(0, NG) as ib:
                for j in range(T):
                    n = ib * T + j
                    pool.wait_ge(s["ahi_ready"], n + 1)
                    pool.wait_ge(s["step_done"], n + 1)
                    pool.tensor_tensor(a_lo[:, j % RING, :], at[:, j % RING, :], a_hi[:, j % RING, :].bitcast(F32),
                                       ALU.subtract).then_inc(s["alo_ready"], 1)
            ffn_consts(0)
            rstd(1)
            rstd(2)
            s = GS[1]
            with pool.Fori(0, NG) as ib:
                for j in range(T):
                    n = ib * T + j
                    pool.wait_ge(s["ehi_ready"], n + 1)
                    pool.wait_ge(s["step_done"], n + 1)
                    pool.tensor_tensor(e_lo[:, j % RING, :], em[:, j % 2, :], e_hi[:, j % RING, :].bitcast(F32),
                                       ALU.subtract).then_inc(s["elo_ready"], 1)
            pool.wait_ge(x_done, 3 * T)
            pool.memset(gw1_raw[:, :, :], 0.0).then_inc(R["gw_room"], 1)
            pool.iota(iota8[:, :, :], pattern=[[1, E]], base=0, channel_multiplier=0,
                      allow_small_or_imprecise_dtypes=True).then_inc(R["consts"], 1)
            pool.iota(iota_t[:, :], pattern=[[1, NT + 1]], base=0, channel_multiplier=0,
                      allow_small_or_imprecise_dtypes=True).then_inc(R["consts"], 1)
            pool.affine_select(out=before[:, :], in_=ones[:, :], compare_op=ALU.is_gt, fill=0.0, base=0,
                               pattern=[[1, P]], channel_multiplier=-1).then_inc(R["consts"], 1)
            rstd(3)
            pool.wait_ge(R["routed"], 1)
            pool.wait_ge(rows_zeroed, 16 * ((NT + 1) * RT // (4 * P)))
            for t in range(T):
                for k in range(2):
                    pool.indirect_dma_start(xg_rows, bass.IndirectOffsetOnAxis(ap=row_u[:, k, t:t + 1], axis=0),
                                            xn_all[:, t, :], None).then_inc(R["scattered"], 16)

            def low_pieces(i, z, q):
                n = i * 2 * G + G + q + 1
                pool.wait_ge(R["w_hi"], n)
                pool.tensor_tensor(w2r_lo[:, z, 2 * q:2 * q + 2, :], w2r_raw[:, z, 2 * q:2 * q + 2, :],
                                   w2r_hi[:, z, 2 * q:2 * q + 2, :].bitcast(F32), ALU.subtract).then_inc(R["w2_split"], 1)

            for q in range(G):
                low_pieces(0, 0, q)
            with pool.Fori(0, (NT - 1) // 2) as ii:
                for z in range(2):
                    for q in range(G):
                        low_pieces(ii * 2 + z + 1, 1 - z, q)
            for z in range(2):
                pool.wait_ge(R["y_kept"][z], 16 * ((NT + 1 - z) // 2 + 1))
            for t in range(T):
                for k, y in enumerate((y1, y2)):
                    pool.indirect_dma_start(y[:, t, :], None, yg_rows,
                                            bass.IndirectOffsetOnAxis(ap=row_u[:, k, t:t + 1], axis=0))\
                        .then_inc(gathered[t // G], 16)

        @block.scalar
        def _(act):
            def high_parts_of_x(stage_no, g, wide):
                for u in range(G):
                    act.wait_ge(xt_psum, g * G + u + 1 + stage_no * T)
                    src = PS[:, u, 0:D].rearrange("p (k n) -> p k n", k=KD)
                    dst = xt_hi[:, :, ds((g * G + u) * P, P)] if wide else xr_hi[:, u, :, :]
                    alone(act)
                    act.activation(dst, src, ACT.Copy).then_inc(xt_hi_ready, 1)

            def rows_out(k, dst):
                with act.Fori(0, NG) as q:
                    act.wait_ge(row_psum, (k * NG + 2) + q)
                    alone(act)
                    act.activation(dst[:, ds(q * GW, GW)], PS[:, 0, :], ACT.Copy).then_inc(row_copied, 1)

            def ffn(layer):
                s = FS[layer]
                with act.Fori(0, NG) as g:
                    high_parts_of_x(1 + 2 * layer, g, True)
                    act.wait_ge(s["lgt_psum"], g + 1)
                    act.activation(lg_t[:, :], PS[:, 4, :], ACT.Tanh, bias=rb_col[:, :], scale=0.5).then_inc(s["lgt_ready"], 1)
                    act.wait_ge(s["g2_psum"], g + 1)
                    alone(act)
                    act.activation(g_row[:, ds(g * GW, GW)], PS[:, 6, :], ACT.Copy).then_inc(s["g_row_ready"], 1)

                act.wait_ge(s["aux_in"], 16 * (4 if layer == 0 else 3))
                with act.Fori(0, E) as e:
                    with act.Fori(0, 2) as gp:
                        for pg in range(2):
                            n = e * NG + gp * 2 + pg
                            for c in range(HC + 1):
                                act.wait_ge(s["hid_psum"], n * (HC + 1) + c + 1)
                                if c == 0:
                                    act.wait_ge(s["acc_done"], n + 1)
                                    act.activation(gate_b[:, pg, :], PS[:, 0, :], ACT.Copy).then_inc(s["hid_act"], 1)
                                else:
                                    act.wait_ge(s["lo_ready"], n * HC + c)
                                    alone(act)
                                    act.activation(hf[:, (c - 1) % 2, :], PS[:, c % 3, :], ACT.Gelu,
                                                   bias=b1_cols[:, ds(e, 1), c - 1], scale=1.0).then_inc(s["hid_act"], 1)

            act.wait_ge(const_ready, 5)
            act.activation(hh[:, :, D:D + 1].rearrange("p t o -> p (t o)"), zt[:, 0, 0:T], ACT.Copy).then_inc(act_seq, 1)
            act.activation(hh[:, :, D + 1:D + 2].rearrange("p t o -> p (t o)"), zt[:, 1, 0:T], ACT.Copy).then_inc(act_seq, 1)
            act.activation(hl[:, :, D:D + 1].rearrange("p t o -> p (t o)"), zt[:, 1, 0:T], ACT.Copy).then_inc(act_seq, 1)
            act.activation(hl[:, :, D + 1:D + 2].rearrange("p t o -> p (t o)"), zt[:, 1, 0:T], ACT.Copy).then_inc(act_seq, 1)
            act.activation(ones_r[:, :], ones[:, :], ACT.Copy).then_inc(act_seq, 1)
            with act.Fori(0, NG) as g:
                high_parts_of_x(0, g, False)
                for u in range(G):
                    act.wait_ge(proj_done, g * G + u + 1)
                    alone(act)
                    act.activation(vh[:, ds(g * G + u, 1), :], bank(4 + u % 2, 0, VW), ACT.Copy).then_inc(proj_hi, 1)
                    act.activation(hh[:, ds(g * G + u, 1), 0:D], bank(6 + u % 2, 0, D), ACT.Copy).then_inc(proj_hi, 1)
            rows_out(0, row_a)

            def graph_steps(s, layer):
                ra, rb = (row_a, row_a) if layer == 0 else (row_a, row_b)
                k1, k2 = (-1.0, -LEAK0) if layer == 0 else (1.0, 1.0)
                with act.Fori(0, NG) as ib:
                    for j in range(T):
                        n = ib * T + j
                        act.wait_ge(s["exp_used"], n + 1)
                        alone(act)
                        act.activation(e1[:, j % 2, :], ra[:, ds(ib * GW, GW)], ACT.Exp, bias=cols2[:, j, 0:1],
                                       scale=k1).then_inc(s["exp_ready"], 1)
                        act.activation(e2[:, j % 2, :], rb[:, ds(ib * GW, GW)], ACT.Exp, bias=cols2[:, j, 1:2],
                                       scale=k2).then_inc(s["exp_ready"], 1)
                        if layer == 0:
                            act.wait_ge(s["at_in"][j % RING], (ib * (T // RING) + j // RING + 1) * 16)
                            act.wait_ge(s["step_done"], n + 1)
                            act.activation(a_hi[:, j % RING, :], at[:, j % RING, :], ACT.Copy).then_inc(s["ahi_ready"], 1)
                    for it in range(G):
                        if layer == 0:
                            act.wait_ge(s["acc_e"], ib * G + it + 1)
                        elif it < G - 1:
                            act.wait_ge(s["acc_e"], ib * (G - 1) + it + 1)
                        else:
                            act.wait_ge(s["step_done"], ib * T + T + RING)
                        act.wait_ge(s["fin"], ib + 1)
                        act.activation(stage[:, it, 0, :], PS[:, it, 0:VW], ACT.Copy).then_inc(s["st_e"], 1)
                    if layer == 0:
                        for k in range(2):
                            act.wait_ge(s["z_ready"], ib * 2 + k + 1)
                            if k == 0:
                                act.activation(small[:, 4:6, :], small[:, 2:4, :], ACT.Tanh, scale=0.5).then_inc(s["th_ready"], 1)
                            else:
                                act.activation(th[:, :, :], zt[:, :, :], ACT.Tanh, scale=0.5).then_inc(s["th_ready"], 1)

            act.wait_ge(wts_ready, 2)
            graph_steps(GS[0], 0)
            ffn(0)
            act.wait_ge(const_ready, 5)
            with act.Fori(0, NG) as g:
                high_parts_of_x(2, g, False)
                for u in range(G):
                    act.wait_ge(proj_out, g * G + u + 1 + T)
                    alone(act)
                    act.activation(hh[:, ds(g * G + u, 1), 0:D], ff[:, u % 2:u % 2 + 1, :], ACT.Copy).then_inc(proj_hi, 1)
            rows_out(1, s2_row)
            rows_out(2, row_a)
            rows_out(3, row_b)
            graph_steps(GS[1], 1)
            with act.Fori(0, NG) as g:
                high_parts_of_x(3, g, True)
                act.wait_ge(R["lgt_psum"], g + 1)
                act.activation(lg1_t[:, :], PS[:, 4, :], ACT.Copy).then_inc(R["lgt_ready"], 1)
            act.wait_ge(R["gap_ready"], 1)
            act.activation(gate_e[:, 1, :], gate_e[:, 0, :], ACT.Exp).then_inc(R["gap_exp"], 1)

            def piece(i, z, c, uses):
                if c % G == 0:
                    act.wait_ge(R["raw1" if c == 0 else "raw2"][z], uses * 16)
                if c < G:
                    src, dst = w1r_raw[:, z, :, c * D:(c + 1) * D], w1r_hi[:, z, :, c * D:(c + 1) * D]
                else:
                    b = 2 * (c - G)
                    src, dst = w2r_raw[:, z, b:b + 2, :], w2r_hi[:, z, b:b + 2, :]
                act.activation(dst, src, ACT.Copy).then_inc(R["w_hi"], 1)

            def rows_high(i, z):
                act.wait_ge(R["xg_psum"], i + 1)
                act.activation(xg_hi[:, z, :, :], PS[:, 2, :].rearrange("p (k n) -> p k n", k=KD), ACT.Copy)\
                    .then_inc(R["xg_hi"], 1)

            def tile(i, z, uses, more):
                act.wait_ge(R["b1"][z], uses * 16)
                for c in range(HC):
                    act.wait_ge(R["hid_psum"], i * HC + c + 1)
                    act.wait_ge(R["lo_ready"], i * HC + c + 1)
                    act.activation(hfr[:, c % 2, :], PS[:, c % 2, 0:RT], ACT.Gelu, bias=b1_t[:, z, c:c + 1], scale=1.0)\
                        .then_inc(R["hid_act"], 1)
                    if more:
                        if c == 0:
                            act.wait_ge(R["y_done"], i * 2 + 1)
                        piece(i + 1, 1 - z, c, uses + z)
                        if c == G:
                            rows_high(i + 1, 1 - z)

            for c in range(HC):
                piece(0, 0, c, 1)
            rows_high(0, 0)
            with act.Fori(0, (NT - 1) // 2) as ii:
                for z in range(2):
                    tile(ii * 2 + z, z, ii + 1, True)
            tile(NT - 1, 0, (NT + 1) // 2, False)

        @block.tensor
        def _(pe):
            def three(out, l_hi, l_lo, r_hi, r_lo, start, stop, sem_of=None):
                pe.matmul(out, l_hi, r_hi, start=start, stop=False)
                pe.matmul(out, l_hi, r_lo, start=False, stop=False)
                m = pe.matmul(out, l_lo, r_hi, start=False, stop=stop)
                if sem_of is not None:
                    m.then_inc(sem_of, 1)

            def transposes_of_x(stage_no, g):
                for u in range(G):
                    pe.wait_ge(xn_ready, g * G + u + 1 + stage_no * T)
                    pe.transpose(PS[:, u, 0:P], xn[:, u, 0:P], ident[:, :])
                    pe.transpose(PS[:, u, P:D], xn[:, u, P:D], ident[:, :]).then_inc(xt_psum, 1)

            def rows(k):
                alone(pe)
                with pe.Fori(0, NG) as q:
                    for r in range(G):
                        pe.wait_ge(diag_ready, q * G + (k * T + r + 1))
                        m = pe.matmul(PS[:, 0, r * P:(r + 1) * P], ones[:, :], diag[:, r, :], start=True, stop=True)
                    m.then_inc(row_psum, 1)
                    pe.wait_ge(row_copied, q + (k * NG + 1))

            def graph_steps(s, layer):
                alone(pe)
                with pe.Fori(0, NG) as ib:
                    for j in range(T):
                        n = ib * T + j
                        pe.wait_ge(s["elo_ready"], n + 1)
                        for it in range(G):
                            if j == 0:
                                pe.wait_ge(s["st_e"], ib * G + it + 1)
                            w = slice(it * P, (it + 1) * P)
                            done = s["acc_e"] if j == T - 1 else None
                            if layer == 1 and it == G - 1:
                                done = s["step_done"]
                            three(PS[:, it, 0:VW], e_hi[:, j % RING, w], e_lo[:, j % RING, w],
                                  hh[:, j, :], hl[:, j, :], j == 0, j == T - 1, done)
                        if layer == 1:
                            continue
                        pe.wait_ge(s["alo_ready"], n + 1 + RING)
                        for it in range(G):
                            if j == 0:
                                pe.wait_ge(s["st_a"], ib * G + it + 1)
                            w = slice(it * P, (it + 1) * P)
                            done = s["acc_a"] if j == T - 1 and it < G - 1 else s["step_done"] if it == G - 1 else None
                            three(PS[:, 4 + it, 0:VW], a_hi[:, j % RING, w], a_lo[:, j % RING, w],
                                  vh[:, j, :], vl[:, j, :], j == 0, j == T - 1, done)

            def ffn(layer):
                s = FS[layer]
                pe.wait_ge(wts_ready, 3 if layer == 0 else 6)
                alone(pe)
                with pe.Fori(0, NG) as g:
                    transposes_of_x(1 + 2 * layer, g)
                    pe.wait_ge(xt_lo_ready, (g + 1) * G + (1 + 2 * layer) * T)
                    for k in range(KD):
                        three(PS[:, 4, :], gw_hi[:, k, :], gw_lo[:, k, :], xt_hi[:, k, ds(g * GW, GW)],
                              xt_lo[:, k, ds(g * GW, GW)], k == 0, k == KD - 1,
                              s["lgt_psum"] if k == KD - 1 else None)
                    pe.wait_ge(s["lgt_ready"], g + 1)
                    for u in range(G):
                        m = pe.transpose(PS[:, 5, u * P:(u + 1) * P], lg_t[:, u * P:(u + 1) * P], ident[:, :])
                    m.then_inc(s["lg_psum"], 1)
                    pe.wait_ge(s["gate2_ready"], g + 1)
                    for u in range(G):
                        m = pe.transpose(PS[:, 6, u * P:(u + 1) * P], gate2[:, u, :], ident[:, :])
                    m.then_inc(s["g2_psum"], 1)
                pe.wait_ge(s["g_row_ready"], NG)

                def second(n, pg, c, par):
                    pe.wait_ge(s["lo_ready"], n * HC + c + 3)
                    if c == 0:
                        pe.wait_ge(s["y_free"], n + 1)
                    for d in range(KD):
                        w = slice(d * P, (d + 1) * P)
                        last = c == HC - 1
                        three(PS[:, 3 + 2 * pg + d, :], w2_hi[:, par, c, w], w2_lo[:, par, c, w],
                              hid_hi[:, c % RING, :], hid_lo[:, c % RING, :], c == 0, last,
                              s["hid_used"] if d == KD - 1 else s["y_done"] if last else None)

                alone(pe)
                with pe.Fori(0, E // 2) as ep:
                    for par in range(2):
                        e = ep * 2 + par
                        pe.wait_ge(s["split_done"], (e + 1) * NG)
                        alone(pe)
                        with pe.Fori(0, 2) as gp:
                            for pg in range(2):
                                n = e * NG + gp * 2 + pg
                                gcol = (gp * 2 + pg) * GW
                                for c in range(HC + 1):
                                    pe.wait_ge(s["hid_act"], n * (HC + 1) + c + 1)
                                    if c == 0:
                                        pe.matmul(PS[:, 0, :], sel[:, par, :], g_row[:, ds(gcol, GW)],
                                                  start=True, stop=True).then_inc(s["hid_psum"], 1)
                                        continue
                                    w = slice((c - 1) * P, c * P)
                                    for k in range(KD):
                                        three(PS[:, c % 3, :], w1_hi[:, par, k, w], w1_lo[:, par, k, w],
                                              xt_hi[:, k, ds(gcol, GW)], xt_lo[:, k, ds(gcol, GW)], k == 0, k == KD - 1,
                                              s["hid_psum"] if k == KD - 1 else None)
                                    if c >= 3:
                                        second(n, pg, c - 3, par)
                                second(n, pg, HC - 2, par)
                                second(n, pg, HC - 1, par)
                for t in range(T):
                    pe.wait_ge(s["acc_done"], E * NG + 2)
                    if t >= G:
                        pe.wait_ge(s["back_done"], t - G + 1)
                    for d in range(KD):
                        m = pe.transpose(PS[:, t % G, d * P:(d + 1) * P], acc[:, d, t * P:(t + 1) * P], ident[:, :])
                    m.then_inc(s["back_psum"], 1)

            pe.wait_ge(const_ready, 5)
            pe.wait_ge(wts_ready, 1)
            with pe.Fori(0, NG) as g:
                transposes_of_x(0, g)
                for u in range(G):
                    pe.wait_ge(xt_lo_ready, g * G + u + 1)
                    if u >= 2:
                        pe.wait_ge(proj_out, g * G + u - 1)
                    for k in range(KD):
                        three(PS[:, 4 + u % 2, 0:VW], xr_hi[:, u, k, :], xr_lo[:, u, k, :], w_hi[:, k, :], w_lo[:, k, :],
                              k == 0, k == KD - 1)
                    for k in range(KD):
                        three(PS[:, 6 + u % 2, 0:PW], xr_hi[:, u, k, :], xr_lo[:, u, k, :], h_hi[:, k, :], h_lo[:, k, :],
                              k == 0, k == KD - 1, proj_done if k == KD - 1 else None)
            rows(0)
            graph_steps(GS[0], 0)
            ffn(0)
            pe.wait_ge(wts_ready, 4)
            with pe.Fori(0, NG) as g:
                transposes_of_x(2, g)
                for u in range(G):
                    pe.wait_ge(xt_lo_ready, g * G + u + 1 + 2 * T)
                    if u >= 2:
                        pe.wait_ge(proj_out, g * G + u - 1 + T)
                    for k in range(KD):
                        three(PS[:, 4 + u % 2, 0:VW], xr_hi[:, u, k, :], xr_lo[:, u, k, :], w_hi[:, k, :], w_lo[:, k, :],
                              k == 0, k == KD - 1, proj_done if k == KD - 1 else None)
            pe.wait_ge(wts_ready, 5)
            for j in range(T):
                pe.matmul(PS[:, 6, 0:D], ones_r[:, :], hh[:, j, 0:D], start=j == 0, stop=False)
                m = pe.matmul(PS[:, 6, 0:D], ones_r[:, :], hl[:, j, 0:D], start=False, stop=j == T - 1)
            m.then_inc(mean_psum, 1)
            for k in (1, 2, 3):
                rows(k)
            graph_steps(GS[1], 1)
            pe.wait_ge(wts_ready, 6)
            with pe.Fori(0, NG) as g:
                transposes_of_x(3, g)
                pe.wait_ge(xt_lo_ready, (g + 1) * G + 3 * T)
                for k in range(KD):
                    three(PS[:, 4, :], gw1_hi[:, k, :], gw1_lo[:, k, :], xt_hi[:, k, ds(g * GW, GW)],
                          xt_lo[:, k, ds(g * GW, GW)], k == 0, k == KD - 1, R["lgt_psum"] if k == KD - 1 else None)
                pe.wait_ge(R["lgt_ready"], g + 1)
                for u in range(G):
                    m = pe.transpose(PS[:, 5, u * P:(u + 1) * P], lg1_t[:, u * P:(u + 1) * P], ident[:, :])
                m.then_inc(R["lg_psum"], 1)
            pe.wait_ge(R["hot_ready"], 1)
            hot_rows = hot[:, 2, :, :].rearrange("p t e -> p (t e)")
            pe.matmul(PS[:, 6, 0:T * E], before[:, :], hot_rows, start=True, stop=True)
            pe.matmul(PS[:, 7, 0:T * E], ones[:, :], hot_rows, start=True, stop=True).then_inc(R["count_psum"], 1)

            def rows_in(i, z, uses):
                pe.wait_ge(R["xg"][z], uses * 16)
                for k in range(KD):
                    for r in range(2):
                        m = pe.transpose(PS[:, 2, (2 * k + r) * P:(2 * k + r + 1) * P], xg[:, z, r, k * P:(k + 1) * P],
                                         ident[:, :])
                m.then_inc(R["xg_psum"], 1)

            def second(i, z, c):
                pe.wait_ge(R["lo_ready"], i * HC + c + 3)
                if c == 0:
                    pe.wait_ge(R["y_out"], i + 1)
                for r in range(2):
                    w = slice(r * P, (r + 1) * P)
                    last = c == HC - 1
                    three(PS[:, 4 + 2 * z + r, 0:D], hr_hi[:, c % RING, w], hr_lo[:, c % RING, w],
                          w2r_hi[:, z, c, :], w2r_lo[:, z, c, :], c == 0, last,
                          R["y_done"] if last else R["hid_used"] if r == 1 else None)

            def tile(i, z, uses, more):
                pe.wait_ge(R["xg_lo"], i + 1)
                for c in range(HC):
                    if c % 2 == 0:
                        pe.wait_ge(R["w1_split"], i * G + c // 2 + 1 + 2 * G)
                    pe.wait_ge(R["hid_act"], i * HC + c + 1)
                    for k in range(KD):
                        three(PS[:, c % 2, 0:RT], w1r_hi[:, z, k, c * P:(c + 1) * P], w1r_lo[:, z, k, c * P:(c + 1) * P],
                              xg_hi[:, z, k, :], xg_lo[:, z, k, :], k == 0, k == KD - 1,
                              R["hid_psum"] if k == KD - 1 else None)
                    if c == 1:
                        pe.wait_ge(R["w2_split"], i * G + G + 2 * G)
                    if c >= 2:
                        second(i, z, c - 2)
                    if c == G - 1 and more:
                        rows_in(i + 1, 1 - z, uses + z)
                second(i, z, HC - 2)
                second(i, z, HC - 1)

            rows_in(0, 0, 1)
            with pe.Fori(0, (NT - 1) // 2) as ii:
                for z in range(2):
                    tile(ii * 2 + z, z, ii + 1, True)
            tile(NT - 1, 0, (NT + 1) // 2, False)

        @block.vector
        def _(dve):
            seq = Count(dve, dve_seq)
            V = nc.vector

            for s in GS:
                dve.sem_inc(s["exp_used"], 2)
                dve.sem_inc(s["mask_done"], RING)
                dve.sem_inc(s["alo_ready"], RING)
                dve.sem_inc(s["step_done"], RING)
                dve.sem_inc(s["st_e"], G)
                dve.sem_inc(s["st_a"], G)
                dve.sem_inc(s["fin"], 1)
            for s in FS:
                dve.sem_inc(s["hid_act"], 3)
                dve.sem_inc(s["lo_ready"], 2)
                dve.sem_inc(s["hid_used"], RING)
                dve.sem_inc(s["y_free"], 2)
                dve.sem_inc(s["acc_done"], 2)
            dve.sem_inc(R["w1_split"], 2 * G)
            dve.sem_inc(R["w2_split"], 2 * G)
            dve.sem_inc(R["hid_act"], 2)
            dve.sem_inc(R["lo_ready"], 2)
            dve.sem_inc(R["y_done"], 1)
            for z in range(2):
                dve.sem_inc(R["y_kept"][z], 16)
            dve.sem_inc(R["y_out"], 2)
            dve.sem_inc(row_psum, 1)
            dve.sem_inc(nat_used, 2)

            def norm_stats(stage_no):
                for t in range(T):
                    if stage_no == 0 and t % G == 0:
                        dve.wait_ge(x_in[t // G], 16)
                    V.bn_stats(ln_stat[:, t, :], X[:, t, :]).then_inc(dve_seq, 1)
                    seq.n += 1
                dve.wait_ge(dve_seq, seq.n)
                for t in range(T):
                    V.bn_aggr(ln_mv[:, t, :], ln_stat[:, t, :]).then_inc(dve_seq, 1)
                    seq.n += 1
                dve.wait_ge(dve_seq, seq.n)
                V.tensor_scalar(ln_var[:, :], ln_mv[:, :, 1], LN_EPS, None, ALU.add).then_inc(var_ready, 1)
                dve.wait_ge(rstd_ready, stage_no + 1)
                seq.link(V.tensor_tensor(ln_t[:, :], ln_rstd[:, :], ln_rstd[:, :], ALU.mult))
                seq.link(V.tensor_tensor(ln_t[:, :], ln_t[:, :], ln_var[:, :], ALU.mult))
                seq.link(V.tensor_scalar(ln_t[:, :], ln_t[:, :], -0.5, 1.5, ALU.mult, ALU.add))
                seq.link(V.tensor_tensor(ln_rstd[:, :], ln_rstd[:, :], ln_t[:, :], ALU.mult))

            def normalise(stage_no, g, wide):
                for u in range(G):
                    t = g * G + u
                    V.tensor_scalar(xn[:, u:u + 1, :], X[:, ds(t, 1), :], ln_mv[:, ds(t, 1), 0], ln_rstd[:, ds(t, 1)],
                                    ALU.subtract, ALU.mult).then_inc(xn_ready, 1)
                    if stage_no == 3:
                        V.tensor_scalar(xn_all[:, ds(t, 1), :], X[:, ds(t, 1), :], ln_mv[:, ds(t, 1), 0],
                                        ln_rstd[:, ds(t, 1)], ALU.subtract, ALU.mult)
                for u in range(G):
                    dve.wait_ge(xt_hi_ready, g * G + u + 1 + stage_no * T)
                    src = PS[:, u, 0:D].rearrange("p (k n) -> p k n", k=KD)
                    tok = ds((g * G + u) * P, P)
                    hi = xt_hi[:, :, tok] if wide else xr_hi[:, u, :, :]
                    lo = xt_lo[:, :, tok] if wide else xr_lo[:, u, :, :]
                    V.tensor_tensor(lo, src, hi.bitcast(F32), ALU.subtract).then_inc(xt_lo_ready, 1)

            def split(raw, hi, lo):
                seq.link(V.tensor_copy(hi, raw))
                seq.link(V.tensor_tensor(lo, raw, hi.bitcast(F32), ALU.subtract))

            def diagonals(k, col):
                alone(dve)
                with dve.Fori(0, NG) as q:
                    dve.wait_ge(row_psum, q + (k * NG + 1))
                    for r in range(G):
                        V.tensor_scalar(diag[:, r, :], ident[:, :], col(q * G + r), None, ALU.mult).then_inc(diag_ready, 1)

            def product_column(dst, w, row):
                seq.link(V.tensor_tensor_reduce(scratch[:, :], w, row, 1.0, 0.0, ALU.mult, ALU.add, dst))

            dve.wait_ge(const_ready, 5)
            dve.wait_ge(w_in, 160)
            for k in range(KD):
                product_column(h_raw[:, k, D:D + 1], h_raw[:, k, 0:D], vec_row[:, 0:D])
                product_column(h_raw[:, k, D + 1:D + 2], h_raw[:, k, 0:D], vec_row[:, D:2 * D])
            split(w_raw[:, :, :], w_hi[:, :, :], w_lo[:, :, :])
            seq.link(V.tensor_copy(h_hi[:, :, :], h_raw[:, :, :]))
            V.tensor_tensor(h_lo[:, :, :], h_raw[:, :, :], h_hi[:, :, :].bitcast(F32), ALU.subtract).then_inc(wts_ready, 1)
            norm_stats(0)
            with dve.Fori(0, NG) as g:
                normalise(0, g, False)
                for u in range(G):
                    t = ds(g * G + u, 1)
                    dve.wait_ge(proj_hi, (g * G + u) * 2 + 2)
                    V.tensor_tensor(vl[:, t, :], bank(4 + u % 2, 0, VW), vh[:, t, :].bitcast(F32), ALU.subtract)
                    V.tensor_tensor(hl[:, t, 0:D], bank(6 + u % 2, 0, D), hh[:, t, 0:D].bitcast(F32), ALU.subtract)
                    V.tensor_copy(cols[:, t, :], bank(6 + u % 2, D, D + 4)).then_inc(proj_out, 1)
            dve.wait_ge(proj_out, T)
            seq.link(V.tensor_scalar(cols2[:, :, 0], cols[:, :, 1], -1.0, None, ALU.mult))
            V.tensor_scalar(cols2[:, :, 1], cols[:, :, 1], -LEAK0, None, ALU.mult).then_inc(wts_ready, 1)
            for k in range(2):
                seq.link(V.tensor_scalar(cols2[:, :, 2 + k], cols[:, :, 2 + k], gate_bias[:, k:k + 1], None, ALU.add))
            diagonals(0, lambda t: cols[:, ds(t, 1), 0])
            s = GS[0]
            with dve.Fori(0, NG) as ib:
                for j in range(T):
                    n = ib * T + j
                    b, r = j % 2, j % RING
                    dve.wait_ge(s["exp_ready"], n * 2 + 2)
                    V.scalar_tensor_tensor(out=ee[:, b, :], in0=e1[:, b, :], scalar=BIG, in1=e2[:, b, :],
                                           op0=ALU.min, op1=ALU.min).then_inc(s["exp_used"], 1)
                    dve.wait_ge(s["exp_used"], n + 3)
                    dve.wait_ge(s["at_in"][r], (ib * (T // RING) + j // RING + 1) * 16)
                    V.scalar_tensor_tensor(out=em[:, b, :], in0=at[:, r, :], scalar=0.0, in1=ee[:, b, :],
                                           op0=ALU.not_equal, op1=ALU.mult).then_inc(s["mask_done"], 1)
                    dve.wait_ge(s["mask_done"], n + 1 + RING)
                    dve.wait_ge(s["step_done"], n + 1)
                    V.tensor_copy(e_hi[:, r, :], em[:, b, :]).then_inc(s["ehi_ready"], 1)
                    dve.wait_ge(s["ehi_ready"], n + 1)
                    V.tensor_tensor(e_lo[:, r, :], em[:, b, :], e_hi[:, r, :].bitcast(F32), ALU.subtract)\
                        .then_inc(s["elo_ready"], 1)
                end = seq.loop(ib, 13)
                for it in range(G):
                    if it < G - 1:
                        dve.wait_ge(s["acc_a"], ib * (G - 1) + it + 1)
                    else:
                        dve.wait_ge(s["step_done"], ib * T + T + RING)
                    V.tensor_copy(stage[:, it, 1, :], PS[:, 4 + it, 0:VW]).then_inc(s["st_a"], 1)
                dve.wait_ge(s["st_a"], ib * G + 2 * G)
                dve.wait_ge(s["st_e"], ib * G + 2 * G)
                seq.link(V.tensor_scalar(small[:, 0, :], stage[:, :, 0, D], 1e-5, None, ALU.add))
                seq.link(V.reciprocal(small[:, 1, :], small[:, 0, :]))
                seq.link(V.tensor_tensor(small[:, 2, :], stage[:, :, 1, D], cols2[:, ds(ib * G, G), 2], ALU.add))
                V.tensor_tensor(small[:, 3, :], stage[:, :, 1, D + 1], cols2[:, ds(ib * G, G), 3], ALU.add)\
                    .then_inc(s["z_ready"], 1)
                dve.wait_ge(s["th_ready"], ib * 2 + 1)
                seq.link(V.tensor_scalar(small[:, 6:8, :], small[:, 4:6, :], 0.5, 0.5, ALU.mult, ALU.add))
                seq.link(V.tensor_tensor(small[:, 0, :], small[:, 6, :], small[:, 1, :], ALU.mult))
                for it in range(G):
                    i1 = V.tensor_tensor(stage[:, it, 1, 0:D], stage[:, it, 1, 0:D], bias_row[:, :], ALU.add)
                    i1.then_inc(dve_seq, 1)
                seq.n = seq.n + G
                dve.wait_ge(dve_seq, seq.n)
                for it in range(G):
                    i1 = V.tensor_scalar(stage[:, it, 1, 0:D], stage[:, it, 1, 0:D], small[:, 7, it:it + 1], None, ALU.mult)
                    i1.then_inc(dve_seq, 1)
                seq.n = seq.n + G
                dve.wait_ge(dve_seq, seq.n)
                for it in range(G):
                    i1 = V.scalar_tensor_tensor(out=zt[:, it, :], in0=stage[:, it, 0, 0:D], scalar=small[:, 0, it:it + 1],
                                                in1=stage[:, it, 1, 0:D], op0=ALU.mult, op1=ALU.add)
                i1.then_inc(s["z_ready"], 1)
                dve.wait_ge(s["th_ready"], ib * 2 + 2)
                xg = X[:, ds(ib * G, G), :]
                V.scalar_tensor_tensor(out=xg.rearrange("p t d -> p (t d)"), in0=th[:, :, :].rearrange("p t d -> p (t d)"), scalar=0.5,
                                       in1=xg.rearrange("p t d -> p (t d)"), op0=ALU.mult, op1=ALU.add).then_inc(s["fin"], 1)
                dve.wait_ge(s["fin"], ib + 2)
                V.tensor_scalar(xg.rearrange("p t d -> p (t d)"), xg.rearrange("p t d -> p (t d)"), 0.5, None, ALU.add).then_inc(x_done, G)
                end(NG)
            dve.wait_ge(x_done, T)

            def ffn(layer):
                s = FS[layer]
                st = 1 + 2 * layer
                norm_stats(st)
                dve.wait_ge(s["aux_in"], 16 * (4 if layer == 0 else 3))
                dve.wait_ge(s["tree_in"], 2)
                split(gw_raw[:, :, :], gw_hi[:, :, :], gw_lo[:, :, :])
                if layer == 0:
                    seq.link(V.tensor_scalar(rb_col[:, :], rb_col[:, :], 0.5, None, ALU.mult))
                V.tensor_copy(sel[:, 0, :], sel_f[:, 0, :]).then_inc(wts_ready, 1)
                alone(dve)
                with dve.Fori(0, NG) as g:
                    normalise(st, g, True)
                    end = seq.loop(g, 10)
                    dve.wait_ge(s["lg_psum"], g + 1)
                    lgp = PS[:, 5, :].rearrange("p (u n) -> p u n", u=G)[:, :, 0:E]
                    if layer == 0:
                        seq.link(V.tensor_scalar(pq[:, 0, :, :], lgp, 0.5, 0.5, ALU.mult, ALU.add))
                        seq.link(V.tensor_scalar(pq[:, 1, :, :], lgp, -0.5, 0.5, ALU.mult, ALU.add))
                        p_, q_ = pq[:, 0], pq[:, 1]
                        seq.link(V.tensor_copy(tree[:, 0, :, 0:1], q_[:, :, 0:1]))
                        seq.link(V.tensor_copy(tree[:, 0, :, 1:2], p_[:, :, 0:1]))
                        seq.link(V.tensor_tensor(tree[:, 1, :, 0:4:2], tree[:, 0, :, 0:2], q_[:, :, 1:3], ALU.mult))
                        seq.link(V.tensor_tensor(tree[:, 1, :, 1:4:2], tree[:, 0, :, 0:2], p_[:, :, 1:3], ALU.mult))
                        seq.link(V.tensor_tensor(gate[:, :, 0:8:2], tree[:, 1, :, 0:4], q_[:, :, 3:7], ALU.mult))
                        seq.link(V.tensor_tensor(gate[:, :, 1:8:2], tree[:, 1, :, 0:4], p_[:, :, 3:7], ALU.mult))
                    seq.link(V.tensor_copy(gate_hi[:, :, :], gate[:, :, :]))
                    seq.link(V.tensor_copy(gate2[:, :, 0:E], gate_hi[:, :, :].bitcast(F32)))
                    V.tensor_tensor(gate2[:, :, E:2 * E], gate[:, :, :], gate_hi[:, :, :].bitcast(F32), ALU.subtract)\
                        .then_inc(s["gate2_ready"], 1)
                    end(NG)
                dve.memset(acc[:, :, :], 0.0).then_inc(dve_seq, 1)
                seq.n += 1
                dve.wait_ge(dve_seq, seq.n)

                def split_quarter(e_next, q, par, first=False):
                    c1 = ds(q * D, D)
                    c2 = ds(q * 2, 2)
                    n = e_next * (2 * NG) + q * 2
                    V.tensor_copy(w1_hi[:, par, :, c1], w1_raw[:, :, c1]).then_inc(s["whi"], 1)
                    V.tensor_copy(w2_hi[:, par, c2, :], w2_raw[:, c2, :]).then_inc(s["whi"], 1)
                    if not first:
                        V.tensor_copy(sel[:, par:par + 1, :], sel_f[:, ds(e_next, 1), :])
                    dve.wait_ge(s["whi"], n + 2)
                    V.tensor_tensor(w1_lo[:, par, :, c1], w1_raw[:, :, c1], w1_hi[:, par, :, c1].bitcast(F32), ALU.subtract)
                    V.tensor_tensor(w2_lo[:, par, c2, :], w2_raw[:, c2, :], w2_hi[:, par, c2, :].bitcast(F32), ALU.subtract)\
                        .then_inc(s["split_done"], 1)

                dve.wait_ge(s["raw1_in"], 16)
                dve.wait_ge(s["raw2_in"], 16)
                for q in range(NG):
                    split_quarter(0, q, 0, first=True)

                def pair(ep, last):
                    for par in range(2):
                        e = ep * 2 + par
                        more = not (last and par == 1)
                        if more:
                            dve.wait_ge(s["raw1_in"], (e + 2) * 16)
                            dve.wait_ge(s["raw2_in"], (e + 2) * 16)
                        alone(dve)
                        with dve.Fori(0, 2) as gp:
                            for pg in range(2):
                                g = gp * 2 + pg
                                n = e * NG + g
                                for c in range(HC):
                                    m = n * HC + c
                                    dve.wait_ge(s["hid_act"], n * (HC + 1) + c + 2 + 3)
                                    dve.wait_ge(s["hid_used"], m + 1)
                                    V.tensor_copy(hid_hi[:, c % RING, :], hf[:, c % 2, :]).then_inc(s["hi_ready"], 1)
                                    dve.wait_ge(s["hi_ready"], m + 1)
                                    V.tensor_tensor(hid_lo[:, c % RING, :], hf[:, c % 2, :],
                                                    hid_hi[:, c % RING, :].bitcast(F32), ALU.subtract).then_inc(s["lo_ready"], 1)
                                    if c == RING and more:
                                        split_quarter(e + 1, g, 1 - par)
                                for d in range(KD):
                                    dve.wait_ge(s["y_done"], n + 1)
                                    if d == KD - 1:
                                        dve.wait_ge(s["hid_used"], (n + 1) * HC + RING)
                                    i1 = V.scalar_tensor_tensor(out=yt[:, d, :], in0=PS[:, 3 + 2 * pg + d, :],
                                                                scalar=b2_cols[:, ds(e, 1), d], in1=gate_b[:, pg, :],
                                                                op0=ALU.add, op1=ALU.mult)
                                    i1.then_inc(s["y_tmp"], 1)
                                dve.wait_ge(s["y_tmp"], n * 2 + 2)
                                dve.sem_inc(s["y_free"], 1)
                                i1 = V.tensor_tensor(acc[:, :, ds(g * GW, GW)], acc[:, :, ds(g * GW, GW)], yt[:, :, :], ALU.add)
                                i1.then_inc(s["acc_done"], 1)

                alone(dve)
                with dve.Fori(0, E // 2 - 1) as ep:
                    pair(ep, False)
                pair(E // 2 - 1, True)
                for t in range(T):
                    dve.wait_ge(s["back_psum"], t + 1)
                    V.tensor_tensor(X[:, t, :], X[:, t, :], PS[:, t % G, 0:D], ALU.add).then_inc(s["back_done"], 1)
                    dve.wait_ge(s["back_done"], t + 1)
                    dve.sem_inc(x_done, 1)

            ffn(0)
            dve.wait_ge(w_in, 160 + 80)
            for k in range(KD):
                product_column(w_raw[:, k, D:D + 1], h_raw[:, k, 0:D], vec_row[:, 0:D])
            dve.sem_inc(h_free, 1)
            dve.wait_ge(w_in, 160 + 96)
            for k in range(KD):
                product_column(w_raw[:, k, D + 1:D + 2], h_raw[:, k, 0:D], vec_row[:, 0:D])
            seq.link(V.memset(ff[:, :, 0:T], 0.0))
            seq.link(V.memset(ff[:, 0, 0:T], 1.0))
            seq.link(V.tensor_copy(hh[:, :, D], ff[:, 0, 0:T]))
            seq.link(V.tensor_copy(hh[:, :, D + 1], ff[:, 1, 0:T]))
            seq.link(V.tensor_copy(hl[:, :, D], ff[:, 1, 0:T]))
            seq.link(V.tensor_copy(hl[:, :, D + 1], ff[:, 1, 0:T]))
            seq.link(V.tensor_copy(w_hi[:, :, :], w_raw[:, :, :]))
            V.tensor_tensor(w_lo[:, :, :], w_raw[:, :, :], w_hi[:, :, :].bitcast(F32), ALU.subtract).then_inc(wts_ready, 1)
            norm_stats(2)
            with dve.Fori(0, NG) as g:
                normalise(2, g, False)
                for u in range(G):
                    t = ds(g * G + u, 1)
                    dve.wait_ge(proj_done, g * G + u + 1 + T)
                    if u >= 2:
                        dve.wait_ge(proj_hi, g * G + u + 2 * T - 1)
                    V.tensor_copy(cols[:, t, 0:2], bank(4 + u % 2, D, D + 2))
                    V.tensor_tensor(ff[:, u % 2, :], PS[:, 4 + u % 2, 0:D], bias_row[:, :], ALU.add).then_inc(proj_out, 1)
                    dve.wait_ge(proj_hi, g * G + u + 1 + 2 * T)
                    V.tensor_tensor(hl[:, t, 0:D], ff[:, u % 2:u % 2 + 1, :], hh[:, t, 0:D].bitcast(F32), ALU.subtract)\
                        .then_inc(dve_seq, 1)
            seq.n += T
            dve.wait_ge(dve_seq, seq.n)
            seq.link(V.tensor_scalar(cols2[:, :, 2], cols[:, :, 0], gate_bias[:, 0:1], None, ALU.add))
            seq.link(V.tensor_copy(cols2[:, :, 0], cols[:, :, 1]))
            V.tensor_scalar(cols2[:, :, 1], cols[:, :, 1], LEAK1, None, ALU.mult).then_inc(wts_ready, 1)
            diagonals(1, lambda t: cols[:, ds(t, 1), 1])
            dve.wait_ge(row_copied, 2 * NG)
            seq.link(V.tensor_reduce(s2_min[:, :], s2_row[:, :], AX.X, ALU.min))
            seq.link(V.tensor_scalar(s2_pos[:, :], s2_row[:, :], s2_min[:, :], 1.0, ALU.subtract, ALU.add))
            with dve.Fori(0, T // 2) as q:
                end = seq.loop(q, 2)
                for r in range(2):
                    dve.wait_ge(nat_in[r], q * 16 + 16)
                    V.scalar_tensor_tensor(out=masked[:, r, :], in0=adj_rows[:, r, :], scalar=0.0, in1=s2_pos[:, :],
                                           op0=ALU.is_gt, op1=ALU.mult).then_inc(nat_used, 1)
                    dve.wait_ge(nat_used, q * 2 + r + 3)
                    seq.link(V.tensor_reduce(mx[:, 0, ds(q * 2 + r, 1)], masked[:, r, :], AX.X, ALU.max))
                end(T // 2)
            seq.link(V.tensor_scalar(mx[:, 1, :], mx[:, 0, :], 0.0, None, ALU.is_le))
            seq.link(V.tensor_scalar(mx[:, 2, :], mx[:, 0, :], s2_min[:, :], -1.0, ALU.add, ALU.add))
            seq.link(V.tensor_tensor(mx[:, 2, :], mx[:, 2, :], cols2[:, :, 2], ALU.add))
            seq.link(V.scalar_tensor_tensor(out=mx[:, 3, :], in0=mx[:, 2, :], scalar=LEAK1, in1=mx[:, 2, :],
                                            op0=ALU.mult, op1=ALU.max))
            seq.link(V.tensor_tensor(mx[:, 4, :], cols2[:, :, 2], mx[:, 3, :], ALU.subtract))
            seq.link(V.scalar_tensor_tensor(out=mx[:, 5, :], in0=cols2[:, :, 2], scalar=LEAK1, in1=mx[:, 3, :],
                                            op0=ALU.mult, op1=ALU.subtract))
            diagonals(2, lambda t: mx[:, 4, ds(t, 1)])
            diagonals(3, lambda t: mx[:, 5, ds(t, 1)])
            dve.wait_ge(mean_psum, 1)
            seq.link(V.tensor_scalar(mean_row[:, :], PS[:, 6, 0:D], 1.0 / N, None, ALU.mult))
            s = GS[1]
            with dve.Fori(0, NG) as ib:
                for j in range(T):
                    n = ib * T + j
                    b, r = j % 2, j % RING
                    dve.wait_ge(s["exp_ready"], n * 2 + 2)
                    V.tensor_tensor(ee[:, b, :], e1[:, b, :], e2[:, b, :], ALU.max).then_inc(s["exp_used"], 1)
                    dve.wait_ge(s["exp_used"], n + 3)
                    dve.wait_ge(s["at_in"][r], (ib * (T // RING) + j // RING + 1) * 16)
                    if j >= 2:
                        dve.wait_ge(s["elo_ready"], n - 1)
                    V.scalar_tensor_tensor(out=em[:, b, :], in0=at[:, r, :], scalar=0.0, in1=ee[:, b, :],
                                           op0=ALU.is_gt, op1=ALU.min).then_inc(s["mask_done"], 1)
                    dve.wait_ge(s["mask_done"], n + 1 + RING)
                    dve.wait_ge(s["step_done"], n + 1)
                    V.tensor_copy(e_hi[:, r, :], em[:, b, :]).then_inc(s["ehi_ready"], 1)
                end = seq.loop(ib, 10)
                dve.wait_ge(s["st_e"], ib * G + 2 * G)
                iso = mx[:, 1, ds(ib * G, G)]
                seq.link(V.tensor_tensor(small[:, 0, :], stage[:, :, 0, D], iso, ALU.add))
                seq.link(V.reciprocal(small[:, 1, :], small[:, 0, :]))
                for it in range(G):
                    seq.link(V.scalar_tensor_tensor(out=X[:, ds(ib * G + it, 1), :], in0=stage[:, it:it + 1, 0, 0:D],
                                                    scalar=small[:, 1, it:it + 1], in1=X[:, ds(ib * G + it, 1), :],
                                                    op0=ALU.mult, op1=ALU.add))
                dve.sem_inc(s["fin"], 1)
                for it in range(G):
                    seq.link(V.scalar_tensor_tensor(out=X[:, ds(ib * G + it, 1), :], in0=mean_row[:, :].unsqueeze(1),
                                                    scalar=mx[:, 1, ds(ib * G + it, 1)], in1=X[:, ds(ib * G + it, 1), :],
                                                    op0=ALU.mult, op1=ALU.add))
                dve.sem_inc(x_done, G)
                end(NG)
            norm_stats(3)
            dve.wait_ge(R["gw_in"], 16)
            seq.link(V.tensor_copy(gw1_hi[:, :, :], gw1_raw[:, :, :]))
            V.tensor_tensor(gw1_lo[:, :, :], gw1_raw[:, :, :], gw1_hi[:, :, :].bitcast(F32), ALU.subtract).then_inc(wts_ready, 1)
            with dve.Fori(0, NG) as g:
                normalise(3, g, True)
                dve.wait_ge(R["lg_psum"], g + 1)
                V.tensor_copy(lga[:, ds(g * G, G), :], PS[:, 5, :].rearrange("p (u n) -> p u n", u=G)[:, :, 0:E])\
                    .then_inc(dve_seq, 1)
            seq.n += NG
            dve.wait_ge(dve_seq, seq.n)
            dve.wait_ge(R["consts"], 3)
            for t in range(T):
                V.max(top[:, t, :], lga[:, t, :]).then_inc(dve_seq, 1)
            seq.n += T
            dve.wait_ge(dve_seq, seq.n)
            for t in range(T):
                V.max_index(topi[:, t, :], top[:, t, :], lga[:, t, :]).then_inc(dve_seq, 1)
            seq.n += T
            V.tensor_tensor(gate_e[:, 0, :], top[:, :, 1], top[:, :, 0], ALU.subtract).then_inc(R["gap_ready"], 1)
            dve.wait_ge(dve_seq, seq.n)
            seq.link(V.tensor_copy(topf[:, :, :], topi[:, :, 0:2]))
            for k in range(2):
                seq.link(V.tensor_tensor(hot[:, k, :, :], iota8[:, :, :].to_broadcast([P, T, E]),
                                         topf[:, :, k:k + 1].to_broadcast([P, T, E]), ALU.is_equal))
            V.tensor_tensor(hot[:, 2, :, :], hot[:, 0, :, :], hot[:, 1, :, :], ALU.add).then_inc(R["hot_ready"], 1)
            dve.wait_ge(R["gap_exp"], 1)
            seq.link(V.tensor_scalar(gate_e[:, 0, :], gate_e[:, 1, :], 1.0, None, ALU.add))
            seq.link(V.reciprocal(gate_e[:, 2, :], gate_e[:, 0, :]))
            seq.link(V.tensor_tensor(gate_e[:, 3, :], gate_e[:, 1, :], gate_e[:, 2, :], ALU.mult))
            seq.link(V.memset(count_t[:, 0:1, :], 0.0))
            dve.wait_ge(R["count_psum"], 1)
            per_tile = PS[:, 7, 0:T * E].rearrange("p (t e) -> p t e", t=T)
            for t in range(T):
                seq.link(V.tensor_tensor(count_t[:, t + 1, :], count_t[:, t, :], per_tile[:, t, :], ALU.add))
            seq.link(V.tensor_scalar(tiles_e[:, 0, :], count_t[:, T, :], 0.0, None, ALU.is_gt))
            for k in range(1, N // RT):
                seq.link(V.scalar_tensor_tensor(out=tiles_e[:, 0, :], in0=count_t[:, T, :], scalar=float(k * RT),
                                                in1=tiles_e[:, 0, :], op0=ALU.is_gt, op1=ALU.add))
            seq.link(V.memset(tile_end[:, 0, 0:1], 0.0))
            for e in range(E):
                seq.link(V.tensor_tensor(tile_end[:, 0, e + 1:e + 2], tile_end[:, 0, e:e + 1], tiles_e[:, 0, e:e + 1], ALU.add))
            seq.link(V.tensor_scalar(tiles_e[:, 0, :], tile_end[:, 0, 0:E], float(RT), None, ALU.mult))
            seq.link(V.tensor_tensor(slot[:, :, :], PS[:, 6, 0:T * E].rearrange("p (t e) -> p t e", t=T),
                                     count_t[:, 0:T, :], ALU.add))
            seq.link(V.tensor_tensor(slot[:, :, :], slot[:, :, :], tiles_e[:, :, :].to_broadcast([P, T, E]), ALU.add))
            for k in range(2):
                seq.link(V.tensor_tensor(slot_t[:, :, :], slot[:, :, :], hot[:, k, :, :], ALU.mult))
                seq.link(V.tensor_reduce(row_of[:, k, :], slot_t[:, :, :], AX.X, ALU.add))
            seq.link(V.tensor_copy(row_u[:, :, :], row_of[:, :, :]))
            seq.link(V.tensor_scalar(tile_e[:, :], iota_t[:, :], tile_end[:, 0, 1:2], None, ALU.is_ge))
            for e in range(1, E):
                seq.link(V.scalar_tensor_tensor(out=tile_e[:, :], in0=iota_t[:, :], scalar=tile_end[:, 0, e + 1:e + 2],
                                                in1=tile_e[:, :], op0=ALU.is_ge, op1=ALU.add))
            seq.link(V.tensor_scalar(tile_e[:, :], tile_e[:, :], float(E - 1), None, ALU.min))
            V.tensor_copy(tile_u[:, :], tile_e[:, :]).then_inc(R["routed"], 1)

            def w1_low(i, z, q):
                dve.wait_ge(R["w_hi"], i * 2 * G + q + 1)
                c = slice(q * D, (q + 1) * D)
                V.tensor_tensor(w1r_lo[:, z, :, c], w1r_raw[:, z, :, c], w1r_hi[:, z, :, c].bitcast(F32), ALU.subtract)\
                    .then_inc(R["w1_split"], 1)

            def rows_low(i, z):
                dve.wait_ge(R["xg_hi"], i + 1)
                V.tensor_tensor(xg_lo[:, z, :, :], PS[:, 2, :].rearrange("p (k n) -> p k n", k=KD),
                                xg_hi[:, z, :, :].bitcast(F32), ALU.subtract).then_inc(R["xg_lo"], 1)

            def tile(i, z, uses, more):
                for c in range(HC):
                    m = i * HC + c
                    dve.wait_ge(R["hid_act"], m + 3)
                    if c >= RING:
                        dve.wait_ge(R["hid_used"], i * (HC - 1) + c - RING + 1)
                    V.tensor_copy(hr_hi[:, c % RING, :], hfr[:, c % 2, :]).then_inc(R["hi_ready"], 1)
                    dve.wait_ge(R["hi_ready"], m + 1)
                    V.tensor_tensor(hr_lo[:, c % RING, :], hfr[:, c % 2, :], hr_hi[:, c % RING, :].bitcast(F32),
                                    ALU.subtract).then_inc(R["lo_ready"], 1)
                    if more and c < G:
                        w1_low(i + 1, 1 - z, c)
                    if more and c == G + 1:
                        rows_low(i + 1, 1 - z)
                dve.wait_ge(R["b2"][z], uses * 16)
                dve.wait_ge(R["y_kept"][z], uses * 16)
                dve.wait_ge(R["y_done"], i * 2 + 3)
                for r in range(2):
                    m = V.tensor_tensor(y_sb[:, z, r, :], PS[:, 4 + 2 * z + r, 0:D], b2_t[:, z, :], ALU.add)
                m.then_inc(R["y_out"], 1)

            for q in range(G):
                w1_low(0, 0, q)
            rows_low(0, 0)
            with dve.Fori(0, (NT - 1) // 2) as ii:
                for z in range(2):
                    tile(ii * 2 + z, z, ii + 1, True)
            tile(NT - 1, 0, (NT + 1) // 2, False)
            for t in range(T):
                dve.wait_ge(gathered[t // G], 2 * G * 16)
                for k, y in enumerate((y1, y2)):
                    seq.link(V.scalar_tensor_tensor(out=X[:, t, :], in0=y[:, t, :], scalar=gate_e[:, 2 + k, t:t + 1],
                                                    in1=X[:, t, :], op0=ALU.mult, op1=ALU.add))
                dve.sem_inc(x_done, 1)


def kernel(**inputs):
    import numpy as np
    import concourse.bacc as bacc
    from concourse.bass_utils import run_bass_kernel_spmd

    def laid(b):
        e, n = b.shape
        return np.ascontiguousarray(b.reshape(e, n // 128, 128).transpose(2, 0, 1))

    arrays = {k: np.ascontiguousarray(v) for k, v in inputs.items()}
    arrays["L1_gnn_a_b"] = arrays["L1_gnn_a_b"].reshape(1)
    arrays["adj_t"] = np.ascontiguousarray(arrays["adj"].T)
    arrays["L0_ffn_rw_t"] = np.ascontiguousarray(arrays.pop("L0_ffn_rw").T)
    for layer in (0, 1):
        for b in ("b1", "b2"):
            if (layer, b) != (1, "b2"):
                arrays[f"L{layer}_ffn_{b}_p"] = laid(arrays.pop(f"L{layer}_ffn_{b}"))
    nc = bacc.Bacc("TRN2", target_bir_lowering=False, num_devices=1)
    aps = {k: nc.dram_tensor(k + "_dram", v.shape, mybir.dt.from_np(v.dtype), kind="ExternalInput").ap()
           for k, v in arrays.items()}
    aps["out"] = nc.dram_tensor("out_dram", (2048, 256), mybir.dt.float32, kind="ExternalOutput").ap()
    gnn_ffn_program(nc, aps)
    r = run_bass_kernel_spmd(nc, [{k + "_dram": v for k, v in arrays.items()}], core_ids=[0])
    return r.results[0]["out_dram"]
```

```python
from contextlib import ExitStack

import concourse.bass as bass
from concourse import mybir
from concourse.alu_op_type import AluOpType as ALU

ACT = mybir.ActivationFunctionType
AX = mybir.AxisListType
F32 = mybir.dt.float32
F32R = mybir.dt.float32r
U32 = mybir.dt.uint32
U8 = mybir.dt.uint8
ds = bass.ds

P = 128
N = 2048
D = 256
KD = D // P
T = N // P
G = 4
NG = T // G
GW = G * P
E = 8
HID = 1024
HC = HID // P
VW = D + 2
PW = D + 4
RING = 4
LN_EPS = 1e-5
BIG = 3.0e38
RT = 2 * P
NT = (2 * N + E * (RT - 1)) // RT
HT = 2 * NT
ROUND = 1.5 * 2 ** 23
CUT = 2 * GW // E
LEAK0, LEAK1 = 0.01, 0.2
EVAC, GATES = 2, (4, 9)


class Count:

    def __init__(self, eng, sem):
        self.eng, self.sem, self.n = eng, sem, 0

    def link(self, ins):
        ins.then_inc(self.sem, 1)
        self.n = self.n + 1
        self.eng.wait_ge(self.sem, self.n)

    def loop(self, i, per):
        start = self.n
        self.n = i * per + start

        def end(turns):
            self.n = start + per * turns
        return end


def gnn_ffn_program(nc, a):
    with ExitStack() as ctx:
        place = {"at": -(-nc.sbuf_base // 32) * 32}
        limit = nc.sbuf_usable_end

        def sb(name, shape, dt=F32):
            size = 1 if dt == U8 else 4
            for s in shape[1:]:
                size *= s
            t = nc.alloc_sbuf_tensor_at(name, shape, dt, offset=place["at"])
            place["at"] += -(-size // 32) * 32
            assert place["at"] <= limit, (name, place["at"] - limit)
            return t

        def sem(name):
            return ctx.enter_context(nc.semaphore(name))

        PS = ctx.enter_context(nc.psum_tensor("PS", [P, 8, 512], F32))

        X = sb("X", [P, T, D])
        ident = sb("ident", [P, P])
        ones = sb("ones", [P, P])
        ones_r = sb("ones_r", [P, P], F32R)
        ln_stat = sb("ln_stat", [P, G, 6])
        ln_b = sb("ln_b", [P, NG, G, 2])
        ln_mv = sb("ln_mv", [P, T, 2])
        ln_v = sb("ln_v", [P, G])
        ln_r = sb("ln_r", [P, G])
        ln_rstd = sb("ln_rstd", [P, T])
        ln_t = sb("ln_t", [P, G])
        minus_half = sb("minus_half", [P, G])
        xn = sb("xn", [P, G, D])
        cols = sb("cols", [P, T, 4])
        cols2 = sb("cols2", [P, T, 4])
        warm = sb("warm", [P, 2])
        shared_end = place["at"]

        xr_hi = sb("xr_hi", [P, G, KD, P], F32R)
        xr_lo = sb("xr_lo", [P, G, KD, P], F32R)
        w_raw = sb("w_raw", [P, KD, VW])
        w_hi = sb("w_hi", [P, KD, VW], F32R)
        w_lo = sb("w_lo", [P, KD, VW], F32R)
        h_raw = sb("h_raw", [P, KD, PW])
        h_hi = sb("h_hi", [P, KD, PW], F32R)
        h_lo = sb("h_lo", [P, KD, PW], F32R)
        vec_row = sb("vec_row", [P, 2 * D])
        bias_row = sb("bias_row", [P, D])
        gate_bias = sb("gate_bias", [P, 2])
        scratch = sb("scratch", [P, D])
        graph_w_end = place["at"]
        row_a = sb("row_a", [P, N])
        at_place = place["at"]
        at = sb("at", [P, RING, GW])
        row_b = sb("row_b", [P, N])
        arg = sb("arg", [P, 2, GW])
        ex = sb("ex", [P, 2, GW])
        em = sb("em", [P, RING, GW])
        e_hi = sb("e_hi", [P, RING, GW], F32R)
        e_lo = sb("e_lo", [P, RING, GW], F32R)
        stage = sb("stage", [P, G, 2, VW])
        small = sb("small", [P, 8, G])
        zt = sb("zt", [P, G, D])
        th = sb("th", [P, G, D])
        hh = sb("hh", [P, T, VW], F32R)
        hl = sb("hl", [P, T, VW], F32R)
        graph_end = place["at"]
        a_hi = sb("a_hi", [P, RING, GW], F32R)
        a_lo = sb("a_lo", [P, RING, GW], F32R)
        vh = sb("vh", [P, T, VW], F32R)
        vl = sb("vl", [P, T, VW], F32R)

        b1_cols = sb("b1_cols", [P, E, HC])
        b2_cols = sb("b2_cols", [P, E, KD])
        gw_raw = sb("gw_raw", [P, KD, P])
        gw_hi = sb("gw_hi", [P, KD, P], F32R)
        gw_lo = sb("gw_lo", [P, KD, P], F32R)
        rb_col = sb("rb_col", [P, 1])
        sel_f = sb("sel_f", [P, E, P])

        place["at"] = graph_end
        s2_row = sb("s2_row", [P, N])
        near = sb("near", [P, T, N], U8)
        masked = sb("masked", [P, N])
        mean_row = sb("mean_row", [P, D])
        s2_min = sb("s2_min", [P, 1])
        s2_mins = sb("s2_mins", [P, NG])
        mx = sb("mx", [P, 8, T])
        ff = sb("ff", [P, 2, D])
        ff_end = place["at"]

        place["at"] = shared_end
        w1_raw = sb("w1_raw", [P, KD, HID])
        w2_raw = sb("w2_raw", [P, HC, D])
        xt_at = place["at"]
        xt_hi = sb("xt_hi", [P, KD, N], F32R)
        xt_lo = sb("xt_lo", [P, KD, N], F32R)
        acc = sb("acc", [P, KD, N])
        g_row = sb("g_row", [P, N], F32R)
        w1_hi = sb("w1_hi", [P, 2, KD, HID], F32R)
        w1_lo = sb("w1_lo", [P, 2, KD, HID], F32R)
        w2_hi = sb("w2_hi", [P, 2, HC, D], F32R)
        w2_lo = sb("w2_lo", [P, 2, HC, D], F32R)
        hf = sb("hf", [P, 2, GW])
        hid_hi = sb("hid_hi", [P, RING, GW], F32R)
        hid_lo = sb("hid_lo", [P, RING, GW], F32R)
        place_out = place["at"]
        gate_b = sb("gate_b", [P, 2, GW])
        yt = sb("yt", [P, 2, GW])
        place_gate = place["at"]
        lg_t = sb("lg_t", [P, GW])
        lg = sb("lg", [P, T, E])
        pq = sb("pq", [P, 2, T, E])
        tree = sb("tree", [P, 2, T, E])
        gate = sb("gate", [P, T, E])
        gate_hi = sb("gate_hi", [P, T, E], F32R)
        place["at"] = max(place["at"], place_gate + 2 * (N // 2) * 4 + 2 * (N // 2))
        sel = sb("sel", [P, 2, P], F32R)

        place["at"] = place_gate
        half = sb("half", [P, 2, N // 2])
        half8 = sb("half8", [P, 2, N // 2], U8)

        place["at"] = place_out
        gate2 = sb("gate2", [P, T, P])

        place["at"] = shared_end
        w1r_raw = sb("w1r_raw", [P, 2, KD, HID])
        place["at"] = xt_at + 2 * KD * N * 4
        lg1_t = sb("lg1_t", [P, GW])
        xn_all = sb("xn_all", [P, T, D])
        lga = sb("lga", [P, T, E])
        top = sb("top", [P, T, 8])
        topi = sb("topi", [P, T, 8], U32)
        topf = sb("topf", [P, T, 2])
        gate_e = sb("gate_e", [P, 4, T])
        iota8 = sb("iota8", [P, 1, E])
        before = sb("before", [P, P])
        hot = sb("hot", [P, 3, T, E])
        slot = sb("slot", [P, T, E])
        slot_t = sb("slot_t", [P, T, E])
        counts = sb("counts", [P, 2, T + 1, E])
        over = sb("over", [P, E, N // RT])
        ended = sb("ended", [P, NT + 1, E])
        tiles_e = sb("tiles_e", [P, 1, E])
        ends = sb("ends", [P, 2, E + 1, 1])
        row_of = sb("row_of", [P, 2, T])
        row_hi = sb("row_hi", [P, 2, T])
        row_lo = sb("row_lo", [P, 2, T])
        node_k = sb("node_k", [P, 2, T])
        iota_p = sb("iota_p", [P, P])
        iota_row = sb("iota_row", [P, HT + 1])
        spare_row = sb("spare_row", [P, HT])
        place_f = sb("place_f", [P, 4, HT + 1])
        node_u = sb("node_u", [P, HT], U32)
        dest_u = sb("dest_u", [P, HT], U32)
        iota_t = sb("iota_t", [P, NT + 1])
        tile_e = sb("tile_e", [P, NT + 1])
        tile_u = sb("tile_u", [P, NT + 1], U32)
        w2r_raw = sb("w2r_raw", [P, 2, HC, D])
        w1r_hi = sb("w1r_hi", [P, 2, KD, HID], F32R)
        w1r_lo = sb("w1r_lo", [P, 2, KD, HID], F32R)
        w2r_hi = sb("w2r_hi", [P, 2, HC, D], F32R)
        w2r_lo = sb("w2r_lo", [P, 2, HC, D], F32R)
        routed_end = place["at"]
        place["at"] = xt_at
        y1 = sb("y1", [P, T, D])
        xg = sb("xg", [P, 2, 2, D])
        xg_hi = sb("xg_hi", [P, 2, KD, RT], F32R)
        xg_lo = sb("xg_lo", [P, 2, KD, RT], F32R)
        assert place["at"] <= xt_at + 2 * KD * N * 4
        place["at"] = routed_end
        b1_t = sb("b1_t", [P, 2, HC])
        b2_t = sb("b2_t", [P, 2, D])
        hidden_at = place["at"]
        hfr = sb("hfr", [P, 2, 2 * RT])
        hr_hi = sb("hr_hi", [P, 2, 2 * RT], F32R)
        hr_lo = sb("hr_lo", [P, 2, 2 * RT], F32R)
        y_sb = sb("y_sb", [P, 2, 2, D])
        pick = sb("pick", [P, 2, 2], U32)
        put = sb("put", [P, 2, 2], U32)
        put_end = place["at"]
        place["at"] = hidden_at
        at_lo = sb("at_lo", [P, 2, T, P])
        place["at"] = xt_at
        up_to = sb("up_to", [P, 2, T, HT + 1])
        place["at"] = shared_end
        y2 = sb("y2", [P, T, D])

        place["at"] = at_place
        near_t = sb("near_t", [P, 2, T // 2, GW], U8)

        near_v = nc.dram_tensor("near", [2, T, P, N], U8).ap()
        assert max(ff_end, put_end) <= limit // 32 * 32 - 3 * KD * P * 4
        place["at"] = limit // 32 * 32 - 3 * KD * P * 4
        gw1_raw = sb("gw1_raw", [P, KD, P])
        gw1_hi = sb("gw1_hi", [P, KD, P], F32R)
        gw1_lo = sb("gw1_lo", [P, KD, P], F32R)

        xn_rows = nc.dram_tensor("xn_rows", [N, D], F32).ap()
        yn_rows = nc.dram_tensor("yn_rows", [2 * N + NT * RT, D], F32).ap()

        x_in = [sem(f"x_in{g}") for g in range(NG)]
        w_in = sem("w_in")
        const_ready = sem("const_ready")
        pool_seq = sem("pool_seq")
        dve_seq = sem("dve_seq")
        act_seq = sem("act_seq")
        wts_ready = sem("wts_ready")
        var_ready = sem("var_ready")
        rstd_ready = sem("rstd_ready")
        xn_ready = sem("xn_ready")
        xt_psum = sem("xt_psum")
        xt_hi_ready = sem("xt_hi_ready")
        xt_lo_ready = sem("xt_lo_ready")
        proj_done = sem("proj_done")
        proj_hi = sem("proj_hi")
        proj_out = sem("proj_out")
        low_done = sem("low_done")
        diag_ready = [sem(f"diag_ready{k}") for k in range(4)]
        row_psum = [sem(f"row_psum{k}") for k in range(4)]
        row_copied = [sem(f"row_copied{k}") for k in range(4)]
        h_free = sem("h_free")
        near_in = [sem(f"near_in{i}") for i in range(2)]
        half_in = [sem(f"half_in{i}") for i in range(2)]
        half_done = sem("half_done")
        half_kept = [sem(f"half_kept{i}") for i in range(2)]
        mean_psum = sem("mean_psum")
        x_done = sem("x_done")
        out_done = sem("out_done")

        waited = {e.engine: sem(f"waited_{k}") for k, e in
                  (("act", nc.scalar), ("pe", nc.tensor), ("dve", nc.vector), ("pool", nc.gpsimd), ("sp", nc.sync))}

        def graph_sems(n):
            s = {k: sem(f"{k}_{n}") for k in (
                "arg_ready", "exp_ready", "mask_done", "ehi_ready", "elo_ready", "step_done", "acc_e", "st_e", "fin")
                 + (("ahi_ready", "alo_ready", "acc_a", "st_a", "z_ready", "th_ready") if n == 0 else ())}
            s["at_in"] = [sem(f"at_in{i}_{n}") for i in range(RING if n == 0 else 2)]
            return s

        def ffn_sems(n):
            return {k: sem(f"{k}_{n}") for k in (
                "lgt_psum", "lgt_ready", "lg_psum", "lg_copied", "gate2_ready", "g2_psum", "g_row_ready",
                "raw1_in", "raw2_in", "split_done", "whi", "hid_psum", "hid_act", "hi_ready", "lo_ready",
                "hid_used", "y_done", "y_free", "y_tmp", "acc_done", "back_psum", "back_done",
                "aux_in", "tree_in", "zeroed")}

        GS = [graph_sems(0), graph_sems(1)]
        FS = [ffn_sems(0)]
        R = {k: sem(f"r_{k}") for k in (
            "gw_room", "gw_in", "consts", "lgt_psum", "lgt_ready", "lg_psum", "lg_copied", "gap_ready", "gap_exp", "hot_ready",
            "count_psum", "routed", "rows_kept", "row_hot", "inverse_psum", "placed", "pool_seq", "w1_split", "w2_split", "w_hi", "xg_psum", "xg_hi", "xg_lo",
            "hid_psum", "hid_act", "hi_ready", "lo_ready", "hid_used", "y_done", "y_out")}
        for k in ("raw1", "raw2", "b1", "b2", "xg", "y_kept"):
            R[k] = [sem(f"r_{k}{i}") for i in range(2)]
        gathered = [sem(f"gathered{g}") for g in range(NG)]

        def alone(eng):
            eng.sem_inc(waited[eng.engine], 1)

        def bank(i, lo, hi):
            return PS[:, i:i + 1, lo:hi]

        x_v = a["x"].rearrange("(g t p) d -> g p t d", p=P, t=G)
        out_v = a["out"].rearrange("(g t p) d -> g p t d", p=P, t=G)
        adj_v = a["adj"].rearrange("(t p) n -> p t n", p=P)
        adj_t_v = a["adj_t"].rearrange("(t p) n -> p t n", p=P)
        adj_t = a["adj_t"].rearrange("(j p) (b w) -> j p b w", p=P, w=GW)
        block = ctx.enter_context(nc.Block())

        @block.sync
        def _(sp):
            def weights(src, dst, slow=False):
                sp.dma_start(dst, src, allow_slow_non_contiguous=slow).then_inc(w_in, 16)

            def chunked(w):
                return w.rearrange("(k p) n -> p k n", p=P)

            def column(v):
                return v.rearrange("(k p o) -> p k o", p=P, o=1)

            def adj_stream(s):
                with sp.Fori(0, NG) as ib:
                    for j in range(T):
                        n = ib * T + j
                        sp.wait_ge(s["mask_done"], n + 1)
                        if s is GS[0]:
                            sp.wait_ge(s["alo_ready"], n + 1)
                        sp.dma_start(at[:, j % RING:j % RING + 1, :], adj_t[j][:, ds(ib, 1), :]).then_inc(s["at_in"][j % RING], 16)

            def masks(q):
                for m in range(2):
                    src = (adj_v, adj_t_v)[m]
                    for r in range(T // E):
                        t = q * (T // E) + r
                        n = (q * 2 + m) * (T // E) + r
                        for h in range(2):
                            w = slice(h * (N // 2), (h + 1) * (N // 2))
                            sp.dma_start(half[:, h:h + 1, :], src[:, ds(t, 1), w]).then_inc(half_in[h], 16)
                        for h in range(2):
                            w = slice(h * (N // 2), (h + 1) * (N // 2))
                            sp.wait_ge(half_done, n * 2 + h + 1)
                            alone(sp)
                            sp.dma_start(near_v[m].rearrange("t p n -> p t n")[:, ds(t, 1), w], half8[:, h:h + 1, :])\
                              .then_inc(half_kept[h], 16)

            def ffn_loads():
                s = FS[0]
                sp.wait_ge(proj_out, T)
                w1, w2 = a["L0_ffn_w1"], a["L0_ffn_w2"]
                sp.dma_start(w1_raw[:, :, :], w1[0].rearrange("(k p) n -> p k n", p=P)).then_inc(s["raw1_in"], 16)
                sp.dma_start(w2_raw[:, :, :], w2[0].rearrange("(c p) n -> p c n", p=P)).then_inc(s["raw2_in"], 16)
                sp.wait_ge(s["g_row_ready"], NG)
                with sp.Fori(0, E - 1) as q:
                    sp.wait_ge(s["split_done"], q * NG + NG)
                    alone(sp)
                    sp.dma_start(w1_raw[:, :, :].unsqueeze(1), w1.rearrange("e (k p) n -> p e k n", p=P)[:, ds(q + 1, 1)])\
                      .then_inc(s["raw1_in"], 16)
                    sp.dma_start(w2_raw[:, :, :].unsqueeze(1), w2.rearrange("e (c p) n -> p e c n", p=P)[:, ds(q + 1, 1)])\
                      .then_inc(s["raw2_in"], 16)
                    masks(q)
                masks(E - 1)

            for g in range(NG):
                sp.dma_start(X[:, g * G:(g + 1) * G, :], x_v[g]).then_inc(x_in[g], 16)
            weights(chunked(a["L0_gnn_W_gcnb"]), w_raw[:, :, 0:D])
            weights(column(a["L0_gnn_Wa"][0, 0:D]), w_raw[:, :, D:D + 1], slow=True)
            weights(column(a["L0_gnn_Wb"][0, 0:D]), w_raw[:, :, D + 1:D + 2], slow=True)
            weights(chunked(a["L0_gnn_W_sa"]), h_raw[:, :, 0:D])
            weights(column(a["L0_gnn_Wa"][0, D:2 * D]), h_raw[:, :, D + 2:D + 3], slow=True)
            weights(column(a["L0_gnn_Wb"][0, D:2 * D]), h_raw[:, :, D + 3:D + 4], slow=True)
            weights(a["L0_gnn_a_sa"][0, :].partition_broadcast(P), vec_row[:, :])
            weights(a["L0_gnn_b_gcnb"].partition_broadcast(P), bias_row[:, :])
            weights(a["L0_gnn_ba"].partition_broadcast(P), gate_bias[:, 0:1])
            weights(a["L0_gnn_bb"].partition_broadcast(P), gate_bias[:, 1:2])
            sp.dma_start(b1_cols[:, :, :], a["L0_ffn_b1_p"]).then_inc(FS[0]["aux_in"], 16)
            sp.dma_start(b2_cols[:, :, :], a["L0_ffn_b2_p"]).then_inc(FS[0]["aux_in"], 16)
            sp.wait_ge(FS[0]["tree_in"], 1)
            sp.dma_start(rb_col[0:E - 1, :], a["L0_ffn_rb"].rearrange("(e o) -> e o", o=1), allow_slow_non_contiguous=True)\
              .then_inc(FS[0]["aux_in"], 16)
            sp.dma_start(gw_raw[:, :, 0:E - 1], chunked(a["L0_ffn_rw_t"])).then_inc(FS[0]["aux_in"], 16)
            adj_stream(GS[0])
            ffn_loads()
            sp.wait_ge(FS[0]["acc_done"], E * NG + 2)
            weights(chunked(a["L1_gnn_fc_w"]), w_raw[:, :, 0:D])
            weights(chunked(a["L1_gnn_W"][0:D, :]), h_raw[:, :, 0:D])
            weights(a["L1_gnn_a_w"].partition_broadcast(P), vec_row[:, 0:D])
            weights(a["L1_gnn_fc_b"].partition_broadcast(P), bias_row[:, :])
            weights(a["L1_gnn_a_b"].partition_broadcast(P), gate_bias[:, 0:1])
            sp.wait_ge(h_free, 1)
            weights(chunked(a["L1_gnn_W"][D:2 * D, :]), h_raw[:, :, 0:D])
            for h in range(2):
                sp.wait_ge(half_kept[h], 16 * (2 * T + 1))
            for h in range(2):
                w = slice(h * (T // 2), (h + 1) * (T // 2))
                sp.dma_start(near[:, w, :], near_v[0].rearrange("t p n -> p t n")[:, w]).then_inc(near_in[h], 16)
            sp.wait_ge(R["gw_room"], 1)
            sp.dma_start(gw1_raw[:, :, 0:E], chunked(a["L1_ffn_gate_w"])).then_inc(R["gw_in"], 16)
            near_t_v = near_v[1].rearrange("t p (b w) -> p t b w", w=GW)
            s = GS[1]
            with sp.Fori(0, NG) as ib:
                for h in range(2):
                    sp.wait_ge(s["mask_done"], ib * T + h * (T // 2) + 1)
                    alone(sp)
                    sp.dma_start(near_t[:, h, :, :].unsqueeze(2), near_t_v[:, h * (T // 2):(h + 1) * (T // 2), ds(ib, 1), :])\
                      .then_inc(s["at_in"][h], 16)
            sp.wait_ge(x_done, 3 * T)
            for g in range(NG):
                sp.wait_ge(xn_ready, 3 * T + (g + 1) * G)
                sp.dma_start(xn_rows.rearrange("(t p) d -> p t d", p=P)[:, g * G:(g + 1) * G, :], xn_all[:, g * G:(g + 1) * G, :])\
                  .then_inc(R["rows_kept"], 16)
            sp.wait_ge(R["routed"], 1)
            w1, w2 = a["L1_ffn_w1"], a["L1_ffn_w2"]

            def raw_loads(i, z):
                e = sp.value_load(tile_u[0:1, ds(i, 1)], min_val=0, max_val=E - 1)
                sp.wait_ge(R["w1_split"], i * G + G)
                sp.dma_start(w1r_raw[:, z:z + 1, :, :],
                             w1.rearrange("e (k p) n -> p e k n", p=P)[:, ds(e, 1)]).then_inc(R["raw1"][z], 16)
                sp.wait_ge(R["w2_split"], i * G + G)
                sp.dma_start(w2r_raw[:, z:z + 1, :, :],
                             w2.rearrange("e (c p) n -> p e c n", p=P)[:, ds(e, 1)]).then_inc(R["raw2"][z], 16)

            def bias_loads(i, z):
                e = sp.value_load(tile_u[0:1, ds(i, 1)], min_val=0, max_val=E - 1)
                sp.wait_ge(R["y_out"], i + 1)
                sp.dma_start(b1_t[:, z:z + 1, :], a["L1_ffn_b1_p"][:, ds(e, 1), :]).then_inc(R["b1"][z], 16)
                sp.dma_start(b2_t[:, z, :], a["L1_ffn_b2"][ds(e, 1), :].rearrange("e d -> (e d)").partition_broadcast(P))\
                  .then_inc(R["b2"][z], 16)

            bias_loads(0, 0)
            bias_loads(1, 1)
            for i in range(3):
                raw_loads(i, i % 2)
            with sp.Fori(0, (NT - 3) // 2) as q:
                for i, z in ((q * 2 + 1, 1), (q * 2 + 2, 0)):
                    raw_loads(i + 2, z)
                    bias_loads(i + 1, 1 - z)
            bias_loads(NT - 1, (NT - 1) % 2)

            for z in range(2):
                sp.wait_ge(R["y_kept"][z], 32 * ((NT + 1 - z) // 2))
            yn_v = yn_rows[0:2 * N].rearrange("(k t p) d -> k p t d", k=2, p=P)
            for g in range(NG):
                for k, y in enumerate((y1, y2)):
                    sp.dma_start(y[:, g * G:(g + 1) * G, :], yn_v[k][:, g * G:(g + 1) * G, :]).then_inc(gathered[g], 16)

            for g in range(NG):
                sp.wait_ge(x_done, 3 * T + (g + 1) * G)
                sp.dma_start(out_v[g], X[:, g * G:(g + 1) * G, :]).then_inc(out_done, 16)
            sp.wait_ge(out_done, 16 * NG)

        @block.gpsimd
        def _(pool):
            seq = Count(pool, pool_seq)
            seq.link(pool.memset(ident[:, :], 0.0))
            pool.affine_select(out=ident[:, :], in_=ident[:, :], compare_op=ALU.not_equal, fill=1.0, base=0,
                               pattern=[[-1, P]], channel_multiplier=1).then_inc(const_ready, 1)
            pool.memset(ones[:, :], 1.0).then_inc(const_ready, 1)
            pool.memset(minus_half[:, :], -0.5).then_inc(const_ready, 1)
            pool.memset(zt[:, 0, 0:T], 1.0).then_inc(const_ready, 1)
            pool.memset(zt[:, 1, 0:T], 0.0).then_inc(const_ready, 1)

            def rstd(n, b, slot):
                pool.wait_ge(var_ready, n + 1)
                alone(pool)
                seq.link(pool.tensor_scalar(ln_v[:, :], ln_b[:, slot, :, 1], LN_EPS, None, ALU.add))
                seq.link(pool.tensor_tensor(ln_r[:, :], ln_v[:, :], minus_half[:, :], ALU.pow))
                seq.link(pool.tensor_tensor(ln_t[:, :], ln_r[:, :], ln_r[:, :], ALU.mult))
                seq.link(pool.tensor_tensor(ln_t[:, :], ln_t[:, :], ln_v[:, :], ALU.mult))
                alone(pool)
                seq.link(pool.tensor_scalar(ln_t[:, :], ln_t[:, :], -0.5, 1.5, ALU.mult, ALU.add))
                seq.link(pool.tensor_tensor(ln_rstd[:, ds(b * G, G)], ln_r[:, :], ln_t[:, :], ALU.mult))
                pool.tensor_copy(ln_mv[:, ds(b * G, G), :], ln_b[:, slot, :, :]).then_inc(rstd_ready, 1)

            pool.memset(gw_raw[:, :, :], 0.0).then_inc(pool_seq, 1)
            pool.memset(sel_f[:, :, :], 0.0).then_inc(pool_seq, 1)
            seq.n += 2
            seq.link(pool.memset(rb_col[:, :], 0.0))
            pool.sem_inc(FS[0]["tree_in"], 1)
            seq.link(pool.affine_select(out=sel_f[:, :, :], in_=sel_f[:, :, :], compare_op=ALU.not_equal,
                                        fill=1.0, base=0, pattern=[[-1, E], [0, P]], channel_multiplier=1))
            pool.affine_select(out=sel_f[:, :, :], in_=sel_f[:, :, :], compare_op=ALU.not_equal,
                               fill=1.0, base=-E, pattern=[[-1, E], [0, P]], channel_multiplier=1)\
                .then_inc(FS[0]["tree_in"], 1)
            for b in range(NG):
                rstd(b, b, b)

            def graph_steps(stage_no, step):
                for j in range(T):
                    step(j, j)
                with pool.Fori(0, NG - 1) as q:
                    end = seq.loop(q, 6)
                    for j in range(T):
                        step((q + 1) * T + j, j)
                    rstd(stage_no * NG + q, q, 0)
                    end(NG - 1)
                rstd(stage_no * NG + NG - 1, NG - 1, 1)

            def low_adjacency(n, j):
                s = GS[0]
                pool.wait_ge(s["ahi_ready"], n + 1)
                pool.wait_ge(s["step_done"], n + 1)
                pool.tensor_tensor(a_lo[:, j % RING, :], at[:, j % RING, :], a_hi[:, j % RING, :].bitcast(F32),
                                   ALU.subtract).then_inc(s["alo_ready"], 1)

            graph_steps(1, low_adjacency)
            pool.wait_ge(x_done, T)
            pool.memset(acc[:, :, :], 0.0).then_inc(FS[0]["zeroed"], 1)
            pool.memset(gate2[:, :, :], 0.0).then_inc(FS[0]["zeroed"], 1)
            with pool.Fori(0, 2 * T) as n:
                for h in range(2):
                    pool.wait_ge(half_in[h], n * 16 + 16)
                    pool.wait_ge(half_kept[h], n * 16 + 16)
                    alone(pool)
                    pool.tensor_scalar(half8[:, h, :], half[:, h, :], 0.0, None, ALU.is_gt).then_inc(half_done, 1)
            pool.wait_ge(FS[0]["acc_done"], E * NG + 2)
            pool.memset(gw1_raw[:, :, :], 0.0).then_inc(R["gw_room"], 1)
            for b in range(NG):
                rstd(2 * NG + b, b, b)

            def low_exponentials(n, j):
                s = GS[1]
                pool.wait_ge(s["ehi_ready"], n + 1)
                pool.wait_ge(s["step_done"], n + 1)
                pool.tensor_tensor(e_lo[:, j % RING, :], em[:, j % RING, :], e_hi[:, j % RING, :].bitcast(F32),
                                   ALU.subtract).then_inc(s["elo_ready"], 1)

            graph_steps(3, low_exponentials)
            pool.wait_ge(x_done, 3 * T)
            pool.iota(iota8[:, :, :], pattern=[[1, E]], base=0, channel_multiplier=0,
                      allow_small_or_imprecise_dtypes=True).then_inc(R["consts"], 1)
            pool.iota(iota_t[:, :], pattern=[[1, NT + 1]], base=0, channel_multiplier=0,
                      allow_small_or_imprecise_dtypes=True).then_inc(R["consts"], 1)
            pool.iota(node_k[:, :, :], pattern=[[N, 2], [P, T]], base=1, channel_multiplier=1,
                      allow_small_or_imprecise_dtypes=True).then_inc(R["consts"], 1)
            pool.iota(iota_p[:, :], pattern=[[1, P]], base=0, channel_multiplier=0,
                      allow_small_or_imprecise_dtypes=True).then_inc(R["consts"], 1)
            pool.iota(iota_row[:, :], pattern=[[P, HT + 1]], base=0, channel_multiplier=0,
                      allow_small_or_imprecise_dtypes=True).then_inc(R["consts"], 1)
            pool.iota(spare_row[:, :], pattern=[[P, HT]], base=2 * N + 1, channel_multiplier=1,
                      allow_small_or_imprecise_dtypes=True).then_inc(R["consts"], 1)
            pool.affine_select(out=before[:, :], in_=ones[:, :], compare_op=ALU.is_gt, fill=0.0, base=0,
                               pattern=[[1, P]], channel_multiplier=-1).then_inc(R["consts"], 1)
            rows_seq = Count(pool, R["pool_seq"])

            def gather(i, z):
                pool.wait_ge(R["xg_lo"], i + 1)
                rows_seq.link(pool.tensor_copy(pick[:, z, :], node_u[:, ds(i * 2, 2)]))
                alone(pool)
                for r in range(2):
                    pool.indirect_dma_start(xg[:, z, r, :], None, xn_rows,
                                            bass.IndirectOffsetOnAxis(ap=pick[:, z, r:r + 1], axis=0)).then_inc(R["xg"][z], 16)

            def scatter(i, z):
                pool.wait_ge(R["y_out"], i + 3)
                rows_seq.link(pool.tensor_copy(put[:, z, :], dest_u[:, ds(i * 2, 2)]))
                alone(pool)
                for r in range(2):
                    pool.indirect_dma_start(yn_rows, bass.IndirectOffsetOnAxis(ap=put[:, z, r:r + 1], axis=0),
                                            y_sb[:, z, r, :], None).then_inc(R["y_kept"][z], 16)

            def low_pieces(i, z, q):
                n = i * 2 * G + G + q + 1
                pool.wait_ge(R["w_hi"], n)
                pool.tensor_tensor(w2r_lo[:, z, 2 * q:2 * q + 2, :], w2r_raw[:, z, 2 * q:2 * q + 2, :],
                                   w2r_hi[:, z, 2 * q:2 * q + 2, :].bitcast(F32), ALU.subtract).then_inc(R["w2_split"], 1)

            pool.wait_ge(R["rows_kept"], 16 * NG)
            pool.wait_ge(R["placed"], 1)
            gather(0, 0)
            gather(1, 1)
            for q in range(G):
                low_pieces(0, 0, q)
            gather(2, 0)
            for q in range(G):
                low_pieces(1, 1, q)
            with pool.Fori(0, (NT - 3) // 2) as ii:
                end = rows_seq.loop(ii, 4)
                for i, z in ((ii * 2 + 1, 1), (ii * 2 + 2, 0)):
                    gather(i + 2, z)
                    scatter(i - 1, 1 - z)
                    for q in range(G):
                        low_pieces(i + 1, 1 - z, q)
                end((NT - 3) // 2)
            scatter(NT - 3, (NT - 3) % 2)
            for q in range(G):
                low_pieces(NT - 1, (NT - 1) % 2, q)
            scatter(NT - 2, (NT - 2) % 2)
            scatter(NT - 1, (NT - 1) % 2)

        @block.scalar
        def _(act):
            def high_x(stage_no, g, u, wide):
                act.wait_ge(xt_psum, g * G + u + 1 + stage_no * T)
                src = PS[:, u, 0:D].rearrange("p (k n) -> p k n", k=KD)
                dst = xt_hi[:, :, ds((g * G + u) * P, P)] if wide else xr_hi[:, u, :, :]
                alone(act)
                act.activation(dst, src, ACT.Copy).then_inc(xt_hi_ready, 1)

            def high_parts_and(stage_no, logits):
                for u in range(G):
                    high_x(stage_no, 0, u, True)
                with act.Fori(0, NG - 1) as g:
                    for u in range(G):
                        high_x(stage_no, g + 1, u, True)
                    logits(g)
                logits(NG - 1)

            def load_gelu(k):
                act.activation(warm[:, k:k + 1], ones[:, 0:1], ACT.Gelu)

            def project(stage_no, high):
                def group(g, first):
                    for u in range(G):
                        high_x(stage_no, g, u, False)
                        if not (first and u == 0):
                            high(g * G + u - 1, (u - 1) % 2)

                group(0, True)
                with act.Fori(0, NG - 1) as q:
                    group(q + 1, False)
                high(T - 1, 1)

            def rows_out(*jobs):
                for q in range(NG):
                    for k, row, factor in jobs:
                        act.wait_ge(row_psum[k], q + 1)
                        act.activation(row[:, q * GW:(q + 1) * GW], PS[:, (4 if k == 3 else 0) + q, :], ACT.Copy, scale=factor)\
                            .then_inc(row_copied[k], 1)

            def ffn():
                s = FS[0]
                def tanh(g):
                    act.wait_ge(s["lgt_psum"], g + 1)
                    act.activation(lg_t[:, :], PS[:, 4, :], ACT.Tanh, bias=rb_col[:, :], scale=0.5).then_inc(s["lgt_ready"], 1)

                act.wait_ge(x_done, T)
                act.wait_ge(s["raw1_in"], 16)
                act.wait_ge(s["raw2_in"], 16)
                for q in range(NG):
                    c1, c2 = slice(q * D, (q + 1) * D), slice(q * 2, q * 2 + 2)
                    act.activation(w1_hi[:, 0, :, c1], w1_raw[:, :, c1], ACT.Copy).then_inc(s["whi"], 1)
                    act.activation(w2_hi[:, 0, c2, :], w2_raw[:, c2, :], ACT.Copy).then_inc(s["whi"], 1)
                high_parts_and(1, tanh)
                for g in range(NG):
                    act.wait_ge(s["g2_psum"], g + 1)
                    act.activation(g_row[:, g * GW:(g + 1) * GW], PS[:, g, :], ACT.Copy).then_inc(s["g_row_ready"], 1)

                act.wait_ge(s["aux_in"], 16 * 4)
                load_gelu(0)
                with act.Fori(0, E) as e:
                    with act.Fori(0, 2) as gp:
                        for pg in range(2):
                            n = e * NG + gp * 2 + pg
                            for c in range(HC + 1):
                                act.wait_ge(s["hid_psum"], n * (HC + 1) + c + 1)
                                if c == 0:
                                    act.wait_ge(s["acc_done"], n + 1)
                                    act.activation(gate_b[:, pg, :], PS[:, 0, :], ACT.Copy).then_inc(s["hid_act"], 1)
                                else:
                                    act.wait_ge(s["lo_ready"], n * HC + c)
                                    alone(act)
                                    act.activation(hf[:, (c - 1) % 2, :], PS[:, c % 3, :], ACT.Gelu,
                                                   bias=b1_cols[:, ds(e, 1), c - 1], scale=1.0).then_inc(s["hid_act"], 1)

            act.wait_ge(const_ready, 5)
            act.activation(hh[:, :, D:D + 1].rearrange("p t o -> p (t o)"), zt[:, 0, 0:T], ACT.Copy).then_inc(act_seq, 1)
            act.activation(hh[:, :, D + 1:D + 2].rearrange("p t o -> p (t o)"), zt[:, 1, 0:T], ACT.Copy).then_inc(act_seq, 1)
            act.activation(hl[:, :, D:D + 1].rearrange("p t o -> p (t o)"), zt[:, 1, 0:T], ACT.Copy).then_inc(act_seq, 1)
            act.activation(hl[:, :, D + 1:D + 2].rearrange("p t o -> p (t o)"), zt[:, 1, 0:T], ACT.Copy).then_inc(act_seq, 1)
            act.activation(ones_r[:, :], ones[:, :], ACT.Copy).then_inc(act_seq, 1)
            def high_0(t, par):
                act.wait_ge(proj_done, t + 1)
                alone(act)
                act.activation(vh[:, ds(t, 1), :], bank(4 + par, 0, VW), ACT.Copy).then_inc(proj_hi, 1)
                act.activation(hh[:, ds(t, 1), 0:D], bank(6 + par, 0, D), ACT.Copy).then_inc(proj_hi, 1)

            project(0, high_0)
            rows_out((0, row_a, -1.0), (0, row_b, -LEAK0))

            def graph_steps(s, layer):
                def exponential(n, j):
                    act.wait_ge(s["arg_ready"], n + 1)
                    act.wait_ge(s["mask_done"], n + RING - 1)
                    act.activation(ex[:, j % 2, :], arg[:, j % 2, :], ACT.Exp, bias=cols2[:, j, 0:1], scale=1.0)\
                        .then_inc(s["exp_ready"], 1)

                def sums_out(b):
                    for it in range(G):
                        if layer == 0:
                            act.wait_ge(s["acc_e"], b * G + it + 1)
                        elif it < G - 1:
                            act.wait_ge(s["acc_e"], b * (G - 1) + it + 1)
                        else:
                            act.wait_ge(s["step_done"], b * T + T + RING)
                        act.wait_ge(s["fin"], b + 1)
                        act.activation(stage[:, it, 0, :], PS[:, it, 0:VW], ACT.Copy).then_inc(s["st_e"], 1)

                def gates(b, k):
                    act.wait_ge(s["z_ready"], b * 2 + k + 1)
                    if k == 0:
                        act.activation(small[:, 4:6, :], small[:, 2:4, :], ACT.Tanh, scale=0.5).then_inc(s["th_ready"], 1)
                    else:
                        act.activation(th[:, :, :], zt[:, :, :], ACT.Tanh, scale=0.5).then_inc(s["th_ready"], 1)

                def steps(ib, finish):
                    exponential(ib * T, 0)
                    for j in range(T):
                        n = ib * T + j
                        if j < T - 1:
                            exponential(n + 1, j + 1)
                        act.wait_ge(s["mask_done"], n + RING + 1)
                        act.wait_ge(s["step_done"], n + 1)
                        act.activation(e_hi[:, j % RING, :], em[:, j % RING, :], ACT.Copy).then_inc(s["ehi_ready"], 1)
                        if layer == 0:
                            act.wait_ge(s["at_in"][j % RING], (ib * (T // RING) + j // RING + 1) * 16)
                            act.activation(a_hi[:, j % RING, :], at[:, j % RING, :], ACT.Copy).then_inc(s["ahi_ready"], 1)
                        if finish and j == EVAC:
                            sums_out(ib - 1)
                        if finish and layer == 0 and j in GATES:
                            gates(ib - 1, GATES.index(j))

                steps(0, False)
                with act.Fori(0, NG - 1) as q:
                    steps(q + 1, True)
                sums_out(NG - 1)
                if layer == 0:
                    for k in range(2):
                        gates(NG - 1, k)

            act.wait_ge(wts_ready, 2)
            graph_steps(GS[0], 0)
            ffn()
            act.wait_ge(const_ready, 5)

            def high_1(t, par):
                act.wait_ge(proj_out, t + 1 + T)
                alone(act)
                act.activation(hh[:, ds(t, 1), 0:D], ff[:, par:par + 1, :], ACT.Copy).then_inc(proj_hi, 1)

            project(2, high_1)
            rows_out((1, s2_row, 1.0))
            rows_out((2, row_a, 1.0), (3, row_b, 1.0))
            graph_steps(GS[1], 1)
            def copy_logits(g):
                act.wait_ge(R["lgt_psum"], g + 1)
                act.activation(lg1_t[:, :], PS[:, 4, :], ACT.Copy).then_inc(R["lgt_ready"], 1)

            high_parts_and(3, copy_logits)
            act.wait_ge(R["gap_ready"], 1)
            act.activation(gate_e[:, 1, :], gate_e[:, 0, :], ACT.Exp).then_inc(R["gap_exp"], 1)

            def piece(i, z, c, uses):
                if c % G == 0:
                    act.wait_ge(R["raw1" if c == 0 else "raw2"][z], uses * 16)
                if c < G:
                    src, dst = w1r_raw[:, z, :, c * D:(c + 1) * D], w1r_hi[:, z, :, c * D:(c + 1) * D]
                else:
                    b = 2 * (c - G)
                    src, dst = w2r_raw[:, z, b:b + 2, :], w2r_hi[:, z, b:b + 2, :]
                act.activation(dst, src, ACT.Copy).then_inc(R["w_hi"], 1)

            def rows_high(i, z):
                act.wait_ge(R["xg_psum"], i + 1)
                act.activation(xg_hi[:, z, :, :], PS[:, 2, :].rearrange("p (k n) -> p k n", k=KD), ACT.Copy)\
                    .then_inc(R["xg_hi"], 1)

            def tile(i, z, uses, more):
                act.wait_ge(R["b1"][z], uses * 16)
                for p in range(G):
                    act.wait_ge(R["hid_psum"], i * G + p + 1)
                    act.wait_ge(R["lo_ready"], i * G + p + 1)
                    for h in range(2):
                        act.activation(hfr[:, p % 2, h * RT:(h + 1) * RT], PS[:, p % 2, h * RT:(h + 1) * RT], ACT.Gelu,
                                       bias=b1_t[:, z, 2 * p + h:2 * p + h + 1], scale=1.0).then_inc(R["hid_act"], 1)
                    if more:
                        if p == 2:
                            act.wait_ge(R["hid_used"], i * G + 2)
                        for h in range(2):
                            piece(i + 1, 1 - z, 2 * p + h, uses + z)
                        if p == 2:
                            rows_high(i + 1, 1 - z)

            load_gelu(1)
            for c in range(HC):
                piece(0, 0, c, 1)
            rows_high(0, 0)
            tile(0, 0, 1, True)
            with act.Fori(0, (NT - 3) // 2) as ii:
                tile(ii * 2 + 1, 1, ii + 1, True)
                tile(ii * 2 + 2, 0, ii + 2, True)
            tile(NT - 2, (NT - 2) % 2, NT // 2, True)
            tile(NT - 1, (NT - 1) % 2, (NT + 1) // 2, False)

        @block.tensor
        def _(pe):
            def three(out, l_hi, l_lo, r_hi, r_lo, start, stop, sem_of=None):
                pe.matmul(out, l_hi, r_hi, start=start, stop=False)
                pe.matmul(out, l_hi, r_lo, start=False, stop=False)
                m = pe.matmul(out, l_lo, r_hi, start=False, stop=stop)
                if sem_of is not None:
                    m.then_inc(sem_of, 1)

            def transpose_x(stage_no, g, u):
                src = xn_all[:, g * G + u, :] if stage_no == 3 else xn[:, u, :]
                pe.wait_ge(xn_ready, g * G + u + 1 + stage_no * T)
                pe.transpose(PS[:, u, 0:P], src[:, 0:P], ident[:, :])
                pe.transpose(PS[:, u, P:D], src[:, P:D], ident[:, :]).then_inc(xt_psum, 1)

            def project(stage_no, products):
                def group(g, first, last):
                    for u in range(G):
                        if u < G - 1:
                            transpose_x(stage_no, g, u + 1)
                        elif not last:
                            transpose_x(stage_no, g + 1, 0)
                        pe.wait_ge(xt_lo_ready, g * G + u + 1 + stage_no * T)
                        if not (first and u < 2):
                            pe.wait_ge(proj_out, g * G + u - 1 + stage_no // 2 * T)
                        products(u)

                transpose_x(stage_no, 0, 0)
                group(0, True, False)
                with pe.Fori(0, NG - 2) as q:
                    group(q + 1, False, False)
                group(NG - 1, False, True)

            def logits(stage_no, hi, lo, lgt, s):
                def of_group(g):
                    pe.wait_ge(xt_lo_ready, (g + 1) * G + stage_no * T)
                    for k in range(KD):
                        three(PS[:, 4, :], hi[:, k, :], lo[:, k, :], xt_hi[:, k, ds(g * GW, GW)],
                              xt_lo[:, k, ds(g * GW, GW)], k == 0, k == KD - 1, s["lgt_psum"] if k == KD - 1 else None)
                    pe.wait_ge(s["lgt_ready"], g + 1)
                    pe.wait_ge(s["lg_copied"], g + 1)
                    for u in range(G):
                        m = pe.transpose(PS[:, 5, u * P:(u + 1) * P], lgt[:, u * P:(u + 1) * P], ident[:, :])
                    m.then_inc(s["lg_psum"], 1)

                for u in range(G):
                    transpose_x(stage_no, 0, u)
                for g in range(NG - 1):
                    for u in range(G):
                        pe.wait_ge(xt_lo_ready, g * G + u + 1 + stage_no * T)
                        transpose_x(stage_no, g + 1, u)
                    of_group(g)
                of_group(NG - 1)

            def rows(ks):
                for q in range(NG):
                    for k in ks:
                        pe.wait_ge(diag_ready[k], q + 1)
                        rhs = masked[:, q * GW:(q + 1) * GW] if k == 3 else em[:, q, :]
                        pe.matmul(PS[:, (4 if k == 3 else 0) + q, :], ones[:, :], rhs, start=True, stop=True)\
                            .then_inc(row_psum[k], 1)

            def graph_steps(s, layer):
                alone(pe)
                with pe.Fori(0, NG) as ib:
                    for j in range(T):
                        n = ib * T + j
                        pe.wait_ge(s["elo_ready"], n + 1 + RING)
                        for it in range(G):
                            if j == 0:
                                pe.wait_ge(s["st_e"], ib * G + it + 1)
                            w = slice(it * P, (it + 1) * P)
                            done = s["acc_e"] if j == T - 1 else None
                            if layer == 1 and it == G - 1:
                                done = s["step_done"]
                            three(PS[:, it, 0:VW], e_hi[:, j % RING, w], e_lo[:, j % RING, w],
                                  hh[:, j, :], hl[:, j, :], j == 0, j == T - 1, done)
                        if layer == 1:
                            continue
                        pe.wait_ge(s["alo_ready"], n + 1 + RING)
                        for it in range(G):
                            if j == 0:
                                pe.wait_ge(s["st_a"], ib * G + it + 1)
                            w = slice(it * P, (it + 1) * P)
                            done = s["acc_a"] if j == T - 1 and it < G - 1 else s["step_done"] if it == G - 1 else None
                            three(PS[:, 4 + it, 0:VW], a_hi[:, j % RING, w], a_lo[:, j % RING, w],
                                  vh[:, j, :], vl[:, j, :], j == 0, j == T - 1, done)

            def ffn():
                s = FS[0]
                pe.wait_ge(wts_ready, 3)
                logits(1, gw_hi, gw_lo, lg_t, s)
                for g in range(NG):
                    pe.wait_ge(s["gate2_ready"], 1)
                    for u in range(G):
                        m = pe.transpose(PS[:, g, u * P:(u + 1) * P], gate2[:, g * G + u, :], ident[:, :])
                    m.then_inc(s["g2_psum"], 1)
                pe.wait_ge(s["g_row_ready"], NG)

                def second(n, pg, c, par):
                    pe.wait_ge(s["lo_ready"], n * HC + c + 3)
                    if c == 0:
                        pe.wait_ge(s["y_free"], n + 1)
                    for d in range(KD):
                        w = slice(d * P, (d + 1) * P)
                        last = c == HC - 1
                        three(PS[:, 3 + 2 * pg + d, :], w2_hi[:, par, c, w], w2_lo[:, par, c, w],
                              hid_hi[:, c % RING, :], hid_lo[:, c % RING, :], c == 0, last,
                              s["hid_used"] if d == KD - 1 else s["y_done"] if last else None)

                alone(pe)
                with pe.Fori(0, E // 2) as ep:
                    for par in range(2):
                        e = ep * 2 + par
                        pe.wait_ge(s["split_done"], (e + 1) * NG)
                        alone(pe)
                        with pe.Fori(0, 2) as gp:
                            for pg in range(2):
                                n = e * NG + gp * 2 + pg
                                gcol = (gp * 2 + pg) * GW
                                for c in range(HC + 1):
                                    pe.wait_ge(s["hid_act"], n * (HC + 1) + c + 1)
                                    if c == 0:
                                        pe.matmul(PS[:, 0, :], sel[:, par, :], g_row[:, ds(gcol, GW)],
                                                  start=True, stop=True).then_inc(s["hid_psum"], 1)
                                        continue
                                    w = slice((c - 1) * P, c * P)
                                    for k in range(KD):
                                        three(PS[:, c % 3, :], w1_hi[:, par, k, w], w1_lo[:, par, k, w],
                                              xt_hi[:, k, ds(gcol, GW)], xt_lo[:, k, ds(gcol, GW)], k == 0, k == KD - 1,
                                              s["hid_psum"] if k == KD - 1 else None)
                                    if c >= 3:
                                        second(n, pg, c - 3, par)
                                second(n, pg, HC - 2, par)
                                second(n, pg, HC - 1, par)
                for t in range(T):
                    pe.wait_ge(s["acc_done"], E * NG + 2)
                    if t >= G:
                        pe.wait_ge(s["back_done"], t - G + 1)
                    for d in range(KD):
                        m = pe.transpose(PS[:, t % G, d * P:(d + 1) * P], acc[:, d, t * P:(t + 1) * P], ident[:, :])
                    m.then_inc(s["back_psum"], 1)

            pe.wait_ge(const_ready, 5)
            pe.wait_ge(wts_ready, 1)

            def products_0(u):
                for k in range(KD):
                    three(PS[:, 4 + u % 2, 0:VW], xr_hi[:, u, k, :], xr_lo[:, u, k, :], w_hi[:, k, :], w_lo[:, k, :],
                          k == 0, k == KD - 1)
                for k in range(KD):
                    three(PS[:, 6 + u % 2, 0:PW], xr_hi[:, u, k, :], xr_lo[:, u, k, :], h_hi[:, k, :], h_lo[:, k, :],
                          k == 0, k == KD - 1, proj_done if k == KD - 1 else None)

            project(0, products_0)
            rows((0,))
            graph_steps(GS[0], 0)
            ffn()
            pe.wait_ge(wts_ready, 4)

            def products_1(u):
                for k in range(KD):
                    three(PS[:, 4 + u % 2, 0:VW], xr_hi[:, u, k, :], xr_lo[:, u, k, :], w_hi[:, k, :], w_lo[:, k, :],
                          k == 0, k == KD - 1, proj_done if k == KD - 1 else None)

            project(2, products_1)
            pe.wait_ge(wts_ready, 5)
            rows((1,))
            for j in range(T):
                pe.matmul(PS[:, 6, 0:D], ones_r[:, :], hh[:, j, 0:D], start=j == 0, stop=False)
                m = pe.matmul(PS[:, 6, 0:D], ones_r[:, :], hl[:, j, 0:D], start=False, stop=j == T - 1)
            m.then_inc(mean_psum, 1)
            rows((2, 3))
            graph_steps(GS[1], 1)
            pe.wait_ge(wts_ready, 6)
            logits(3, gw1_hi, gw1_lo, lg1_t, R)
            pe.wait_ge(R["hot_ready"], 1)
            hot_rows = hot[:, 2, :, :].rearrange("p t e -> p (t e)")
            pe.matmul(PS[:, 6, 0:T * E], before[:, :], hot_rows, start=True, stop=True)
            pe.matmul(PS[:, 7, 0:T * E], ones[:, :], hot_rows, start=True, stop=True).then_inc(R["count_psum"], 1)

            for k in range(2):
                for t in range(T):
                    pe.wait_ge(R["row_hot"], k * T + t + 1)
                    m = pe.matmul(PS[:, 5, 0:HT + 1], at_lo[:, k, t, :], up_to[:, k, t, :], start=k + t == 0,
                                  stop=k * T + t == 2 * T - 1)
            m.then_inc(R["inverse_psum"], 1)

            def rows_in(i, z, uses):
                pe.wait_ge(R["xg"][z], uses * 32)
                for k in range(KD):
                    for r in range(2):
                        m = pe.transpose(PS[:, 2, (2 * k + r) * P:(2 * k + r + 1) * P], xg[:, z, r, k * P:(k + 1) * P],
                                         ident[:, :])
                m.then_inc(R["xg_psum"], 1)

            def first(i, z, p):
                pe.wait_ge(R["w1_split"], i * G + p + 1 + 2 * G)
                pe.wait_ge(R["hid_act"], i * HC + 2 * p + 2)
                for h in range(2):
                    c = 2 * p + h
                    for k in range(KD):
                        three(PS[:, p % 2, h * RT:(h + 1) * RT], w1r_hi[:, z, k, c * P:(c + 1) * P],
                              w1r_lo[:, z, k, c * P:(c + 1) * P], xg_hi[:, z, k, :], xg_lo[:, z, k, :],
                              k == 0, k == KD - 1, R["hid_psum"] if h == 1 and k == KD - 1 else None)

            def second(i, z, p):
                pe.wait_ge(R["lo_ready"], i * G + p + 3)
                pe.wait_ge(R["w2_split"], i * G + p + 1 + 2 * G)
                if p == 0:
                    pe.wait_ge(R["y_out"], i + 1)
                for h in range(2):
                    c = 2 * p + h
                    for r in range(2):
                        w = slice(h * RT + r * P, h * RT + (r + 1) * P)
                        last = c == HC - 1
                        three(PS[:, 4 + 2 * z + r, 0:D], hr_hi[:, p % 2, w], hr_lo[:, p % 2, w],
                              w2r_hi[:, z, c, :], w2r_lo[:, z, c, :], c == 0, last,
                              R["hid_used"] if h == 1 and r == 1 else R["y_done"] if last else None)

            def tile(i, z, uses, more):
                pe.wait_ge(R["xg_lo"], i + 3)
                for p in range(G):
                    first(i, z, p)
                    if p > 0:
                        second(i, z, p - 1)
                    elif isinstance(i, int) and i == 0:
                        continue
                    else:
                        second(i - 1, 1 - z, G - 1)
                    if p == 1 and more:
                        rows_in(i + 1, 1 - z, uses + z)

            rows_in(0, 0, 1)
            tile(0, 0, 1, True)
            with pe.Fori(0, (NT - 3) // 2) as ii:
                tile(ii * 2 + 1, 1, ii + 1, True)
                tile(ii * 2 + 2, 0, ii + 2, True)
            tile(NT - 2, (NT - 2) % 2, NT // 2, True)
            tile(NT - 1, (NT - 1) % 2, (NT + 1) // 2, False)
            second(NT - 1, (NT - 1) % 2, G - 1)

        @block.vector
        def _(dve):
            seq = Count(dve, dve_seq)
            V = nc.vector

            for s in GS:
                dve.sem_inc(s["exp_ready"], 2)
                dve.sem_inc(s["elo_ready"], RING)
                dve.sem_inc(s["mask_done"], RING)
                dve.sem_inc(s["step_done"], RING)
                dve.sem_inc(s["st_e"], G)
                dve.sem_inc(s["fin"], 1)
            dve.sem_inc(GS[0]["alo_ready"], RING)
            dve.sem_inc(GS[0]["st_a"], G)
            for s in FS:
                dve.sem_inc(s["hid_act"], 3)
                dve.sem_inc(s["lo_ready"], 2)
                dve.sem_inc(s["hid_used"], RING)
                dve.sem_inc(s["y_free"], 2)
                dve.sem_inc(s["acc_done"], 2)
            dve.sem_inc(R["w1_split"], 2 * G)
            dve.sem_inc(R["w2_split"], 2 * G)
            dve.sem_inc(FS[0]["lg_copied"], 1)
            dve.sem_inc(R["lg_copied"], 1)
            dve.sem_inc(low_done, 2)
            dve.sem_inc(R["hid_act"], 4)
            dve.sem_inc(R["lo_ready"], 2)
            dve.sem_inc(R["hid_used"], 2)
            dve.sem_inc(R["xg_lo"], 2)
            dve.sem_inc(R["y_out"], 2)
            for h in range(2):
                dve.sem_inc(half_kept[h], 16)

            def row_moments(b, it):
                V.bn_stats(ln_stat[:, it, :], X[:, ds(b * G + it, 1), :].rearrange("p t d -> p (t d)")).then_inc(dve_seq, 1)
                seq.n = seq.n + 1

            def block_moments(stage_no, b, slot):
                dve.wait_ge(dve_seq, seq.n)
                if stage_no > 0:
                    dve.wait_ge(rstd_ready, stage_no * NG + (0 if isinstance(b, int) else b))
                alone(dve)
                for it in range(G):
                    m = V.bn_aggr(ln_b[:, slot, it, :], ln_stat[:, it, :])
                    m.then_inc(*((var_ready, 1) if it == G - 1 else (dve_seq, 1)))
                seq.n = seq.n + G - 1
                dve.wait_ge(dve_seq, seq.n)
                dve.wait_ge(var_ready, stage_no * NG + b + 1)

            def row_stats(stage_no, b, slot):
                for it in range(G):
                    row_moments(b, it)
                block_moments(stage_no, b, slot)

            def normalise(stage_no, g, u):
                t = g * G + u
                dst = xn_all[:, ds(t, 1), :] if stage_no == 3 else xn[:, u:u + 1, :]
                V.tensor_scalar(dst, X[:, ds(t, 1), :], ln_mv[:, ds(t, 1), 0], ln_rstd[:, ds(t, 1)],
                                ALU.subtract, ALU.mult).then_inc(xn_ready, 1)

            def low_x(stage_no, g, u, wide):
                dve.wait_ge(xt_hi_ready, g * G + u + 1 + stage_no * T)
                src = PS[:, u, 0:D].rearrange("p (k n) -> p k n", k=KD)
                tok = ds((g * G + u) * P, P)
                hi = xt_hi[:, :, tok] if wide else xr_hi[:, u, :, :]
                lo = xt_lo[:, :, tok] if wide else xr_lo[:, u, :, :]
                V.tensor_tensor(lo, src, hi.bitcast(F32), ALU.subtract).then_inc(xt_lo_ready, 1)

            def project(stage_no, out):
                def group(g, first, last):
                    for u in range(G):
                        low_x(stage_no, g, u, False)
                        if not last:
                            normalise(stage_no, g + 1, u)
                        if not (first and u == 0):
                            out(g * G + u - 1, (u - 1) % 2, first and u == 1)

                dve.wait_ge(rstd_ready, stage_no * NG + 1)
                for u in range(G):
                    normalise(stage_no, 0, u)
                for g in range(NG):
                    dve.wait_ge(rstd_ready, stage_no * NG + min(g + 2, NG))
                    group(g, g == 0, g == NG - 1)
                out(T - 1, 1, False)

            def logits(stage_no, dst, s, also=lambda g: None):
                def read(g):
                    dve.wait_ge(s["lg_psum"], g + 1)
                    V.tensor_copy(dst[:, ds(g * G, G), :], PS[:, 5, :].rearrange("p (u n) -> p u n", u=G)[:, :, 0:E])\
                        .then_inc(s["lg_copied"], 1)

                dve.wait_ge(rstd_ready, stage_no * NG + 1)
                for u in range(G):
                    normalise(stage_no, 0, u)
                for g in range(NG):
                    dve.wait_ge(rstd_ready, stage_no * NG + min(g + 2, NG))
                    for u in range(G):
                        low_x(stage_no, g, u, True)
                        if g < NG - 1:
                            normalise(stage_no, g + 1, u)
                    if g > 0:
                        read(g - 1)
                    also(g)
                read(NG - 1)
                dve.wait_ge(s["lg_copied"], NG + 1)

            def split(raw, hi, lo):
                seq.link(V.tensor_copy(hi, raw))
                seq.link(V.tensor_tensor(lo, raw, hi.bitcast(F32), ALU.subtract))

            def diagonals(*jobs):
                for q in range(NG):
                    for k, col in jobs:
                        dst = masked[:, q * GW:(q + 1) * GW] if k == 3 else em[:, q, :]
                        V.tensor_tensor(dst.rearrange("p (t c) -> p t c", c=P), ident[:, :].unsqueeze(1).to_broadcast([P, G, P]),
                                        col[:, q * G:(q + 1) * G, :].to_broadcast([P, G, P]), ALU.mult)\
                            .then_inc(diag_ready[k], 1)

            def product_column(dst, w, row):
                seq.link(V.tensor_tensor_reduce(scratch[:, :], w, row, 1.0, 0.0, ALU.mult, ALU.add, dst))

            for g in range(NG):
                dve.wait_ge(x_in[g], 16)
                row_stats(0, g, g)
            dve.wait_ge(const_ready, 5)
            dve.wait_ge(w_in, 160)
            for k in range(KD):
                product_column(h_raw[:, k, D:D + 1], h_raw[:, k, 0:D], vec_row[:, 0:D])
                product_column(h_raw[:, k, D + 1:D + 2], h_raw[:, k, 0:D], vec_row[:, D:2 * D])
            split(w_raw[:, :, :], w_hi[:, :, :], w_lo[:, :, :])
            seq.link(V.tensor_copy(h_hi[:, :, :], h_raw[:, :, :]))
            V.tensor_tensor(h_lo[:, :, :], h_raw[:, :, :], h_hi[:, :, :].bitcast(F32), ALU.subtract).then_inc(wts_ready, 1)

            def out_0(t, par, first):
                dve.wait_ge(proj_hi, t * 2 + 2)
                V.tensor_tensor(vl[:, ds(t, 1), :], bank(4 + par, 0, VW), vh[:, ds(t, 1), :].bitcast(F32), ALU.subtract)
                V.tensor_tensor(hl[:, ds(t, 1), 0:D], bank(6 + par, 0, D), hh[:, ds(t, 1), 0:D].bitcast(F32), ALU.subtract)
                V.tensor_copy(cols[:, ds(t, 1), :], bank(6 + par, D, D + 4)).then_inc(proj_out, 1)

            project(0, out_0)
            dve.wait_ge(proj_out, T)
            seq.link(V.tensor_scalar(cols2[:, :, 0], cols[:, :, 1], -1.0, None, ALU.mult))
            V.tensor_scalar(cols2[:, :, 1], cols[:, :, 1], 1.0 - LEAK0, None, ALU.mult).then_inc(wts_ready, 1)
            for k in range(2):
                seq.link(V.tensor_scalar(cols2[:, :, 2 + k], cols[:, :, 2 + k], gate_bias[:, k:k + 1], None, ALU.add))
            diagonals((0, cols[:, :, 0:1]))
            dve.wait_ge(row_copied[0], 2 * NG)
            s = GS[0]
            def graph_steps(s, layer, finish_piece, sums_out, links):
                def exponents(ib, j):
                    dve.wait_ge(s["exp_ready"], ib * T + j + 1)
                    V.scalar_tensor_tensor(out=arg[:, j % 2, :], in0=row_b[:, ds(ib * GW, GW)], scalar=cols2[:, j, 1:2],
                                           in1=row_a[:, ds(ib * GW, GW)], op0=ALU.add,
                                           op1=ALU.min if layer == 0 else ALU.max).then_inc(s["arg_ready"], 1)

                def low(ib, j):
                    dve.wait_ge(s["ehi_ready"], ib * T + j + 1)
                    dve.wait_ge(s["step_done"], ib * T + j + 1)
                    V.tensor_tensor(e_lo[:, j % RING, :], em[:, j % RING, :], e_hi[:, j % RING, :].bitcast(F32), ALU.subtract)\
                        .then_inc(s["elo_ready"], 1)

                def steps(ib, finish):
                    exponents(ib, 0)
                    exponents(ib, 1)
                    for j in range(T):
                        n = ib * T + j
                        dve.wait_ge(s["exp_ready"], n + 3)
                        dve.wait_ge(s["elo_ready"], n + 1)
                        if layer == 0:
                            dve.wait_ge(s["at_in"][j % RING], (ib * (T // RING) + j // RING + 1) * 16)
                            mask, op0, op1 = at[:, j % RING, :], ALU.not_equal, ALU.mult
                        else:
                            dve.wait_ge(s["at_in"][j // (T // 2)], (ib + 1) * 16)
                            mask, op0, op1 = near_t[:, j // (T // 2), j % (T // 2), :], ALU.is_gt, ALU.min
                        V.scalar_tensor_tensor(out=em[:, j % RING, :], in0=mask, scalar=0.0, in1=ex[:, j % 2, :],
                                               op0=op0, op1=op1).then_inc(s["mask_done"], 1)
                        if j + 2 < T:
                            exponents(ib, j + 2)
                        if layer == 0 and j > 0:
                            low(ib, j - 1)
                        if finish and j == EVAC:
                            sums_out(ib - 1)
                        if finish and j > EVAC:
                            finish_piece(ib - 1, j)
                    if layer == 0:
                        low(ib, T - 1)

                steps(0, False)
                with dve.Fori(0, NG - 1) as q:
                    end = seq.loop(q, links)
                    steps(q + 1, True)
                    end(NG - 1)
                sums_out(NG - 1)
                before = seq.n
                for j in range(EVAC + 1, T):
                    finish_piece(NG - 1, j)
                assert seq.n - before == links, (seq.n - before, links)

            def sums_out_0(b):
                for it in range(G):
                    if it < G - 1:
                        dve.wait_ge(s["acc_a"], b * (G - 1) + it + 1)
                    else:
                        dve.wait_ge(s["step_done"], b * T + T + RING)
                    V.tensor_copy(stage[:, it, 1, :], PS[:, 4 + it, 0:VW]).then_inc(s["st_a"], 1)

            def finish_piece_0(b, j):
                xg = X[:, ds(b * G, G), :].rearrange("p t d -> p (t d)")
                if j == 3:
                    dve.wait_ge(s["st_a"], b * G + 2 * G)
                    dve.wait_ge(s["st_e"], b * G + 2 * G)
                    seq.link(V.tensor_scalar(small[:, 0, :], stage[:, :, 0, D], 1e-5, None, ALU.add))
                    seq.link(V.reciprocal(small[:, 1, :], small[:, 0, :]))
                    seq.link(V.tensor_tensor(small[:, 2, :], stage[:, :, 1, D], cols2[:, ds(b * G, G), 2], ALU.add))
                    V.tensor_tensor(small[:, 3, :], stage[:, :, 1, D + 1], cols2[:, ds(b * G, G), 3], ALU.add)\
                        .then_inc(s["z_ready"], 1)
                if j == 4:
                    for it in range(G):
                        V.tensor_tensor(stage[:, it, 1, 0:D], stage[:, it, 1, 0:D], bias_row[:, :], ALU.add).then_inc(dve_seq, 1)
                    seq.n = seq.n + G
                    dve.wait_ge(dve_seq, seq.n)
                if j == 6:
                    dve.wait_ge(s["th_ready"], b * 2 + 1)
                    seq.link(V.tensor_scalar(small[:, 6:8, :], small[:, 4:6, :], 0.5, 0.5, ALU.mult, ALU.add))
                    seq.link(V.tensor_tensor(small[:, 0, :], small[:, 6, :], small[:, 1, :], ALU.mult))
                if j == 7:
                    for it in range(G):
                        V.tensor_scalar(stage[:, it, 1, 0:D], stage[:, it, 1, 0:D], small[:, 7, it:it + 1], None, ALU.mult)\
                            .then_inc(dve_seq, 1)
                    seq.n = seq.n + G
                    dve.wait_ge(dve_seq, seq.n)
                if j == 8:
                    for it in range(G):
                        i1 = V.scalar_tensor_tensor(out=zt[:, it, :], in0=stage[:, it, 0, 0:D], scalar=small[:, 0, it:it + 1],
                                                    in1=stage[:, it, 1, 0:D], op0=ALU.mult, op1=ALU.add)
                    i1.then_inc(s["z_ready"], 1)
                if j == 11:
                    dve.wait_ge(s["th_ready"], b * 2 + 2)
                    V.scalar_tensor_tensor(out=xg, in0=th[:, :, :].rearrange("p t d -> p (t d)"), scalar=0.5,
                                           in1=xg, op0=ALU.mult, op1=ALU.add).then_inc(s["fin"], 1)
                if j == 12:
                    dve.wait_ge(s["fin"], b + 2)
                    seq.link(V.tensor_scalar(xg, xg, 0.5, None, ALU.add))
                    dve.sem_inc(x_done, G)
                if j in (13, 14):
                    for it in range((j - 13) * 2, (j - 13) * 2 + 2):
                        row_moments(b, it)
                if j == 15:
                    block_moments(1, b, int(isinstance(b, int)))

            graph_steps(s, 0, finish_piece_0, sums_out_0, 3 + G + 2 + G + 1 + 2 * G - 1)

            def ffn():
                s = FS[0]
                dve.wait_ge(s["aux_in"], 16 * 4)
                dve.wait_ge(s["tree_in"], 2)
                split(gw_raw[:, :, :], gw_hi[:, :, :], gw_lo[:, :, :])
                seq.link(V.tensor_scalar(rb_col[:, :], rb_col[:, :], 0.5, None, ALU.mult))
                V.tensor_copy(sel[:, 0, :], sel_f[:, 0, :]).then_inc(wts_ready, 1)

                def low_quarter(q, par):
                    c1 = ds(q * D, D)
                    c2 = ds(q * 2, 2)
                    V.tensor_tensor(w1_lo[:, par, :, c1], w1_raw[:, :, c1], w1_hi[:, par, :, c1].bitcast(F32), ALU.subtract)
                    V.tensor_tensor(w2_lo[:, par, c2, :], w2_raw[:, c2, :], w2_hi[:, par, c2, :].bitcast(F32), ALU.subtract)\
                        .then_inc(s["split_done"], 1)

                def low_after(g):
                    for q in range(2 * g - 2, 2 * g) if 0 < g < 3 else ():
                        dve.wait_ge(s["whi"], q * 2 + 2)
                        low_quarter(q, 0)

                logits(1, lg, s, low_after)
                seq.link(V.tensor_scalar(pq[:, 0, :, :], lg[:, :, :], 0.5, 0.5, ALU.mult, ALU.add))
                seq.link(V.tensor_scalar(pq[:, 1, :, :], lg[:, :, :], -0.5, 0.5, ALU.mult, ALU.add))
                p_, q_ = pq[:, 0], pq[:, 1]
                seq.link(V.tensor_copy(tree[:, 0, :, 0:1], q_[:, :, 0:1]))
                seq.link(V.tensor_copy(tree[:, 0, :, 1:2], p_[:, :, 0:1]))
                seq.link(V.tensor_tensor(tree[:, 1, :, 0:4:2], tree[:, 0, :, 0:2], q_[:, :, 1:3], ALU.mult))
                seq.link(V.tensor_tensor(tree[:, 1, :, 1:4:2], tree[:, 0, :, 0:2], p_[:, :, 1:3], ALU.mult))
                seq.link(V.tensor_tensor(gate[:, :, 0:8:2], tree[:, 1, :, 0:4], q_[:, :, 3:7], ALU.mult))
                seq.link(V.tensor_tensor(gate[:, :, 1:8:2], tree[:, 1, :, 0:4], p_[:, :, 3:7], ALU.mult))
                seq.link(V.tensor_copy(gate_hi[:, :, :], gate[:, :, :]))
                dve.wait_ge(s["zeroed"], 2)
                V.tensor_copy(gate2[:, :, 0:E], gate_hi[:, :, :].bitcast(F32))
                V.tensor_tensor(gate2[:, :, E:2 * E], gate[:, :, :], gate_hi[:, :, :].bitcast(F32), ALU.subtract)\
                    .then_inc(s["gate2_ready"], 1)

                def split_quarter(e_next, q, par):
                    c1 = ds(q * D, D)
                    c2 = ds(q * 2, 2)
                    n = e_next * (2 * NG) + q * 2
                    V.tensor_copy(w1_hi[:, par, :, c1], w1_raw[:, :, c1]).then_inc(s["whi"], 1)
                    V.tensor_copy(w2_hi[:, par, c2, :], w2_raw[:, c2, :]).then_inc(s["whi"], 1)
                    V.tensor_copy(sel[:, par:par + 1, :], sel_f[:, ds(e_next, 1), :])
                    dve.wait_ge(s["whi"], n + 2)
                    low_quarter(q, par)

                def pair(ep, last):
                    for par in range(2):
                        e = ep * 2 + par
                        more = not (last and par == 1)
                        alone(dve)
                        with dve.Fori(0, 2) as gp:
                            for pg in range(2):
                                g = gp * 2 + pg
                                n = e * NG + g
                                for c in range(HC):
                                    m = n * HC + c
                                    dve.wait_ge(s["hid_act"], n * (HC + 1) + c + 2 + 3)
                                    dve.wait_ge(s["hid_used"], m + 1)
                                    V.tensor_copy(hid_hi[:, c % RING, :], hf[:, c % 2, :]).then_inc(s["hi_ready"], 1)
                                    dve.wait_ge(s["hi_ready"], m + 1)
                                    V.tensor_tensor(hid_lo[:, c % RING, :], hf[:, c % 2, :],
                                                    hid_hi[:, c % RING, :].bitcast(F32), ALU.subtract).then_inc(s["lo_ready"], 1)
                                    if c == RING and more:
                                        dve.wait_ge(s["raw1_in"], (e + 2) * 16)
                                        dve.wait_ge(s["raw2_in"], (e + 2) * 16)
                                        alone(dve)
                                        split_quarter(e + 1, g, 1 - par)
                                for d in range(KD):
                                    dve.wait_ge(s["y_done"], n + 1)
                                    if d == KD - 1:
                                        dve.wait_ge(s["hid_used"], (n + 1) * HC + RING)
                                    i1 = V.scalar_tensor_tensor(out=yt[:, d, :], in0=PS[:, 3 + 2 * pg + d, :],
                                                                scalar=b2_cols[:, ds(e, 1), d], in1=gate_b[:, pg, :],
                                                                op0=ALU.add, op1=ALU.mult)
                                    i1.then_inc(s["y_tmp"], 1)
                                dve.wait_ge(s["y_tmp"], n * 2 + 2)
                                dve.sem_inc(s["y_free"], 1)
                                i1 = V.tensor_tensor(acc[:, :, ds(g * GW, GW)], acc[:, :, ds(g * GW, GW)], yt[:, :, :], ALU.add)
                                i1.then_inc(s["acc_done"], 1)

                alone(dve)
                with dve.Fori(0, E // 2 - 1) as ep:
                    pair(ep, False)
                pair(E // 2 - 1, True)
                for t in range(T):
                    dve.wait_ge(s["back_psum"], t + 1)
                    V.tensor_tensor(X[:, t, :], X[:, t, :], PS[:, t % G, 0:D], ALU.add).then_inc(s["back_done"], 1)
                    if t % G == G - 1:
                        dve.wait_ge(s["back_done"], t + 1)
                        dve.sem_inc(x_done, G)
                        row_stats(2, t // G, t // G)
                    if t == 3 * G - 1:
                        dve.wait_ge(w_in, 160 + 80)
                        for k in range(KD):
                            product_column(w_raw[:, k, D:D + 1], h_raw[:, k, 0:D], vec_row[:, 0:D])
                        dve.sem_inc(h_free, 1)

            ffn()
            dve.wait_ge(w_in, 160 + 96)
            for k in range(KD):
                product_column(w_raw[:, k, D + 1:D + 2], h_raw[:, k, 0:D], vec_row[:, 0:D])
            seq.link(V.tensor_copy(w_hi[:, :, :], w_raw[:, :, :]))
            V.tensor_tensor(w_lo[:, :, :], w_raw[:, :, :], w_hi[:, :, :].bitcast(F32), ALU.subtract).then_inc(wts_ready, 1)

            def low_1(t, par):
                dve.wait_ge(proj_hi, t + 1 + 2 * T)
                V.tensor_tensor(hl[:, ds(t, 1), 0:D], ff[:, par:par + 1, :], hh[:, ds(t, 1), 0:D].bitcast(F32), ALU.subtract)\
                    .then_inc(low_done, 1)

            def out_1(t, par, first):
                dve.wait_ge(proj_done, t + 1 + T)
                V.tensor_copy(cols[:, ds(t, 1), 0:2], bank(4 + par, D, D + 2))
                dve.wait_ge(low_done, t + 1)
                V.tensor_tensor(ff[:, par:par + 1, :], bank(4 + par, 0, D), bias_row[:, :].unsqueeze(1), ALU.add).then_inc(proj_out, 1)
                if not first:
                    low_1(t - 1, 1 - par)

            project(2, out_1)
            low_1(T - 1, 1)
            dve.wait_ge(proj_out, 2 * T)
            dve.wait_ge(low_done, T + 2)
            seq.link(V.tensor_scalar(cols2[:, :, 2], cols[:, :, 0], gate_bias[:, 0:1], None, ALU.add))
            seq.link(V.tensor_copy(cols2[:, :, 0], cols[:, :, 1]))
            V.tensor_scalar(cols2[:, :, 1], cols[:, :, 1], LEAK1 - 1.0, None, ALU.mult).then_inc(wts_ready, 1)
            diagonals((1, cols[:, :, 1:2]))
            seq.link(V.memset(scratch[:, 0:2 * T], 0.0))
            seq.link(V.memset(scratch[:, 0:T], 1.0))
            seq.link(V.tensor_copy(hh[:, :, D], scratch[:, 0:T]))
            seq.link(V.tensor_copy(hh[:, :, D + 1], scratch[:, T:2 * T]))
            seq.link(V.tensor_copy(hl[:, :, D], scratch[:, T:2 * T]))
            seq.link(V.tensor_copy(hl[:, :, D + 1], scratch[:, T:2 * T]))
            for q in range(NG):
                dve.wait_ge(row_copied[1], q + 1)
                V.tensor_reduce(s2_mins[:, q:q + 1], s2_row[:, q * GW:(q + 1) * GW], AX.X, ALU.min).then_inc(dve_seq, 1)
            seq.n += NG
            dve.wait_ge(dve_seq, seq.n)
            seq.link(V.tensor_reduce(s2_min[:, :], s2_mins[:, :], AX.X, ALU.min))
            seq.link(V.tensor_scalar(s2_row[:, :], s2_row[:, :], s2_min[:, :], 1.0, ALU.subtract, ALU.add))
            for t in range(T):
                dve.wait_ge(near_in[t // (T // 2)], 16)
                seq.link(V.tensor_tensor_reduce(masked[:, :], near[:, t, :], s2_row[:, :], 1.0, 0.0, ALU.mult, ALU.max,
                                                mx[:, 0, t:t + 1]))
            seq.link(V.tensor_scalar(mx[:, 1, :], mx[:, 0, :], 0.0, None, ALU.is_le))
            seq.link(V.tensor_scalar(mx[:, 2, :], mx[:, 0, :], s2_min[:, :], -1.0, ALU.add, ALU.add))
            seq.link(V.tensor_tensor(mx[:, 2, :], mx[:, 2, :], cols2[:, :, 2], ALU.add))
            seq.link(V.scalar_tensor_tensor(out=mx[:, 3, :], in0=mx[:, 2, :], scalar=LEAK1, in1=mx[:, 2, :],
                                            op0=ALU.mult, op1=ALU.max))
            seq.link(V.tensor_tensor(mx[:, 4, :], cols2[:, :, 2], mx[:, 3, :], ALU.subtract))
            seq.link(V.scalar_tensor_tensor(out=mx[:, 5, :], in0=cols2[:, :, 2], scalar=LEAK1, in1=mx[:, 3, :],
                                            op0=ALU.mult, op1=ALU.subtract))
            dve.wait_ge(mean_psum, 1)
            seq.link(V.tensor_scalar(mean_row[:, :], PS[:, 6, 0:D], 1.0 / N, None, ALU.mult))
            diagonals((2, mx[:, 4, :].unsqueeze(2)), (3, mx[:, 5, :].unsqueeze(2)))
            for t in range(T):
                V.scalar_tensor_tensor(out=X[:, t, :], in0=mean_row[:, :], scalar=mx[:, 1, t:t + 1], in1=X[:, t, :],
                                       op0=ALU.mult, op1=ALU.add).then_inc(dve_seq, 1)
            seq.n += T
            dve.wait_ge(dve_seq, seq.n)
            dve.wait_ge(R["gw_in"], 16)
            seq.link(V.tensor_copy(gw1_hi[:, :, :], gw1_raw[:, :, :]))
            V.tensor_tensor(gw1_lo[:, :, :], gw1_raw[:, :, :], gw1_hi[:, :, :].bitcast(F32), ALU.subtract).then_inc(wts_ready, 1)
            for k in (2, 3):
                dve.wait_ge(row_copied[k], NG)
            s = GS[1]

            def finish_piece_1(b, j):
                rows = [X[:, ds(b * G + it, 1), :] for it in range(G)]
                if j == 3:
                    dve.wait_ge(s["st_e"], b * G + 2 * G)
                    seq.link(V.tensor_tensor(small[:, 0, :], stage[:, :, 0, D], mx[:, 1, ds(b * G, G)], ALU.add))
                    seq.link(V.reciprocal(small[:, 1, :], small[:, 0, :]))
                if j in (4, 5):
                    for it in range((j - 4) * 2, (j - 4) * 2 + 2):
                        V.scalar_tensor_tensor(out=rows[it], in0=stage[:, it:it + 1, 0, 0:D], scalar=small[:, 1, it:it + 1],
                                               in1=rows[it], op0=ALU.mult, op1=ALU.add).then_inc(dve_seq, 1)
                    seq.n = seq.n + 2
                if j == 6:
                    dve.wait_ge(dve_seq, seq.n)
                    dve.sem_inc(s["fin"], 1)
                    dve.sem_inc(x_done, G)
                if 9 <= j < 9 + G:
                    row_moments(b, j - 9)
                if j == 9 + G:
                    block_moments(3, b, int(isinstance(b, int)))

            graph_steps(s, 1, finish_piece_1, lambda b: None, 2 + 4 + 2 * G - 1)
            logits(3, lga, R)
            dve.wait_ge(R["consts"], 7)
            for t in range(T):
                V.max(top[:, t, :], lga[:, t, :]).then_inc(dve_seq, 1)
            seq.n += T
            dve.wait_ge(dve_seq, seq.n)
            for t in range(T):
                V.max_index(topi[:, t, :], top[:, t, :], lga[:, t, :]).then_inc(dve_seq, 1)
            seq.n += T
            V.tensor_tensor(gate_e[:, 0, :], top[:, :, 1], top[:, :, 0], ALU.subtract).then_inc(R["gap_ready"], 1)
            dve.wait_ge(dve_seq, seq.n)
            seq.link(V.tensor_copy(topf[:, :, :], topi[:, :, 0:2]))
            for k in range(2):
                seq.link(V.tensor_tensor(hot[:, k, :, :], iota8[:, :, :].to_broadcast([P, T, E]),
                                         topf[:, :, k:k + 1].to_broadcast([P, T, E]), ALU.is_equal))
            V.tensor_tensor(hot[:, 2, :, :], hot[:, 0, :, :], hot[:, 1, :, :], ALU.add).then_inc(R["hot_ready"], 1)
            dve.wait_ge(R["gap_exp"], 1)
            seq.link(V.tensor_scalar(gate_e[:, 0, :], gate_e[:, 1, :], 1.0, None, ALU.add))
            seq.link(V.reciprocal(gate_e[:, 2, :], gate_e[:, 0, :]))
            seq.link(V.tensor_tensor(gate_e[:, 3, :], gate_e[:, 1, :], gate_e[:, 2, :], ALU.mult))
            def sums_up_to(buf, n):
                b, step = 0, 1
                while step < n:
                    V.tensor_copy(buf[:, 1 - b, 1:1 + step], buf[:, b, 1:1 + step]).then_inc(dve_seq, 1)
                    seq.n += 1
                    seq.link(V.tensor_tensor(buf[:, 1 - b, 1 + step:n + 1], buf[:, b, 1 + step:n + 1], buf[:, b, 1:n + 1 - step],
                                             ALU.add))
                    b, step = 1 - b, step * 2
                return b

            V.memset(counts[:, :, 0:1, :], 0.0).then_inc(dve_seq, 1)
            V.memset(ends[:, :, 0:1, :], 0.0).then_inc(dve_seq, 1)
            seq.n += 2
            dve.wait_ge(R["count_psum"], 1)
            seq.link(V.tensor_copy(counts[:, 0, 1:T + 1, :], PS[:, 7, 0:T * E].rearrange("p (t e) -> p t e", t=T)))
            count_t = counts[:, sums_up_to(counts, T)]
            seq.link(V.tensor_tensor(over[:, :, :], iota_row[:, 0:2 * N // RT:2].unsqueeze(1).to_broadcast([P, E, N // RT]),
                                     count_t[:, T, :].unsqueeze(2).to_broadcast([P, E, N // RT]), ALU.is_lt))
            seq.link(V.tensor_reduce(ends[:, 0, 1:E + 1, 0], over[:, :, :], AX.X, ALU.add))
            tile_end = ends[:, sums_up_to(ends, E)].rearrange("p e o -> p o e")
            seq.link(V.tensor_tensor(ended[:, :, :], iota_t[:, :].unsqueeze(2).to_broadcast([P, NT + 1, E]),
                                     tile_end[:, :, 1:E + 1].to_broadcast([P, NT + 1, E]), ALU.is_ge))
            seq.link(V.tensor_reduce(tile_e[:, :], ended[:, :, :], AX.X, ALU.add))
            seq.link(V.tensor_scalar(tile_e[:, :], tile_e[:, :], float(E - 1), None, ALU.min))
            V.tensor_copy(tile_u[:, :], tile_e[:, :]).then_inc(R["routed"], 1)
            seq.link(V.tensor_scalar(tiles_e[:, 0, :], tile_end[:, 0, 0:E], float(RT), None, ALU.mult))
            seq.link(V.tensor_tensor(slot[:, :, :], PS[:, 6, 0:T * E].rearrange("p (t e) -> p t e", t=T),
                                     count_t[:, 0:T, :], ALU.add))
            seq.link(V.tensor_tensor(slot[:, :, :], slot[:, :, :], tiles_e[:, :, :].to_broadcast([P, T, E]), ALU.add))
            for k in range(2):
                seq.link(V.tensor_tensor(slot_t[:, :, :], slot[:, :, :], hot[:, k, :, :], ALU.mult))
                seq.link(V.tensor_reduce(row_of[:, k, :], slot_t[:, :, :], AX.X, ALU.add))
            seq.link(V.tensor_scalar(row_hi[:, :, :], row_of[:, :, :], 1.0 / P, 0.5 / P - 0.5, ALU.mult, ALU.add))
            seq.link(V.tensor_scalar(row_hi[:, :, :], row_hi[:, :, :], ROUND, None, ALU.add))
            seq.link(V.tensor_scalar(row_hi[:, :, :], row_hi[:, :, :], ROUND, None, ALU.subtract))
            seq.link(V.scalar_tensor_tensor(out=row_lo[:, :, :], in0=row_hi[:, :, :], scalar=-float(P), in1=row_of[:, :, :],
                                            op0=ALU.mult, op1=ALU.add))
            for k in range(2):
                for t in range(T):
                    V.tensor_scalar(up_to[:, k, t, :], iota_row[:, :], row_of[:, k, t:t + 1], node_k[:, k, t:t + 1],
                                    ALU.is_le, ALU.mult)
                    V.tensor_scalar(at_lo[:, k, t, :], iota_p[:, :], row_lo[:, k, t:t + 1], None, ALU.is_equal)\
                        .then_inc(R["row_hot"], 1)
            dve.wait_ge(R["inverse_psum"], 1)
            seq.link(V.tensor_copy(place_f[:, 0, :], PS[:, 5, 0:HT + 1]))
            seq.link(V.tensor_tensor(place_f[:, 1, 0:HT], place_f[:, 0, 0:HT], place_f[:, 0, 1:HT + 1], ALU.subtract))
            v = place_f[:, 1, 0:HT]
            seq.link(V.tensor_scalar(place_f[:, 2, 0:HT], v, float(N), -float(N), ALU.is_gt, ALU.mult))
            seq.link(V.tensor_tensor(place_f[:, 2, 0:HT], place_f[:, 2, 0:HT], v, ALU.add))
            seq.link(V.tensor_scalar(place_f[:, 2, 0:HT], place_f[:, 2, 0:HT], -1.0, 0.0, ALU.add, ALU.max))
            seq.link(V.tensor_copy(node_u[:, :], place_f[:, 2, 0:HT]))
            seq.link(V.scalar_tensor_tensor(out=place_f[:, 3, 0:HT], in0=v, scalar=0.0, in1=spare_row[:, :],
                                            op0=ALU.is_equal, op1=ALU.mult))
            seq.link(V.scalar_tensor_tensor(out=place_f[:, 3, 0:HT], in0=v, scalar=-1.0, in1=place_f[:, 3, 0:HT],
                                            op0=ALU.add, op1=ALU.add))
            V.tensor_copy(dest_u[:, :], place_f[:, 3, 0:HT]).then_inc(R["placed"], 1)

            def w1_low(i, z, q):
                dve.wait_ge(R["w_hi"], i * 2 * G + q + 1)
                c = slice(q * D, (q + 1) * D)
                V.tensor_tensor(w1r_lo[:, z, :, c], w1r_raw[:, z, :, c], w1r_hi[:, z, :, c].bitcast(F32), ALU.subtract)\
                    .then_inc(R["w1_split"], 1)

            def rows_low(i, z):
                dve.wait_ge(R["xg_hi"], i + 1)
                V.tensor_tensor(xg_lo[:, z, :, :], PS[:, 2, :].rearrange("p (k n) -> p k n", k=KD),
                                xg_hi[:, z, :, :].bitcast(F32), ALU.subtract).then_inc(R["xg_lo"], 1)

            def sums_out(i, z, uses):
                dve.wait_ge(R["b2"][z], uses * 16)
                if not (isinstance(uses, int) and uses == 1):
                    dve.wait_ge(R["y_kept"][z], uses * 32 - 32)
                dve.wait_ge(R["y_done"], i + 1)
                dve.wait_ge(R["hid_used"], i * G + G + 2)
                for r in range(2):
                    m = V.tensor_tensor(y_sb[:, z, r, :], PS[:, 4 + 2 * z + r, 0:D], b2_t[:, z, :], ALU.add)
                m.then_inc(R["y_out"], 1)

            def tile(i, z, uses, more):
                for p in range(G):
                    m = i * G + p
                    dve.wait_ge(R["hid_act"], i * HC + 2 * p + 6)
                    dve.wait_ge(R["hid_used"], m + 1)
                    V.tensor_copy(hr_hi[:, p % 2, :], hfr[:, p % 2, :]).then_inc(R["hi_ready"], 1)
                    dve.wait_ge(R["hi_ready"], m + 1)
                    V.tensor_tensor(hr_lo[:, p % 2, :], hfr[:, p % 2, :], hr_hi[:, p % 2, :].bitcast(F32),
                                    ALU.subtract).then_inc(R["lo_ready"], 1)
                    if p == 0 and not (isinstance(i, int) and i == 0):
                        sums_out(i - 1, 1 - z, uses + z - 1)
                    if more:
                        w1_low(i + 1, 1 - z, p)
                        if p == 2:
                            rows_low(i + 1, 1 - z)

            for q in range(G):
                w1_low(0, 0, q)
            rows_low(0, 0)
            for i in range(3):
                tile(i, i % 2, i // 2 + 1, True)
            with dve.Fori(0, (NT - 5) // 2) as ii:
                tile(ii * 2 + 3, 1, ii + 2, True)
                tile(ii * 2 + 4, 0, ii + 3, True)
            tile(NT - 2, (NT - 2) % 2, NT // 2, True)
            tile(NT - 1, (NT - 1) % 2, (NT + 1) // 2, False)
            sums_out(NT - 1, (NT - 1) % 2, (NT + 1) // 2)
            for g in range(NG):
                dve.wait_ge(gathered[g], 32)
                for k, y in enumerate((y1, y2)):
                    for t in range(g * G, (g + 1) * G):
                        V.scalar_tensor_tensor(out=X[:, t, :], in0=y[:, t, :], scalar=gate_e[:, 2 + k, t:t + 1],
                                               in1=X[:, t, :], op0=ALU.mult, op1=ALU.add).then_inc(dve_seq, 1)
                    seq.n += G
                    dve.wait_ge(dve_seq, seq.n)
                dve.sem_inc(x_done, G)


def kernel(**inputs):
    import numpy as np
    import concourse.bacc as bacc
    from concourse.bass_utils import run_bass_kernel_spmd

    def laid(b):
        e, n = b.shape
        return np.ascontiguousarray(b.reshape(e, n // 128, 128).transpose(2, 0, 1))

    arrays = {k: np.ascontiguousarray(v) for k, v in inputs.items()}
    arrays["L1_gnn_a_b"] = arrays["L1_gnn_a_b"].reshape(1)
    arrays["adj_t"] = np.ascontiguousarray(arrays["adj"].T)
    arrays["L0_ffn_rw_t"] = np.ascontiguousarray(arrays.pop("L0_ffn_rw").T)
    for layer in (0, 1):
        for b in ("b1", "b2"):
            if (layer, b) != (1, "b2"):
                arrays[f"L{layer}_ffn_{b}_p"] = laid(arrays.pop(f"L{layer}_ffn_{b}"))
    nc = bacc.Bacc("TRN2", target_bir_lowering=False, num_devices=1)
    aps = {k: nc.dram_tensor(k + "_dram", v.shape, mybir.dt.from_np(v.dtype), kind="ExternalInput").ap()
           for k, v in arrays.items()}
    aps["out"] = nc.dram_tensor("out_dram", (2048, 256), mybir.dt.float32, kind="ExternalOutput").ap()
    gnn_ffn_program(nc, aps)
    r = run_bass_kernel_spmd(nc, [{k + "_dram": v for k, v in arrays.items()}], core_ids=[0])
    return r.results[0]["out_dram"]
```
